# Optimizing a Trainium2 kernel written in Bass

```python
import numpy as np
import jax
import jax.numpy as jnp

def _softmax(x, axis=-1):
    return jax.nn.softmax(x, axis=axis)

def _gelu(x):
    return jax.nn.gelu(x, approximate=True)

def _silu(x):
    return jax.nn.silu(x)

def _sigmoid(x):
    return jax.nn.sigmoid(x)

def _layernorm(x, axis=-1, eps=1e-05):
    m = jnp.mean(x, axis=axis, keepdims=True)
    v = jnp.var(x, axis=axis, keepdims=True)
    return (x - m) / jnp.sqrt(v + eps)

def _scatter_add(tgt, idx, src, axis=0):
    return tgt.at[idx].add(src)

def _segment_sum(src, seg, n):
    return jax.ops.segment_sum(src, seg, n)
kernel_name = 'mk_audio_tower_d1_tok_audfeat512_r4_b3d935'

def setup_inputs(seed: int=0):
    np.random.seed(seed)
    _w = jnp.asarray

    def _rec_inputs():
        import jax
        import jax.numpy as jnp
        _rk = jax.random.key(seed)
        x = 3.78913e-05 + 1.00016 * jax.random.normal(jax.random.fold_in(_rk, 1), (64, 125, 64), jnp.float32)
        return x
    x = _rec_inputs()

    def _L0_tok_setup():
        import jax, jax.numpy as jnp
        import numpy as np
        CONTEXT = 5
        DILATION = 1
        EPS = 1e-05
        key = jax.random.key(seed)
        k1, k2, k3 = jax.random.split(key, 3)
        B, T, D, O = (64, 500, 64, 128)
        x = jax.random.normal(k1, (B, T, D), dtype=jnp.float32)
        K = D * CONTEXT
        W = jax.random.normal(k2, (O, K), dtype=jnp.float32) / np.sqrt(K).astype(np.float32)
        b = jax.random.normal(k3, (O,), dtype=jnp.float32) * 0.01
        gamma = jnp.ones((O,), dtype=jnp.float32)
        beta = jnp.zeros((O,), dtype=jnp.float32)
        return {'x': x, 'W': W, 'b': b, 'gamma': gamma, 'beta': beta}
    _L0_tok_all = _L0_tok_setup()
    _L0_tok_in = {k: v for k, v in _L0_tok_all.items() if k in ('W', 'b', 'gamma', 'beta')}
    del _L0_tok_all

    def _L0_attn_setup():
        import jax, jax.numpy as jnp
        import numpy as np
        B, S, INP = (4, 512, 128)
        HIDDEN, NHEADS = (128, 8)
        DH = HIDDEN // NHEADS
        BASE = 10000.0

        def rope(x):
            b, s, h, d = x.shape
            d2 = d // 2
            theta = 1.0 / BASE ** (jnp.arange(0, d, 2, dtype=jnp.float32) / d)
            idx_theta = jnp.arange(s, dtype=jnp.float32)[:, None] * theta[None, :]
            idx_theta2 = jnp.concatenate([idx_theta, idx_theta], axis=1)
            neg_half = jnp.concatenate([-x[..., d2:], x[..., :d2]], axis=-1)
            cos = jnp.cos(idx_theta2)[None, :, None, :]
            sin = jnp.sin(idx_theta2)[None, :, None, :]
            return x * cos + neg_half * sin
        key = jax.random.key(seed)
        ks = jax.random.split(key, 9)
        sd = 1.0 / np.sqrt(INP)
        x = jax.random.normal(ks[0], (B, S, INP), dtype=jnp.float32)
        Wq = jax.random.uniform(ks[1], (INP, HIDDEN), jnp.float32, -sd, sd)
        bq = jax.random.uniform(ks[2], (HIDDEN,), jnp.float32, -sd, sd)
        Wk = jax.random.uniform(ks[3], (INP, HIDDEN), jnp.float32, -sd, sd)
        bk = jax.random.uniform(ks[4], (HIDDEN,), jnp.float32, -sd, sd)
        Wv = jax.random.uniform(ks[5], (INP, HIDDEN), jnp.float32, -sd, sd)
        bv = jax.random.uniform(ks[6], (HIDDEN,), jnp.float32, -sd, sd)
        Wo = jax.random.uniform(ks[7], (HIDDEN, INP), jnp.float32, -sd, sd)
        bo = jax.random.uniform(ks[8], (INP,), jnp.float32, -sd, sd)
        return {'x': x, 'Wq': Wq, 'bq': bq, 'Wk': Wk, 'bk': bk, 'Wv': Wv, 'bv': bv, 'Wo': Wo, 'bo': bo}
    _L0_attn_all = _L0_attn_setup()
    _L0_attn_in = {k: v for k, v in _L0_attn_all.items() if k in ('Wq', 'bq', 'Wk', 'bk', 'Wv', 'bv', 'Wo', 'bo')}
    del _L0_attn_all

    def _L0_ffn_setup():
        import jax, jax.numpy as jnp
        import numpy as np
        G = 4
        EPG = 4
        E = 16
        KG = 2
        K = 2
        GTP = 0.9
        TP = 0.9
        SCALE = 1.0 / float(np.sqrt(G))

        def _routing_weights(xf, Wr, br, Wgate, bgate):
            N = xf.shape[0]
            gp = jax.nn.softmax(xf @ Wr + br, axis=-1)
            order = jnp.argsort(-gp, axis=-1)
            sp_k = jnp.take_along_axis(gp, order, axis=-1)[:, :KG]
            idx_k = order[:, :KG]
            act = jnp.cumsum(sp_k, axis=-1) <= GTP
            act = act.at[:, 0].set(True)
            mp = sp_k * act
            rn = mp / (jnp.sum(mp, axis=-1, keepdims=True) + 1e-09)
            w_group = jnp.zeros((N, G), xf.dtype).at[jnp.arange(N)[:, None], idx_k].set(rn)
            ep = jax.nn.softmax(jnp.einsum('nd,gde->nge', xf, Wgate) + bgate, axis=-1)
            eorder = jnp.argsort(-ep, axis=-1)
            esp = jnp.take_along_axis(ep, eorder, axis=-1)[:, :, :K]
            eidx = eorder[:, :, :K]
            eact = jnp.cumsum(esp, axis=-1) <= TP
            eact = eact.at[:, :, 0].set(True)
            emp = esp * eact
            ern = emp / (jnp.sum(emp, axis=-1, keepdims=True) + 1e-09)
            w_exp = jnp.zeros((N, G, EPG), xf.dtype).at[jnp.arange(N)[:, None, None], jnp.arange(G)[None, :, None], eidx].set(ern)
            return (w_group[:, :, None] * w_exp * SCALE).reshape(N, E)
        key = jax.random.key(seed)
        ks = jax.random.split(key, 6)
        B, T, D, H = (2, 256, 128, 512)
        x = jax.random.normal(ks[0], (B, T, D), jnp.float32)
        Wr = jax.random.normal(ks[1], (D, G), jnp.float32) * 0.02
        br = jnp.zeros((G,), jnp.float32)
        Wgate = jax.random.normal(ks[2], (G, D, EPG), jnp.float32) * 0.02
        bgate = jnp.zeros((G, EPG), jnp.float32)
        W1 = jax.random.normal(ks[3], (E, D, H), jnp.float32) * 0.02
        W3 = jax.random.normal(ks[4], (E, D, H), jnp.float32) * 0.02
        W2 = jax.random.normal(ks[5], (E, H, D), jnp.float32) * 0.02
        return {'x': x, 'Wr': Wr, 'br': br, 'Wgate': Wgate, 'bgate': bgate, 'W1': W1, 'W3': W3, 'W2': W2}
    _L0_ffn_all = _L0_ffn_setup()
    _L0_ffn_in = {k: v for k, v in _L0_ffn_all.items() if k in ('Wr', 'br', 'Wgate', 'bgate', 'W1', 'W3', 'W2')}
    del _L0_ffn_all
    return {'x': x, 'L0_tok_W': _L0_tok_in['W'], 'L0_tok_b': _L0_tok_in['b'], 'L0_tok_gamma': _L0_tok_in['gamma'], 'L0_tok_beta': _L0_tok_in['beta'], 'L0_attn_Wq': _L0_attn_in['Wq'], 'L0_attn_bq': _L0_attn_in['bq'], 'L0_attn_Wk': _L0_attn_in['Wk'], 'L0_attn_bk': _L0_attn_in['bk'], 'L0_attn_Wv': _L0_attn_in['Wv'], 'L0_attn_bv': _L0_attn_in['bv'], 'L0_attn_Wo': _L0_attn_in['Wo'], 'L0_attn_bo': _L0_attn_in['bo'], 'L0_ffn_Wr': _L0_ffn_in['Wr'], 'L0_ffn_br': _L0_ffn_in['br'], 'L0_ffn_Wgate': _L0_ffn_in['Wgate'], 'L0_ffn_bgate': _L0_ffn_in['bgate'], 'L0_ffn_W1': _L0_ffn_in['W1'], 'L0_ffn_W3': _L0_ffn_in['W3'], 'L0_ffn_W2': _L0_ffn_in['W2']}

def reference(x, L0_tok_W, L0_tok_b, L0_tok_gamma, L0_tok_beta, L0_attn_Wq, L0_attn_bq, L0_attn_Wk, L0_attn_bk, L0_attn_Wv, L0_attn_bv, L0_attn_Wo, L0_attn_bo, L0_ffn_Wr, L0_ffn_br, L0_ffn_Wgate, L0_ffn_bgate, L0_ffn_W1, L0_ffn_W3, L0_ffn_W2):
    import jax
    import jax.numpy as jnp

    def _L0_tok_ref(x, W, b, gamma, beta):
        import jax, jax.numpy as jnp
        import numpy as np
        CONTEXT = 5
        DILATION = 1
        EPS = 1e-05
        B, T, D = x.shape
        new_T = T - DILATION * (CONTEXT - 1)
        win = jnp.concatenate([x[:, i * DILATION:i * DILATION + new_T, :] for i in range(CONTEXT)], axis=-1)
        y = jnp.einsum('btk,ok->bto', win, W) + b
        y = jax.nn.relu(y)
        mean = jnp.mean(y, axis=(0, 1))
        var = jnp.mean(jnp.square(y - mean), axis=(0, 1))
        y = (y - mean) * jax.lax.rsqrt(var + EPS) * gamma + beta
        return y

    def _L0_attn_ref(x, Wq, bq, Wk, bk, Wv, bv, Wo, bo):
        import jax, jax.numpy as jnp
        import numpy as np
        B, S, INP = (4, 512, 128)
        HIDDEN, NHEADS = (128, 8)
        DH = HIDDEN // NHEADS
        BASE = 10000.0

        def rope(x):
            b, s, h, d = x.shape
            d2 = d // 2
            theta = 1.0 / BASE ** (jnp.arange(0, d, 2, dtype=jnp.float32) / d)
            idx_theta = jnp.arange(s, dtype=jnp.float32)[:, None] * theta[None, :]
            idx_theta2 = jnp.concatenate([idx_theta, idx_theta], axis=1)
            neg_half = jnp.concatenate([-x[..., d2:], x[..., :d2]], axis=-1)
            cos = jnp.cos(idx_theta2)[None, :, None, :]
            sin = jnp.sin(idx_theta2)[None, :, None, :]
            return x * cos + neg_half * sin
        b, s, _ = x.shape
        scale = DH ** (-0.5)
        q = (x @ Wq + bq).reshape(b, s, NHEADS, DH)
        k = (x @ Wk + bk).reshape(b, s, NHEADS, DH)
        v = (x @ Wv + bv).reshape(b, s, NHEADS, DH)
        q = rope(q)
        k = rope(k)
        att = jnp.einsum('bihd,bjhd->bhij', q, v)
        att = jax.nn.softmax(att * scale, axis=-1)
        h = jnp.einsum('bhij,bjhd->bihd', att, v)
        h = h.reshape(b, s, HIDDEN)
        return h @ Wo + bo + x

    def _L0_ffn_ref(x, Wr, br, Wgate, bgate, W1, W3, W2):
        import jax, jax.numpy as jnp
        import numpy as np
        G = 4
        EPG = 4
        E = 16
        KG = 2
        K = 2
        GTP = 0.9
        TP = 0.9
        SCALE = 1.0 / float(np.sqrt(G))

        def _routing_weights(xf, Wr, br, Wgate, bgate):
            N = xf.shape[0]
            gp = jax.nn.softmax(xf @ Wr + br, axis=-1)
            order = jnp.argsort(-gp, axis=-1)
            sp_k = jnp.take_along_axis(gp, order, axis=-1)[:, :KG]
            idx_k = order[:, :KG]
            act = jnp.cumsum(sp_k, axis=-1) <= GTP
            act = act.at[:, 0].set(True)
            mp = sp_k * act
            rn = mp / (jnp.sum(mp, axis=-1, keepdims=True) + 1e-09)
            w_group = jnp.zeros((N, G), xf.dtype).at[jnp.arange(N)[:, None], idx_k].set(rn)
            ep = jax.nn.softmax(jnp.einsum('nd,gde->nge', xf, Wgate) + bgate, axis=-1)
            eorder = jnp.argsort(-ep, axis=-1)
            esp = jnp.take_along_axis(ep, eorder, axis=-1)[:, :, :K]
            eidx = eorder[:, :, :K]
            eact = jnp.cumsum(esp, axis=-1) <= TP
            eact = eact.at[:, :, 0].set(True)
            emp = esp * eact
            ern = emp / (jnp.sum(emp, axis=-1, keepdims=True) + 1e-09)
            w_exp = jnp.zeros((N, G, EPG), xf.dtype).at[jnp.arange(N)[:, None, None], jnp.arange(G)[None, :, None], eidx].set(ern)
            return (w_group[:, :, None] * w_exp * SCALE).reshape(N, E)
        B, T, D = x.shape
        xf = x.reshape(-1, D)
        tw = _routing_weights(xf, Wr, br, Wgate, bgate)
        out = jnp.zeros_like(xf)
        for e in range(E):
            h = jax.nn.silu(xf @ W1[e]) * (xf @ W3[e])
            out = out + tw[:, e:e + 1] * (h @ W2[e])
        return out.reshape(B, T, D)
    h = _L0_tok_ref(x, L0_tok_W, L0_tok_b, L0_tok_gamma, L0_tok_beta)
    h = h + _L0_attn_ref(_layernorm(h, axis=-1), L0_attn_Wq, L0_attn_bq, L0_attn_Wk, L0_attn_bk, L0_attn_Wv, L0_attn_bv, L0_attn_Wo, L0_attn_bo)
    h = h + _L0_ffn_ref(_layernorm(h, axis=-1), L0_ffn_Wr, L0_ffn_br, L0_ffn_Wgate, L0_ffn_bgate, L0_ffn_W1, L0_ffn_W3, L0_ffn_W2)
    return h

_drawn_inputs = setup_inputs


def setup_inputs(seed=0):
    import zlib

    import numpy as np

    out = dict(_drawn_inputs(seed))
    spreads = {'L0_tok_gamma': (1.0, 0.2),
     'L0_tok_beta': (0.0, 0.1),
     'L0_ffn_br': (0.0, 0.8),
     'L0_ffn_bgate': (0.0, 0.8)}
    factors = {'L0_tok_b': 8.0,
     'L0_attn_Wq': 3.751,
     'L0_attn_bq': 8.0,
     'L0_attn_Wv': 2.727,
     'L0_attn_bv': 3.432,
     'L0_ffn_Wr': 8.0,
     'L0_ffn_Wgate': 8.0,
     'L0_ffn_W1': 8.0,
     'L0_ffn_W3': 8.0,
     'L0_ffn_W2': 8.0}
    for name, (base, spread) in spreads.items():
        noise = np.random.default_rng([zlib.crc32(name.encode()), seed]).standard_normal(out[name].shape)
        drawn = base * np.exp(spread * noise) if base else spread * noise
        out[name] = jnp.asarray(drawn.astype(out[name].dtype))
    for name, factor in factors.items():
        out[name] = (out[name] * factor).astype(out[name].dtype)
    return out
```

```python
from contextlib import ExitStack

import concourse.bass as bass
import numpy as np
from concourse import mybir

ALU = mybir.AluOpType
ACT = mybir.ActivationFunctionType
AX = mybir.AxisListType
F32 = mybir.dt.float32
F32R = mybir.dt.float32r
BF16 = mybir.dt.bfloat16
I32 = mybir.dt.int32
U32 = mybir.dt.uint32

BATCH, TIME, D_IN = 64, 125, 64
CONTEXT = 5
SEQ = TIME - (CONTEXT - 1)
N_TOK = BATCH * SEQ
D = 128
HEADS, DH = 8, 16
EPS = 1e-5
GROUPS, PER_GROUP = 4, 4
EXPERTS = GROUPS * PER_GROUP
PICKED = 4
HID = 512
HC = HID // 128
TOP_P = 0.9
P = 128

CHUNK_B = 4
CHUNKS = BATCH // CHUNK_B
CHUNK = CHUNK_B * SEQ

ROW_W = D
ROW_ID = D + EXPERTS
ROW = D + EXPERTS + 4
TILE = 512
SUB = TILE // P
CAP = N_TOK + TILE
TILES = (N_TOK * PICKED) // TILE + EXPERTS
LOGITS = GROUPS + EXPERTS
ROWS = 4
assert TILES % ROWS == 0

R = 8
ROUTES = BATCH // R
PROBS = 1 + GROUPS

LOOP_FIRST = 8
ROUTE_AT = 6
ROUTE_LINKS = 28
LOOPS = 6
STEP_FIRST, STEP_END = -4, BATCH + R

TR3_FIRST, TR3_LAST = -3, BATCH + 4
SMALL_FIRST, SMALL_LAST = -4, BATCH + 5
LN_FIRST, LN_LAST = -3, BATCH + 4


def ds(at, n):
    return bass.ds(at, n)


def audio_tower(nc, x_t, conv_w, col_params, row_params, rope_tab, attn_w, route_w, expert_w, out):
    routed = nc.dram_tensor("routed", (EXPERTS * CAP + TILE, ROW), F32, kind="Internal").ap()
    with ExitStack() as ctx:
        def sb(name, shape, dt=F32):
            return ctx.enter_context(nc.sbuf_tensor(name, shape, dt))

        def sem(name):
            return ctx.enter_context(nc.semaphore(name))

        ident = sb("ident", [P, P])
        conv_sb = sb("conv_sb", [P, 3, D])
        colp = sb("colp", [P, 6])
        conv_b, gamma_c, beta_c, bq_c, bqr_c, bv_c = (colp[:, i:i + 1] for i in range(6))
        rowp = sb("rowp", [SEQ, 2 * D + LOGITS])
        bv_row, bo_row, route_b = rowp[:, 0:D], rowp[:, D:2 * D], rowp[:, 2 * D:2 * D + LOGITS]
        rope_sb = sb("rope_sb", [P, 2, SEQ])
        attn_sb = sb("attn_sb", [P, 4, D])
        wq_sb, wqr_sb, wv_sb, wo_sb = (attn_sb[:, i, :] for i in range(4))
        route_sb = sb("route_sb", [P, LOGITS])
        head_mask = sb("head_mask", [P, 4])
        minus_half = sb("minus_half", [P, 2])
        marker = sb("marker", [P, 1])
        ones_e = sb("ones_e", [P, EXPERTS])
        eps_t = sb("eps_t", [P, 2])

        conv_in = sb("conv_in", [P, BATCH * TIME])
        y_all = conv_in[:, 0:N_TOK]
        resid = sb("resid", [SEQ, BATCH, D])
        xn_all = sb("xn_all", [P, BATCH * D])
        logits = sb("logits", [SEQ, BATCH, LOGITS])
        stats_y = sb("stats_y", [P, CHUNKS, 6])
        bn = sb("bn", [P, 6])

        h_cm = sb("h_cm", [P, 2, SEQ])
        stat6 = sb("stat6", [SEQ, 2, 6])
        mv = sb("mv", [SEQ, 2, 2, 2])
        var_eps = sb("var_eps", [SEQ, 2, 2])
        rstd = sb("rstd", [SEQ, 2, 2])
        shift1 = sb("shift1", [SEQ, BATCH])
        shift2 = sb("shift2", [SEQ, 2])
        rstd1 = sb("rstd1", [SEQ, 2])
        xn = sb("xn", [SEQ, 2, D])
        xn2 = sb("xn2", [SEQ, 2, D])
        cm3 = sb("cm3", [P, 2, 3, SEQ])
        q_a = sb("q_a", [P, SEQ])
        q_b = sb("q_b", [P, SEQ])
        q_cm = sb("q_cm", [P, 2, SEQ])
        v_heads = sb("v_heads", [P, 2, 4, SEQ])
        v_tok = sb("v_tok", [SEQ, 4, HEADS, 32])
        row_max = sb("row_max", [SEQ, HEADS])
        probs = sb("probs", [SEQ, 2, HEADS, SEQ])
        probs_t = sb("probs_t", [SEQ, 2, HEADS, SEQ])
        o_sb = sb("o_sb", [P, 2, 2, SEQ])
        rz = sb("rz", [SEQ, HEADS])
        att = sb("att", [SEQ, 2, HEADS, DH])

        less = sb("less", [SEQ, 160])
        pmax = sb("pmax", [SEQ, R * PROBS])
        first_p = sb("first_p", [SEQ, R * PROBS])
        second_p = sb("second_p", [SEQ, R * PROBS])
        part = sb("part", [SEQ, R * PROBS])
        ratio = sb("ratio", [SEQ, 2, R * PROBS])
        pairs = sb("pairs", [SEQ, R * PROBS, 4, 4])
        tie = sb("tie", [SEQ, 4, 4])
        rank = sb("rank", [SEQ, R * PROBS * 4])
        picks = sb("picks", [SEQ, 2, R, LOGITS])
        weigh = sb("weigh", [SEQ, 2, R, LOGITS])
        chosen = sb("chosen", [SEQ, R, LOGITS])
        sel = sb("sel", [SEQ, EXPERTS, R], BF16)
        before = sb("before", [SEQ, P], BF16)
        ones_b = sb("ones_b", [SEQ, P], BF16)
        no_carry = sb("no_carry", [P, EXPERTS, R])
        total = sb("total", [P, EXPERTS, R])
        next_row = sb("next_row", [P, EXPERTS])
        flat = pairs[:].rearrange("p q i j -> p (q i j)")
        place = flat[:, 0:128].rearrange("p (b e) -> p b e", e=EXPERTS)
        place2 = flat[:, 128:384].rearrange("p (k b e) -> p k b e", k=2, e=EXPERTS)
        by_group = flat[:, 384:448].rearrange("p (k b g) -> p k b g", k=2, g=GROUPS)
        by_pick = flat[:, 448:576].rearrange("p (a k b g) -> p a k b g", a=2, k=2, g=GROUPS)
        slots_f = sb("slots_f", [SEQ, PICKED * R])
        slots = sb("slots", [SEQ, PICKED * R], U32)
        stage = sb("stage", [SEQ, R, ROW])
        tok_id = sb("tok_id", [SEQ, R])
        pad_rows = sb("pad_rows", [P, SUB, ROW])
        tile_no = sb("tile_no", [P, TILES])
        expert_no = sb("expert_no", [P, EXPERTS])
        region = sb("region", [P, EXPERTS])
        n_tiles = sb("n_tiles", [P, EXPERTS])
        n_tiles_i = sb("n_tiles_i", [P, EXPERTS], I32)
        last_tile = sb("last_tile", [P, EXPERTS])
        tile_row_i = sb("tile_row_i", [P, TILES], I32)
        tile_e_i = sb("tile_e_i", [P, TILES], I32)
        ends_i = sb("ends_i", [P, EXPERTS], I32)
        W_COLS = 3 * HID
        w_hi, w_lo = (sb(n, [P, 2, W_COLS], F32R) for n in ("w_hi", "w_lo"))
        x_hi, x_lo = (sb(n, [P, 2, TILE], F32R) for n in ("x_hi", "x_lo"))
        hid_hi, hid_lo = (sb(n, [P, HC, TILE], F32R) for n in ("hid_hi", "hid_lo"))
        taken = {}

        def in_place_of(name, old, copies, n=TILE):
            at = taken.get(name, 0)
            taken[name] = at + copies * n
            return old[:, at:at + copies * n].rearrange("p (k n) -> p k n", k=copies)
        w_raw = in_place_of("input", conv_in, 2, W_COLS)
        y_cm = in_place_of("input", conv_in, 1)[:, 0, :]
        y_rows = in_place_of("input", conv_in, 2).rearrange("p k (s d) -> p k s d", s=SUB)
        silu, hid = (in_place_of("input", conv_in, 2) for _ in range(2))
        x_rows = in_place_of("norm", xn_all, ROWS, SUB * ROW).rearrange("p k (s c) -> p k s c", s=SUB)
        tile_e, tile_s, tile_v = (in_place_of("norm", xn_all, 1, TILES)[:, 0, :] for _ in range(3))
        past, past2 = (in_place_of("norm", xn_all, TILES, EXPERTS) for _ in range(2))
        w_part = sb("w_part", [P, SUB, EXPERTS])
        w_row = sb("w_row", [P, ROWS, SUB])
        out_ids = sb("out_ids", [P, ROWS, SUB], U32)

        def bank(name, shape=(P, 512)):
            return ctx.enter_context(nc.psum_tensor(name, list(shape), F32))

        scores_ps = bank("scores_ps", (P, 2, 512))
        pt_ps = bank("pt_ps", (P, 2, 512))
        proj_ps = bank("proj_ps")
        dve_ps = bank("dve_ps")
        act_ps = bank("act_ps")
        o_ps = bank("o_ps")
        conv_ps = [proj_ps, dve_ps]
        prefix_ps = proj_ps[0:SEQ, 0:P].rearrange("p (e b) -> p e b", b=R)
        total_ps = proj_ps[:, P:2 * P].rearrange("p (e b) -> p e b", b=R)
        gate_ps, up_ps = [scores_ps[:, i, :] for i in range(2)], [pt_ps[:, i, :] for i in range(2)]
        x_ps, y_ps, y_tok_ps = act_ps, [o_ps, proj_ps], dve_ps
        qT_ps, qrT_ps, vT_ps = (proj_ps[:, i * SEQ:(i + 1) * SEQ] for i in range(3))
        v_ps = proj_ps[0:SEQ, 3 * SEQ:3 * SEQ + D]
        h_tok_ps, wo_ps, logit_ps = dve_ps[0:SEQ, 0:D], dve_ps[0:SEQ, D:2 * D], dve_ps[0:SEQ, 2 * D:2 * D + LOGITS]
        o_cm_ps = o_ps[:, 0:2 * SEQ].rearrange("p (s i) -> p s i", s=2)
        o_tok_ps = o_ps[0:SEQ, 0:2 * D].rearrange("p (h e) -> p h e", e=32)

        w_in = sem("w_in")
        x_in = [sem(f"x_in{i}") for i in range(4)]
        consts = sem("consts")
        conv_done, conv_read, stats_done = sem("conv_done"), sem("conv_read"), sem("stats_done")
        bn_link, bn_var, bn_rstd, bn_ready = sem("bn_link"), sem("bn_var"), sem("bn_rstd"), sem("bn_ready")
        h_ready = sem("h_ready")
        scores_done, scores_read, exp_done = sem("scores_done"), sem("scores_read"), sem("exp_done")
        otr_done, att_ready = sem("otr_done"), sem("att_ready")
        tr3_done, tr3_read = sem("tr3_done"), sem("tr3_read")
        pt_done, pt_read = sem("pt_done"), sem("pt_read")
        proj_done, proj_read = sem("proj_done"), sem("proj_read")
        pv_done, o_read = sem("pv_done"), sem("o_read")
        small_done, small_read = sem("small_done"), sem("small_read")
        mv_ready, ln_link, rstd_ready = sem("mv_ready"), sem("ln_link"), sem("rstd_ready")
        xn_ready, xn2_ready, row_ready = sem("xn_ready"), sem("xn2_ready"), sem("row_ready")
        stats1_done, h1_done, stats2_done, logits_done = sem("stats1_done"), sem("h1_done"), sem("stats2_done"), sem("logits_done")
        rz_done, shift1_done, shift2_done = sem("rz_done"), sem("shift1_done"), sem("shift2_done")
        eps_set = sem("eps_set")
        tables, pool_link = sem("tables"), sem("pool_link")
        route_link = sem("route_link")
        less_ready, exps_ready, sel_ready, prefix_done, prefix_read = (
            sem(n) for n in ("less_ready", "exps_ready", "sel_ready", "prefix_done", "prefix_read"))
        stage_x, stage_ready, scattered = sem("stage_x"), sem("stage_ready"), sem("scattered")
        ends_ready, pads_in, table_ready, resid_out = sem("ends_ready"), sem("pads_in"), sem("table_ready"), sem("resid_out")
        table_link, hid_free = sem("table_link"), sem("hid_free")
        rows_in = [sem(f"rows_in{i}") for i in range(ROWS)]
        weights_in = [sem(f"weights_in{i}") for i in range(2)]
        x_done, x_read, gate_done, up_done, silu_done, hid_ready = (
            sem(n) for n in ("x_done", "x_read", "gate_done", "up_done", "silu_done", "hid_ready"))
        x_hi_done, w_hi_done, w_lo_done, hid_done, hid_hi_done = (
            sem(n) for n in ("x_hi_done", "w_hi_done", "w_lo_done", "hid_done", "hid_hi_done"))
        y_done, y_read, y_tok_done, w_link, w_link2, ids_ready, y_rows_ready, added, down_done = (
            sem(n) for n in ("y_done", "y_read", "y_tok_done", "w_link", "w_link2", "ids_ready", "y_rows_ready", "added",
                             "down_done"))
        max_done, rope_link = sem("max_done"), sem("rope_link")
        marked = sem("marked")

        def ok(b):
            return not isinstance(b, int) or 0 <= b < BATCH

        def need(eng, s, b):
            if isinstance(b, int):
                if b < 0:
                    return
                b = min(b, BATCH - 1)
            eng.wait_ge(s, b + 1)

        def need_step(eng, s, n, first, last):
            if isinstance(n, int):
                if n < first:
                    return
                n = min(n, last)
            eng.wait_ge(s, n - first + 1)

        def steps(eng, step, route=None):
            for n in range(STEP_FIRST, LOOP_FIRST):
                step(n, n, (n - LOOP_FIRST) // R)
            with eng.Fori(0, LOOPS) as g:
                for u in range(R):
                    step(g * R + (LOOP_FIRST + u), u, g)
                    if u == ROUTE_AT and route is not None:
                        route(g)
            for n in range(LOOP_FIRST + LOOPS * R, STEP_END):
                step(n, n, (n - LOOP_FIRST) // R)
                if n % R == ROUTE_AT and route is not None:
                    route((n - LOOP_FIRST) // R)

        def tiles(eng, tile):
            for t in range(ROWS):
                tile(t, t)
            with eng.Fori(1, TILES // ROWS - 1) as i:
                for u in range(ROWS):
                    tile(i * ROWS + u, u)
            for t in range(TILES - ROWS, TILES):
                tile(t, t % ROWS)

        def since(t, first):
            return not isinstance(t, int) or t >= first

        def is_tile(t):
            return not isinstance(t, int) or 0 <= t < TILES

        def loads(t, u, ring):
            return (t - u % ring) * (16 // ring) + 16

        block = ctx.enter_context(nc.Block())

        @block.sync
        def _(sp):
            sp.dma_start(conv_sb[:, 0:2, :], conv_w[0:2 * P, :].rearrange("(c p) o -> p c o", p=P)).then_inc(w_in, 16)
            sp.dma_start(conv_sb[0:64, 2, :], conv_w[2 * P:2 * P + 64, :]).then_inc(w_in, 16)
            sp.dma_start(colp[:], col_params).then_inc(w_in, 16)
            n = BATCH * TIME // 4
            for i in range(4):
                sp.dma_start(conv_in[0:64, i * n:(i + 1) * n], x_t[:, i * n:(i + 1) * n]).then_inc(x_in[i], 16)
                hi = min((i + 1) * n, BATCH * TIME - 1)
                sp.dma_start(conv_in[64:128, i * n:hi], x_t[:, i * n + 1:hi + 1]).then_inc(x_in[i], 16)
            sp.dma_start(attn_sb[:], attn_w.rearrange("w p o -> p w o")).then_inc(w_in, 16)
            sp.dma_start(rope_sb[:], rope_tab.rearrange("w p s -> p w s")).then_inc(w_in, 16)
            sp.dma_start(route_sb[:], route_w).then_inc(w_in, 16)
            sp.dma_start(rowp[:], row_params.rearrange("(a n) -> a n", a=1).broadcast_to([SEQ, 2 * D + LOGITS])).then_inc(w_in, 16)
            sp.wait_ge(tables, 1)
            out_b = out[0:N_TOK, :].rearrange("(b s) d -> s b d", s=SEQ)

            def store_residual(g):
                sp.wait_ge(h1_done, g * R + R)
                sp.dma_start(out_b[:, ds(g * R, R), :], resid[:, ds(g * R, R), :]).then_inc(resid_out, 16)
            with sp.Fori(0, ROUTES) as g:
                store_residual(g)
            sp.dma_start(out[N_TOK:N_TOK + TILE, :].rearrange("(p s) d -> p s d", s=SUB),
                         pad_rows[:, :, 0:D]).then_inc(resid_out, 16)
            sp.wait_ge(ends_ready, 1)
            for e in range(EXPERTS):
                end = sp.value_load(ends_i[0:1, e:e + 1], min_val=e * CAP, max_val=e * CAP + N_TOK)
                sp.dma_start(routed[ds(end, TILE), :].rearrange("(p s) c -> p s c", s=SUB),
                             pad_rows[:]).then_inc(pads_in, 16)
            sp.wait_ge(pads_in, 16 * EXPERTS)
            sp.wait_ge(scattered, 16 * PICKED * BATCH + 16)
            sp.wait_ge(table_ready, 1)

            def load_tile(t, u):
                e = sp.value_load(tile_e_i[0:1, ds(t, 1)], min_val=0, max_val=EXPERTS - 1)
                row = sp.value_load(tile_row_i[0:1, ds(t, 1)], min_val=0, max_val=EXPERTS * CAP)
                if since(t, 2):
                    sp.wait_ge(w_lo_done, t * HC - HC)
                sp.dma_start(w_raw[:, u % 2, :], expert_w[ds(e, 1), :, :].rearrange("e p n -> p (e n)")).then_inc(weights_in[u % 2], 16)
                if since(t, ROWS):
                    sp.wait_ge(x_done, t - (ROWS - 1))
                    sp.wait_ge(ids_ready, t - (ROWS - 1))
                sp.dma_start(x_rows[:, u, :, :], routed[ds(row, TILE), :].rearrange("(p s) c -> p s c", s=SUB)).then_inc(rows_in[u], 16)
            tiles(sp, load_tile)
            sp.wait_ge(added, 16 * SUB * TILES)

        @block.gpsimd
        def _(pool):
            pool.memset(ident[:], 0.0).then_inc(consts, 1)
            pool.memset(v_tok[:], 0.0).then_inc(consts, 1)
            pool.memset(minus_half[:], -0.5).then_inc(consts, 1)
            pool.memset(head_mask[:], 1.0).then_inc(consts, 1)
            pool.memset(eps_t[:], EPS).then_inc(eps_set, 1)
            pool.wait_ge(consts, 4)
            pool.wait_ge(eps_set, 1)
            pool.affine_select(out=ident[:], in_=ident[:], compare_op=ALU.not_equal, fill=1.0, base=0,
                               pattern=[[-1, P]], channel_multiplier=1).then_inc(consts, 1)
            pool.wait_ge(consts, 5)
            pool.memset(v_tok[:, :, :, DH:DH + 1], 1.0).then_inc(consts, 1)
            pool.wait_ge(consts, 6)
            for half in range(2):
                m = head_mask[64 * half:64 * half + 64, :]
                pool.affine_select(out=m, in_=m, compare_op=ALU.is_ge, fill=0.0, base=0,
                                   pattern=[[-DH, 4]], channel_multiplier=1).then_inc(consts, 1)
                pool.wait_ge(consts, 7 + 2 * half)
                pool.affine_select(out=m, in_=m, compare_op=ALU.is_ge, fill=0.0, base=DH - 1,
                                   pattern=[[DH, 4]], channel_multiplier=-1).then_inc(consts, 1)
                pool.wait_ge(consts, 8 + 2 * half)

            pool.memset(ones_e[:], 1.0).then_inc(pool_link, 1)
            pool.memset(pad_rows[:], 0.0).then_inc(pool_link, 1)
            pool.memset(tie[:], 0.0).then_inc(pool_link, 1)
            pool.memset(before[:], 0.0).then_inc(pool_link, 1)
            pool.memset(ones_b[:], 1.0).then_inc(pool_link, 1)
            pool.memset(no_carry[:], 1.0).then_inc(pool_link, 1)
            pool.memset(stage[:, :, ROW_ID + 1:ROW], 0.0).then_inc(pool_link, 1)
            pool.iota(tok_id[:], pattern=[[SEQ, R]], base=0, channel_multiplier=1,
                      allow_small_or_imprecise_dtypes=True).then_inc(pool_link, 1)
            pool.iota(tile_no[:], pattern=[[1, TILES]], base=0, channel_multiplier=0,
                      allow_small_or_imprecise_dtypes=True).then_inc(pool_link, 1)
            pool.iota(expert_no[:], pattern=[[1, EXPERTS]], base=0, channel_multiplier=0,
                      allow_small_or_imprecise_dtypes=True).then_inc(pool_link, 1)
            pool.iota(region[:], pattern=[[CAP, EXPERTS]], base=0, channel_multiplier=0,
                      allow_small_or_imprecise_dtypes=True).then_inc(pool_link, 1)
            pool.iota(next_row[:], pattern=[[CAP, EXPERTS]], base=0, channel_multiplier=0,
                      allow_small_or_imprecise_dtypes=True).then_inc(pool_link, 1)
            pool.wait_ge(pool_link, 12)
            pool.iota(pad_rows[:, :, ROW_ID], pattern=[[1, SUB]], base=N_TOK, channel_multiplier=SUB,
                      allow_small_or_imprecise_dtypes=True).then_inc(pool_link, 1)
            pool.wait_ge(pool_link, 13)
            pool.affine_select(out=tie[:], in_=tie[:], compare_op=ALU.is_ge, fill=1e-37, base=0,
                               pattern=[[1, 4], [-1, 4]], channel_multiplier=0).then_inc(pool_link, 1)
            pool.wait_ge(pool_link, 14)
            pool.affine_select(out=tie[:], in_=tie[:], compare_op=ALU.not_equal, fill=1.0, base=0,
                               pattern=[[1, 4], [-1, 4]], channel_multiplier=0).then_inc(pool_link, 1)
            pool.wait_ge(pool_link, 15)
            pool.affine_select(out=before[:], in_=before[:], compare_op=ALU.is_ge, fill=1.0, base=0,
                               pattern=[[-1, P]], channel_multiplier=1).then_inc(pool_link, 1)
            pool.wait_ge(pool_link, 16)
            pool.memset(no_carry[:, :, 0:1], 0.0).then_inc(tables, 1)
            pool.wait_ge(tables, 1)
            pool.memset(marker[:], 0.0).then_inc(marked, 1)
            pool.dma_start(routed[EXPERTS * CAP:EXPERTS * CAP + TILE, :].rearrange("(p s) c -> p s c", s=SUB),
                           pad_rows[:]).then_inc(scattered, 16)
            pool.wait_ge(bn_var, 1)
            pool.tensor_scalar(bn[:, 2:3], bn[:, 1:2], EPS, None, ALU.add).then_inc(bn_rstd, 1)
            pool.wait_ge(bn_rstd, 1)
            pool.tensor_tensor(bn[:, 3:4], bn[:, 2:3], minus_half[:, 0:1], ALU.pow).then_inc(bn_rstd, 1)

            def step(n, u, group):
                ks = [k for k, b in ((0, n + 3), (1, n - 5)) if ok(b)]
                if ks:
                    a, z = ks[0], ks[-1] + 1
                    need_step(pool, mv_ready, n, LN_FIRST, LN_LAST)
                    pool.tensor_tensor(var_eps[:, u % 2, a:z], mv[:, u % 2, a:z, 1], eps_t[0:SEQ, a:z], ALU.add).then_inc(ln_link, 1)
                    need_step(pool, ln_link, n, LN_FIRST, LN_LAST)
                    pool.tensor_tensor(rstd[:, u % 2, a:z], var_eps[:, u % 2, a:z], minus_half[0:SEQ, a:z],
                                       ALU.pow).then_inc(rstd_ready, 1)
                if ok(n - 5):
                    need(pool, xn2_ready, n - 5)
                    pool.tensor_copy(xn_all[0:SEQ, ds((n - 5) * D, D)],
                                     xn2[:, (u - 5) % 2, :]).then_inc(row_ready, 1)
            def mark(before):
                pool.wait_ge(marked, before + 1)
                pool.tensor_tensor(marker[:], eps_t[:, 0:1], eps_t[:, 0:1], ALU.add).then_inc(marked, 1)

            def route(g):
                pool.wait_ge(stage_ready, g + 1)
                mark(g)
                for b in range(R):
                    for k in range(PICKED):
                        pool.indirect_dma_start(
                            out=routed, out_offset=bass.IndirectOffsetOnAxis(ap=slots[:, k * R + b:k * R + b + 1], axis=0),
                            in_=stage[:, b, :], in_offset=None).then_inc(scattered, 16)
            steps(pool, step, route)

            pool.wait_ge(resid_out, 16 * (ROUTES + 1))

            def add_rows(t, u):
                pool.wait_ge(y_rows_ready, t + 1)
                if since(t, 1):
                    pool.wait_ge(added, t * (16 * SUB))
                mark(ROUTES + t)
                for s in range(SUB):
                    pool.indirect_dma_start(
                        out=out, out_offset=bass.IndirectOffsetOnAxis(ap=out_ids[:, u % ROWS, s:s + 1], axis=0),
                        in_=y_rows[:, u % 2, s, :], in_offset=None, compute_op=ALU.add).then_inc(added, 16)

            def weights_lo(t, u):
                for q in range(HC):
                    pool.wait_ge(w_hi_done, t * HC + (q + 1))
                    r = slice(q * W_COLS // HC, (q + 1) * W_COLS // HC)
                    pool.tensor_tensor(w_lo[:, u % 2, r], w_raw[:, u % 2, r], w_hi[:, u % 2, r].bitcast(F32),
                                       ALU.subtract).then_inc(w_lo_done, 1)

            def tile(t, u):
                if is_tile(t + 1):
                    weights_lo(t + 1, u + 1)
                if is_tile(t - 2):
                    add_rows(t - 2, u - 2)
            weights_lo(0, 0)
            tiles(pool, tile)
            add_rows(TILES - 2, ROWS - 2)
            add_rows(TILES - 1, ROWS - 1)

        @block.tensor
        def _(pe):
            pe.wait_ge(w_in, 16 * 7)
            for c in range(CHUNKS):
                if c % 4 == 0:
                    pe.wait_ge(x_in[c // 4], 32)
                    if c // 4 < 3:
                        pe.wait_ge(x_in[c // 4 + 1], 32)
                if c >= 2:
                    pe.wait_ge(conv_read, c - 1)
                for i, rows in ((0, P), (2, P), (4, 64)):
                    src = conv_in[0:rows, c * CHUNK_B * TIME:(c + 1) * CHUNK_B * TIME].rearrange("p (b t) -> p b t", t=TIME)
                    mm = pe.matmul(conv_ps[c % 2][:, 0:CHUNK], conv_sb[0:rows, i // 2, :], src[:, :, i:i + SEQ],
                                   start=(i == 0), stop=(i == 4))
                mm.then_inc(conv_done, 1)
            pe.wait_ge(conv_read, CHUNKS)
            pe.wait_ge(consts, 10)

            def prefix(g):
                pe.wait_ge(sel_ready, g + 1)
                pe.matmul(prefix_ps, before[:, 0:SEQ], sel[:], start=True, stop=True)
                pe.matmul(total_ps, ones_b[:], sel[:], start=True, stop=True).then_inc(prefix_done, 1)
                pe.wait_ge(prefix_read, g + 1)

            def step(n, u, group):
                if ok(n):
                    need(pe, proj_read, n)
                    need(pe, scores_read, n - 1)
                    for half in range(2):
                        r = slice(64 * half, 64 * half + 64)
                        mm = pe.matmul(scores_ps[0:SEQ, half, 0:4 * SEQ], q_cm[r, u % 2, :],
                                       v_heads[r, u % 2, :, :], start=True, stop=True)
                    mm.then_inc(scores_done, 1)
                if u % R == ROUTE_AT + 1 and not (isinstance(n, int) and n < LOOP_FIRST):
                    prefix(group)
                if ok(n + 2):
                    need_step(pe, tr3_read, n - 1, TR3_FIRST, TR3_LAST)
                    need(pe, proj_read, n + 1)
                    x = cm3[:, (u - 1) % 2, 0, :]
                    pe.matmul(qT_ps, wq_sb, x, start=True, stop=True)
                    pe.matmul(qrT_ps, wqr_sb, x, start=True, stop=True)
                    pe.matmul(vT_ps, wv_sb, x, start=True, stop=True)
                    pe.matmul(v_ps, x, wv_sb, start=True, stop=True).then_inc(proj_done, 1)
                if ok(n - 2):
                    need(pe, pt_read, n - 2)
                    need(pe, att_ready, n - 3)
                    for h in range(HEADS):
                        g, s = h % 4, h // 4
                        mm = pe.matmul(o_cm_ps[32 * g:32 * g + 32, s, :], v_tok[:, (u - 2) % 4, h, :],
                                       probs_t[:, u % 2, h, :], start=True, stop=True)
                    mm.then_inc(pv_done, 1)
                if ok(n - 1):
                    need(pe, exp_done, n - 1)
                    need(pe, pt_read, n - 2)
                    for h in range(HEADS):
                        mm = pe.transpose(pt_ps[0:SEQ, h // 4, (h % 4) * SEQ:(h % 4 + 1) * SEQ],
                                          probs[:, (u - 1) % 2, h, :], ident[0:SEQ, 0:SEQ])
                    mm.then_inc(pt_done, 1)
                if ok(n - 2):
                    need(pe, o_read, n - 2)
                    for s in range(2):
                        mm = pe.transpose(o_ps[0:SEQ, s * D:(s + 1) * D], o_sb[:, u % 2, s, :], ident[:])
                    mm.then_inc(otr_done, 1)
                group = [(0, n + 3, xn_ready, xn[:, (u + 3) % 2, :]),
                         (1, n - 3, att_ready, att[:, (u - 3) % 2, :, :].rearrange("p h e -> p (h e)")),
                         (2, n - 5, xn2_ready, xn2[:, (u - 5) % 2, :])]
                group = [g for g in group if ok(g[1])]
                if group:
                    need_step(pe, tr3_read, n - 1, TR3_FIRST, TR3_LAST)
                    for k, b, ready, src in group:
                        need(pe, ready, b)
                        mm = pe.transpose(act_ps[:, k * SEQ:(k + 1) * SEQ], src, ident[0:SEQ, 0:SEQ])
                    mm.then_inc(tr3_done, 1)
                todo = [ok(n + 4), ok(n - 4), ok(n - 6)]
                if any(todo):
                    need_step(pe, tr3_read, n - 1, TR3_FIRST, TR3_LAST)
                    need(pe, small_read, n + 3)
                    need(pe, h1_done, n - 5)
                    need(pe, logits_done, n - 7)
                    if todo[0]:
                        need(pe, h_ready, n + 4)
                        mm = pe.transpose(h_tok_ps, h_cm[:, u % 2, :], ident[:])
                    if todo[1]:
                        mm = pe.matmul(wo_ps, cm3[:, (u - 1) % 2, 1, :], wo_sb, start=True, stop=True)
                    if todo[2]:
                        mm = pe.matmul(logit_ps, cm3[:, (u - 1) % 2, 2, :], route_sb[:], start=True, stop=True)
                    mm.then_inc(small_done, 1)
            steps(pe, step)

            def product(ps, w, x, start, stop):
                (w_h, w_l), (x_h, x_l) = w, x
                pe.matmul(ps, w_h, x_h, start=start, stop=False)
                pe.matmul(ps, w_h, x_l, start=False, stop=False)
                return pe.matmul(ps, w_l, x_h, start=False, stop=stop)

            def w_part_of(k, i, c):
                r = slice((c * 3 + i) * P, (c * 3 + i + 1) * P)
                return w_hi[:, k, r], w_lo[:, k, r]

            def x_transpose(t, u):
                pe.wait_ge(rows_in[u % ROWS], loads(t, u, ROWS))
                if since(t, 1):
                    pe.wait_ge(x_read, t)
                for s in range(SUB):
                    mm = pe.transpose(x_ps[:, s * P:(s + 1) * P], x_rows[:, u % ROWS, s, 0:D], ident[:])
                mm.then_inc(x_done, 1)

            def down(t, u, c):
                pe.wait_ge(hid_ready, t * HC + (c + 1))
                if c == 0 and since(t, 2):
                    pe.wait_ge(y_read, t - 1)
                product(y_ps[u % 2][:], w_part_of(u % 2, 2, c), (hid_hi[:, c, :], hid_lo[:, c, :]), c == 0,
                        c == HC - 1).then_inc(down_done, 1)

            def y_transpose(t):
                pe.wait_ge(y_read, t + 1)
                if since(t, 1):
                    pe.wait_ge(y_rows_ready, t)
                for s in range(SUB):
                    mm = pe.transpose(y_tok_ps[:, s * P:(s + 1) * P], y_cm[:, s * P:(s + 1) * P], ident[:])
                mm.then_inc(y_tok_done, 1)

            def tile(t, u):
                x = (x_hi[:, u % 2, :], x_lo[:, u % 2, :])
                for c in range(HC):
                    if c == 0:
                        pe.wait_ge(x_read, t + 1)
                    pe.wait_ge(w_lo_done, t * HC + (c + 1))
                    if since(t, 1) or c >= 2:
                        pe.wait_ge(silu_done, t * HC + (c - 1))
                        pe.wait_ge(hid_done, t * HC + (c - 1))
                    product(gate_ps[c % 2], w_part_of(u % 2, 0, c), x, True, True).then_inc(gate_done, 1)
                    product(up_ps[c % 2], w_part_of(u % 2, 1, c), x, True, True).then_inc(up_done, 1)
                    if c < 2 and is_tile(t - 1):
                        down(t - 1, u - 1, HC - 2 + c)
                    if c >= 2:
                        down(t, u, c - 2)
                    if c == 2 and is_tile(t - 1):
                        y_transpose(t - 1)
                    if c == 0 and is_tile(t + 1):
                        x_transpose(t + 1, u + 1)
            x_transpose(0, 0)
            tiles(pe, tile)
            down(TILES - 1, TILES - 1, HC - 2)
            down(TILES - 1, TILES - 1, HC - 1)
            y_transpose(TILES - 1)

        @block.scalar
        def _(act):
            act.wait_ge(w_in, 16 * 7)
            for c in range(CHUNKS):
                act.wait_ge(conv_done, c + 1)
                nc.scalar.activation(y_all[:, c * CHUNK:(c + 1) * CHUNK], conv_ps[c % 2][:, 0:CHUNK], ACT.Relu,
                                     bias=conv_b).then_inc(conv_read, 1)
            act.wait_ge(bn_ready, 1)

            def step(n, u, group):
                if ok(n + 4):
                    need_step(act, small_done, n - 2, SMALL_FIRST, SMALL_LAST)
                    nc.scalar.activation(h_cm[:, u % 2, :], y_all[:, ds((n + 4) * SEQ, SEQ)], ACT.Identity,
                                         bias=bn[:, 5:6], scale=bn[:, 4:5]).then_inc(h_ready, 1)
                if ok(n - 2):
                    need(act, pv_done, n - 2)
                    need(act, otr_done, n - 4)
                    nc.scalar.activation(o_sb[:, u % 2, :, :], o_cm_ps, ACT.Copy).then_inc(o_read, 1)
                if ok(n - 1):
                    need(act, pt_done, n - 1)
                    need(act, pv_done, n - 3)
                    for half in range(2):
                        cp = nc.scalar.activation(probs_t[:, (u - 1) % 2, 4 * half:4 * half + 4, :],
                                                  pt_ps[0:SEQ, half, 0:4 * SEQ].rearrange("p (h s) -> p h s", s=SEQ),
                                                  ACT.Copy)
                    cp.then_inc(pt_read, 1)
                if ok(n):
                    need(act, scores_read, n)
                    nc.scalar.activation(probs[:, u % 2, :, :], probs[:, u % 2, :, :], ACT.Exp).then_inc(exp_done, 1)
                ks = [k for k, b in ((0, n + 3), (1, n - 3), (2, n - 5)) if ok(b)]
                if ks:
                    need_step(act, tr3_done, n, TR3_FIRST, TR3_LAST)
                    need(act, proj_done, n + 1)
                    need_step(act, small_done, n - 1, SMALL_FIRST, SMALL_LAST)
                    runs = [ks] if ks[-1] - ks[0] + 1 == len(ks) else [[k] for k in ks]
                    for r in runs:
                        a, z = r[0], r[-1] + 1
                        cp = nc.scalar.activation(cm3[:, u % 2, a:z, :],
                                                  act_ps[:, a * SEQ:z * SEQ].rearrange("p (k s) -> p k s", s=SEQ),
                                                  ACT.Copy)
                    cp.then_inc(tr3_read, 1)
            def route(g):
                act.wait_ge(row_ready, g * R + R)
                act.wait_ge(scattered, g * (16 * PICKED * R) + 16)
                act.wait_ge(tables, 1)
                nc.scalar.activation(stage[:, :, 0:D], xn_all[0:SEQ, ds(g * (R * D), R * D)].rearrange("p (b d) -> p b d", d=D),
                                     ACT.Copy).then_inc(stage_x, 1)
                act.wait_ge(less_ready, g + 1)
                nc.scalar.activation(less[:], less[:], ACT.Exp).then_inc(exps_ready, 1)
            steps(act, step, route)

            def weights_hi(t, u, q):
                if q == 0:
                    act.wait_ge(weights_in[u % 2], loads(t, u, 2))
                if since(t, 2):
                    act.wait_ge(down_done, t * HC + (q + 1 - 2 * HC))
                r = slice(q * W_COLS // HC, (q + 1) * W_COLS // HC)
                nc.scalar.activation(w_hi[:, u % 2, r], w_raw[:, u % 2, r], ACT.Copy).then_inc(w_hi_done, 1)

            def hidden_hi(t, c):
                act.wait_ge(hid_done, t * HC + (c + 1))
                if since(t, 1):
                    act.wait_ge(down_done, t * HC + (c + 1 - HC))
                nc.scalar.activation(hid_hi[:, c, :], hid[:, c % 2, :], ACT.Copy).then_inc(hid_hi_done, 1)

            def x_round(t, u):
                act.wait_ge(x_done, t + 1)
                if since(t, 2):
                    act.wait_ge(up_done, t * HC - HC)
                nc.scalar.activation(x_hi[:, u % 2, :], x_ps[:], ACT.Copy).then_inc(x_hi_done, 1)

            def out_cm(t, u):
                act.wait_ge(down_done, t * HC + HC)
                if since(t, 1):
                    act.wait_ge(y_tok_done, t)
                nc.scalar.activation(y_cm, y_ps[u % 2][:], ACT.Copy).then_inc(y_read, 1)

            def tile(t, u):
                for c in range(HC):
                    act.wait_ge(gate_done, t * HC + (c + 1))
                    if since(t, 1) or c >= 2:
                        act.wait_ge(hid_done, t * HC + (c - 1))
                    nc.scalar.activation(silu[:, c % 2, :], gate_ps[c % 2], ACT.Silu).then_inc(silu_done, 1)
                    if c == 2 and is_tile(t - 1):
                        out_cm(t - 1, u - 1)
                    if is_tile(t + 1):
                        if c == 1:
                            x_round(t + 1, u + 1)
                        weights_hi(t + 1, u + 1, c)
                    hidden_hi(t, c)
            for q in range(HC):
                weights_hi(0, 0, q)
            x_round(0, 0)
            tiles(act, tile)
            out_cm(TILES - 1, ROWS - 1)

        @block.vector
        def _(dve):
            for c in range(CHUNKS):
                dve.wait_ge(conv_read, c + 1)
                st = nc.vector.bn_stats(stats_y[:, c, :], y_all[:, c * CHUNK:(c + 1) * CHUNK])
            st.then_inc(stats_done, 1)
            dve.wait_ge(stats_done, 1)
            nc.vector.bn_aggr(bn[:, 0:2], stats_y[:]).then_inc(bn_var, 1)
            dve.wait_ge(bn_rstd, 2)
            nc.vector.tensor_tensor(bn[:, 4:5], bn[:, 3:4], gamma_c, ALU.mult).then_inc(bn_link, 1)
            dve.wait_ge(bn_link, 1)
            nc.vector.tensor_tensor(bn[:, 2:3], bn[:, 0:1], bn[:, 4:5], ALU.mult).then_inc(bn_link, 1)
            dve.wait_ge(bn_link, 2)
            nc.vector.tensor_tensor(bn[:, 5:6], beta_c, bn[:, 2:3], ALU.subtract).then_inc(bn_ready, 1)

            def step(n, u, group):
                p = u % 2
                x, r2 = (u + 3) % 2, (u - 5) % 2
                has1, has2, has3 = ok(n + 3), ok(n - 5), ok(n - 7)
                if has1 or has2 or has3:
                    need_step(dve, small_done, n - 1, SMALL_FIRST, SMALL_LAST)
                if has1:
                    nc.vector.bn_stats(stat6[:, 0, :], h_tok_ps).then_inc(stats1_done, 1)
                if has2:
                    h1 = resid[:, ds(n - 5, 1), :].rearrange("p b d -> p (b d)")
                    nc.vector.scalar_tensor_tensor(out=h1, in0=wo_ps, scalar=shift1[:, ds(n - 5, 1)], in1=h1,
                                                   op0=ALU.add, op1=ALU.add).then_inc(h1_done, 1)
                    need(dve, h1_done, n - 5)
                if has3:
                    nc.vector.tensor_tensor(logits[:, ds(n - 7, 1), :].rearrange("p b l -> p (b l)"), logit_ps,
                                            route_b, ALU.add).then_inc(logits_done, 1)
                if has2:
                    nc.vector.bn_stats(stat6[:, 1, :], h1).then_inc(stats2_done, 1)
                need(dve, otr_done, n - 3)
                if has1:
                    need(dve, stats1_done, n + 3)
                need(dve, stats2_done, n - 5)
                if ok(n - 3):
                    nc.vector.reciprocal(rz[:], o_tok_ps[:, :, DH]).then_inc(rz_done, 1)
                if has1:
                    ag = nc.vector.bn_aggr(mv[:, p, 0, :], stat6[:, 0, :])
                if has2:
                    ag = nc.vector.bn_aggr(mv[:, p, 1, :], stat6[:, 1, :])
                if has1 or has2:
                    ag.then_inc(mv_ready, 1)
                if ok(n - 3):
                    need(dve, rz_done, n - 3)
                    need_step(dve, tr3_done, n - 2, TR3_FIRST, TR3_LAST)
                    nc.vector.tensor_tensor(att[:, (u - 3) % 2, :, :], o_tok_ps[:, :, 0:DH],
                                            rz[:].unsqueeze(2).broadcast_to([SEQ, HEADS, DH]),
                                            ALU.mult).then_inc(att_ready, 1)
                if ok(n):
                    need(dve, scores_done, n)
                    sc = scores_ps[0:SEQ, :, 0:4 * SEQ].rearrange("p a (h j) -> p a h j", j=SEQ)
                    mx = row_max[:].rearrange("p (a h) -> p a h", a=2)
                    nc.vector.tensor_reduce(mx, sc, AX.X, ALU.max).then_inc(max_done, 1)
                    need(dve, max_done, n)
                    need(dve, pt_done, n - 2)
                    nc.vector.tensor_tensor(probs[:, p, :, :].rearrange("p (a h) j -> p a h j", a=2), sc,
                                            mx.unsqueeze(3).broadcast_to([SEQ, 2, 4, SEQ]),
                                            ALU.subtract).then_inc(scores_read, 1)
                if has1 or has2:
                    need_step(dve, rstd_ready, n, LN_FIRST, LN_LAST)
                if has1:
                    sh = shift1[:, ds(n + 3, 1)]
                    nc.vector.scalar_tensor_tensor(out=sh, in0=mv[:, p, 0, 0:1], scalar=-1.0, in1=rstd[:, p, 0:1],
                                                   op0=ALU.mult, op1=ALU.mult)
                    nc.vector.tensor_scalar(rstd1[:, p:p + 1], rstd[:, p, 0:1], 1.0, None, ALU.add).then_inc(shift1_done, 1)
                if has2:
                    nc.vector.scalar_tensor_tensor(out=shift2[:, p:p + 1], in0=mv[:, p, 1, 0:1], scalar=-1.0,
                                                   in1=rstd[:, p, 1:2], op0=ALU.mult, op1=ALU.mult).then_inc(shift2_done, 1)
                need_step(dve, tr3_done, n - 2, TR3_FIRST, TR3_LAST)
                if has1:
                    need(dve, shift1_done, n + 3)
                    nc.vector.tensor_scalar(xn[:, x, :], h_tok_ps, rstd[:, p, 0:1], sh, ALU.mult, ALU.add).then_inc(xn_ready, 1)
                if has2:
                    need(dve, shift2_done, n - 5)
                    need(dve, row_ready, n - 7)
                    nc.vector.tensor_scalar(xn2[:, r2, :], h1, rstd[:, p, 1:2], shift2[:, p:p + 1],
                                            ALU.mult, ALU.add).then_inc(xn2_ready, 1)
                if has1:
                    nc.vector.scalar_tensor_tensor(out=resid[:, ds(n + 3, 1), :].rearrange("p b d -> p (b d)"),
                                                   in0=h_tok_ps, scalar=rstd1[:, p:p + 1], in1=bo_row,
                                                   op0=ALU.mult, op1=ALU.add).then_inc(small_read, 1)
                if ok(n + 2):
                    need(dve, proj_done, n + 2)
                    need(dve, pv_done, n - 2)
                    nc.vector.scalar_tensor_tensor(out=q_a[:], in0=qT_ps, scalar=bq_c, in1=rope_sb[:, 0, :],
                                                   op0=ALU.add, op1=ALU.mult)
                    nc.vector.scalar_tensor_tensor(out=q_b[:], in0=qrT_ps, scalar=bqr_c, in1=rope_sb[:, 1, :],
                                                   op0=ALU.add, op1=ALU.mult).then_inc(rope_link, 1)
                    nc.vector.scalar_tensor_tensor(out=v_heads[:, p, :, :],
                                                   in0=vT_ps.unsqueeze(1).broadcast_to([P, 4, SEQ]), scalar=bv_c,
                                                   in1=head_mask[:].unsqueeze(2).broadcast_to([P, 4, SEQ]),
                                                   op0=ALU.add, op1=ALU.mult)
                    nc.vector.tensor_tensor(v_tok[:, (u + 2) % 4, :, 0:DH], v_ps.rearrange("p (h e) -> p h e", e=DH),
                                            bv_row.rearrange("p (h e) -> p h e", e=DH), ALU.add)
                    need(dve, rope_link, n + 2)
                    nc.vector.tensor_tensor(q_cm[:, p, :], q_a[:], q_b[:], ALU.add).then_inc(proj_read, 1)
            links = sem("route_step")

            def route(g):
                at = [0]

                def link(ins):
                    at[0] += 1
                    ins.then_inc(links, 1)
                    dve.wait_ge(links, g * ROUTE_LINKS + at[0])
                lg = logits[:, ds(g * R, R), :].rearrange("p b (q i) -> p (b q) i", i=4)
                prob = less[:].rearrange("p (q i) -> p q i", i=4)

                def over(x, n=4):
                    return x.unsqueeze(2).broadcast_to([SEQ, R * PROBS, n])
                dve.wait_ge(logits_done, g * R + R)
                link(nc.vector.tensor_reduce(pmax[:], lg, AX.X, ALU.max))
                nc.vector.tensor_tensor(prob, lg, over(pmax[:]), ALU.subtract).then_inc(less_ready, 1)
                dve.wait_ge(exps_ready, g + 1)
                link(nc.vector.tensor_reduce(part[:], prob, AX.X, ALU.add))
                link(nc.vector.reciprocal(first_p[:], part[:]))
                link(nc.vector.tensor_tensor(prob, prob, over(first_p[:]), ALU.mult))
                q4 = [SEQ, R * PROBS, 4, 4]
                link(nc.vector.tensor_tensor(pairs[:], prob.unsqueeze(2).broadcast_to(q4), prob.unsqueeze(3).broadcast_to(q4),
                                             ALU.subtract))
                link(nc.vector.tensor_tensor(pairs[:].rearrange("p q i j -> p q (i j)"), pairs[:].rearrange("p q i j -> p q (i j)"),
                                             tie[:].rearrange("p i j -> p (i j)").unsqueeze(1).broadcast_to([SEQ, R * PROBS, 16]),
                                             ALU.is_ge))
                link(nc.vector.tensor_reduce(rank[:].rearrange("p (q i) -> p q i", i=4), pairs[:], AX.X, ALU.add))
                nc.vector.tensor_scalar(picks[:, 0, :, :].rearrange("p b l -> p (b l)"), rank[:], 0.0, None, ALU.is_equal)
                nc.vector.tensor_scalar(picks[:, 1, :, :].rearrange("p b l -> p (b l)"), rank[:], 1.0, None, ALU.is_equal)
                link(nc.vector.tensor_scalar(chosen[:].rearrange("p b l -> p (b l)"), rank[:], 2.0, None, ALU.is_lt))
                ch_g = chosen[:, :, 0:GROUPS]
                ch_e = chosen[:, :, GROUPS:].rearrange("p b (g e) -> p b g e", e=PER_GROUP)
                nc.vector.tensor_tensor(sel[:].rearrange("p (g e) b -> p g e b", e=PER_GROUP),
                                        ch_e.rearrange("p b g e -> p g e b"),
                                        ch_g.rearrange("p b g -> p g b").unsqueeze(2).broadcast_to([SEQ, GROUPS, PER_GROUP, R]),
                                        ALU.mult).then_inc(sel_ready, 1)
                flat = weigh[:, 0, :, :].rearrange("p b l -> p (b l)")
                link(nc.vector.tensor_tensor(flat, less[:], picks[:, 1, :, :].rearrange("p b l -> p (b l)"), ALU.mult))
                link(nc.vector.tensor_reduce(second_p[:], flat.rearrange("p (q i) -> p q i", i=4), AX.X, ALU.add))
                link(nc.vector.tensor_tensor(part[:], first_p[:], second_p[:], ALU.add))
                link(nc.vector.tensor_scalar(part[:], part[:], TOP_P, None, ALU.is_le))
                link(nc.vector.tensor_tensor(second_p[:], second_p[:], part[:], ALU.mult))
                link(nc.vector.tensor_tensor(part[:], first_p[:], second_p[:], ALU.add))
                link(nc.vector.tensor_scalar(part[:], part[:], 1e-9, None, ALU.add))
                link(nc.vector.reciprocal(pmax[:], part[:]))
                nc.vector.tensor_tensor(ratio[:, 0, :], first_p[:], pmax[:], ALU.mult)
                link(nc.vector.tensor_tensor(ratio[:, 1, :], second_p[:], pmax[:], ALU.mult))
                half = ratio[:].rearrange("p k (b q) -> p k b q", q=PROBS)[:, :, :, 0]
                link(nc.vector.tensor_scalar(half, half, GROUPS ** -0.5, None, ALU.mult))
                for k in range(2):
                    last = nc.vector.tensor_tensor(weigh[:, k, :, :].rearrange("p b (q i) -> p (b q) i", i=4),
                                                   picks[:, k, :, :].rearrange("p b (q i) -> p (b q) i", i=4),
                                                   over(ratio[:, k, :]), ALU.mult)
                link(last)
                link(nc.vector.tensor_tensor(weigh[:, 0, :, :], weigh[:, 0, :, :], weigh[:, 1, :, :], ALU.add))
                dve.wait_ge(stage_x, g + 1)
                nc.vector.tensor_tensor(stage[:, :, ROW_W:ROW_ID].rearrange("p b (g e) -> p b g e", e=PER_GROUP),
                                        weigh[:, 0, :, GROUPS:].rearrange("p b (g e) -> p b g e", e=PER_GROUP),
                                        weigh[:, 0, :, 0:GROUPS].unsqueeze(3).broadcast_to([SEQ, R, GROUPS, PER_GROUP]),
                                        ALU.mult)
                nc.vector.tensor_copy(stage[:, :, ROW_ID], tok_id[:])
                link(nc.vector.tensor_scalar(tok_id[:], tok_id[:], float(R * SEQ), None, ALU.add))
                dve.wait_ge(prefix_done, g + 1)
                link(nc.vector.tensor_tensor_scan(total[:].rearrange("p e b -> p (e b)"), no_carry[:].rearrange("p e b -> p (e b)"),
                                                  total_ps.rearrange("p e b -> p (e b)"), 0.0, ALU.mult, ALU.add))
                pl = place[:].rearrange("p b e -> p e b")
                link(nc.vector.tensor_tensor(pl, prefix_ps, total[0:SEQ, :, :], ALU.add))
                link(nc.vector.tensor_tensor(pl, pl, total_ps[0:SEQ], ALU.subtract))
                last = nc.vector.tensor_tensor(place[:], place[:], next_row[0:SEQ, :].unsqueeze(1).broadcast_to([SEQ, R, EXPERTS]),
                                               ALU.add)
                last.then_inc(prefix_read, 1)
                dve.wait_ge(prefix_read, g + 1)
                nc.vector.tensor_tensor(next_row[:], next_row[:], total[:, :, R - 1], ALU.add)
                link(nc.vector.tensor_tensor(place2[:], picks[:, :, :, GROUPS:],
                                             place[:].unsqueeze(1).broadcast_to([SEQ, 2, R, EXPERTS]), ALU.mult))
                link(nc.vector.tensor_reduce(by_group[:].rearrange("p k b g -> p (k b g)"),
                                             place2[:].rearrange("p k b (g e) -> p (k b g) e", e=PER_GROUP), AX.X, ALU.add))
                for gp in range(2):
                    last = nc.vector.tensor_tensor(by_pick[:, gp, :, :, :], by_group[:],
                                                   picks[:, gp, :, 0:GROUPS].unsqueeze(1).broadcast_to([SEQ, 2, R, GROUPS]), ALU.mult)
                link(last)
                link(nc.vector.tensor_reduce(slots_f[:], by_pick[:].rearrange("p a k b g -> p (a k b) g"), AX.X, ALU.add))
                dve.wait_ge(scattered, g * (16 * PICKED * R) + 16)
                nc.vector.tensor_copy(slots[:], slots_f[:]).then_inc(stage_ready, 1)
                assert at[0] == ROUTE_LINKS, at
            steps(dve, step, route)

            count = [0]

            def link(ins):
                count[0] += 1
                ins.then_inc(table_link, 1)
                dve.wait_ge(table_link, count[0])
            dve.wait_ge(stage_ready, ROUTES)
            nc.vector.tensor_copy(ends_i[:], next_row[:]).then_inc(ends_ready, 1)
            link(nc.vector.tensor_tensor(n_tiles[:], next_row[:], region[:], ALU.subtract))
            link(nc.vector.tensor_scalar(n_tiles_i[:], n_tiles[:], float(TILE - 1), None, ALU.add))
            link(nc.vector.tensor_scalar(n_tiles_i[:], n_tiles_i[:], TILE.bit_length() - 1, None, ALU.logical_shift_right))
            link(nc.vector.tensor_copy(n_tiles[:], n_tiles_i[:]))
            link(nc.vector.tensor_tensor_scan(last_tile[:], ones_e[:], n_tiles[:], 0.0, ALU.mult, ALU.add))
            t_e = [P, TILES, EXPERTS]
            link(nc.vector.tensor_tensor(past[:], tile_no[:].unsqueeze(2).broadcast_to(t_e),
                                         last_tile[:].unsqueeze(1).broadcast_to(t_e), ALU.is_ge))
            nc.vector.tensor_tensor(past2[:], past[:], n_tiles[:].unsqueeze(1).broadcast_to(t_e), ALU.mult)
            link(nc.vector.tensor_reduce(tile_e[:], past[:], AX.X, ALU.add))
            link(nc.vector.tensor_reduce(tile_s[:], past2[:], AX.X, ALU.add))
            nc.vector.tensor_tensor(past[:], tile_e[:].unsqueeze(2).broadcast_to(t_e),
                                    expert_no[:].unsqueeze(1).broadcast_to(t_e), ALU.is_equal)
            nc.vector.tensor_scalar(tile_v[:], tile_e[:], float(EXPERTS), float(TILE), ALU.is_lt, ALU.mult)
            link(nc.vector.tensor_tensor(tile_s[:], tile_no[:], tile_s[:], ALU.subtract))
            link(nc.vector.tensor_tensor(tile_s[:], tile_s[:], tile_v[:], ALU.mult))
            link(nc.vector.scalar_tensor_tensor(out=tile_row_i[:], in0=tile_e[:], scalar=float(CAP), in1=tile_s[:],
                                                op0=ALU.mult, op1=ALU.add))
            nc.vector.tensor_scalar(tile_e_i[:], tile_e[:], float(EXPERTS - 1), None, ALU.min).then_inc(table_ready, 1)

            def x_rest(t, u):
                dve.wait_ge(x_hi_done, t + 1)
                nc.vector.tensor_tensor(x_lo[:, u % 2, :], x_ps[:], x_hi[:, u % 2, :].bitcast(F32), ALU.subtract).then_inc(x_read, 1)

            def hidden_lo(t, c):
                dve.wait_ge(hid_hi_done, t * HC + (c + 1))
                nc.vector.tensor_tensor(hid_lo[:, c, :], hid[:, c % 2, :], hid_hi[:, c, :].bitcast(F32),
                                        ALU.subtract).then_inc(hid_ready, 1)

            def weights(t, u):
                dve.wait_ge(rows_in[u], loads(t, u, ROWS))
                nc.vector.tensor_tensor(w_part[:], x_rows[:, u, :, ROW_W:ROW_ID],
                                        past[:, ds(t, 1), :].broadcast_to([P, SUB, EXPERTS]), ALU.mult).then_inc(w_link, 1)
                dve.wait_ge(w_link, t + 1)
                nc.vector.tensor_reduce(w_row[:, u, :], w_part[:], AX.X, ALU.add).then_inc(w_link2, 1)
                if since(t, ROWS):
                    dve.wait_ge(added, (t - (ROWS - 1)) * (16 * SUB))
                nc.vector.tensor_copy(out_ids[:, u, :], x_rows[:, u, :, ROW_ID]).then_inc(ids_ready, 1)

            def out_half(t, u, half):
                if half == 0:
                    dve.wait_ge(y_tok_done, t + 1)
                    dve.wait_ge(w_link2, t + 1)
                    if since(t, 2):
                        dve.wait_ge(added, (t - 1) * (16 * SUB))
                for s in range(half * SUB // 2, (half + 1) * SUB // 2):
                    last = nc.vector.tensor_scalar(y_rows[:, u % 2, s, :], y_tok_ps[:, s * P:(s + 1) * P],
                                                   w_row[:, u % ROWS, s:s + 1], None, ALU.mult)
                if half == 1:
                    last.then_inc(y_rows_ready, 1)

            def tile(t, u):
                for c in range(HC):
                    dve.wait_ge(silu_done, t * HC + (c + 1))
                    dve.wait_ge(up_done, t * HC + (c + 1))
                    if since(t, 1) or c >= 2:
                        dve.wait_ge(hid_ready, t * HC + (c - 1))
                    nc.vector.tensor_tensor(hid[:, c % 2, :], silu[:, c % 2, :], up_ps[c % 2], ALU.mult).then_inc(hid_done, 1)
                    if c == 0 and is_tile(t - 2):
                        out_half(t - 2, u - 2, 1)
                    if c == 1:
                        weights(t, u)
                    if c == 2 and is_tile(t + 1):
                        x_rest(t + 1, u + 1)
                    if c == 3 and is_tile(t - 1):
                        out_half(t - 1, u - 1, 0)
                    hidden_lo(t, c)
            x_rest(0, 0)
            tiles(dve, tile)
            out_half(TILES - 2, ROWS - 2, 1)
            out_half(TILES - 1, ROWS - 1, 0)
            out_half(TILES - 1, ROWS - 1, 1)


def lay_out(inputs):
    a = {k: np.asarray(v) for k, v in inputs.items()}
    perm = np.arange(D).reshape(HEADS, 2, DH // 2)[:, ::-1, :].reshape(-1)
    theta = (1.0 / 10000.0 ** (np.arange(0, DH, 2, dtype=np.float32) / np.float32(DH))).astype(np.float32)
    angle = np.arange(SEQ, dtype=np.float32)[None, :] * np.tile(theta, 2 * HEADS)[:, None]
    sign = np.tile(np.repeat(np.array([-1.0, 1.0], np.float32), DH // 2), HEADS)[:, None]
    scale = np.float32(DH ** -0.5)
    gate, up = (a[k].reshape(EXPERTS, P, HC, P) for k in ("L0_ffn_W1", "L0_ffn_W3"))
    down = a["L0_ffn_W2"].reshape(EXPERTS, HC, P, D).transpose(0, 2, 1, 3)
    arrays = {
        "x_t": a["x"].reshape(BATCH * TIME, D_IN).T,
        "conv_w": a["L0_tok_W"].T,
        "col_params": np.stack([a["L0_tok_b"], a["L0_tok_gamma"], a["L0_tok_beta"], a["L0_attn_bq"],
                                a["L0_attn_bq"][perm], a["L0_attn_bv"]], axis=1),
        "row_params": np.concatenate([a["L0_attn_bv"], a["L0_attn_bo"], a["L0_ffn_br"], a["L0_ffn_bgate"].reshape(-1)]),
        "rope_tab": np.stack([np.cos(angle) * scale, np.sin(angle) * sign * scale]).astype(np.float32),
        "attn_w": np.stack([a["L0_attn_Wq"], a["L0_attn_Wq"][:, perm], a["L0_attn_Wv"], a["L0_attn_Wo"]]),
        "route_w": np.concatenate([a["L0_ffn_Wr"], a["L0_ffn_Wgate"].transpose(1, 0, 2).reshape(D, EXPERTS)], axis=1),
        "expert_w": np.stack([gate, up, down], axis=3).reshape(EXPERTS, P, 3 * HID),
    }
    return {k: np.ascontiguousarray(v) for k, v in arrays.items()}


def kernel(**inputs):
    import concourse.bacc as bacc
    from concourse.bass_utils import run_bass_kernel_spmd

    arrays = lay_out(inputs)
    nc = bacc.Bacc("TRN2", target_bir_lowering=False, num_devices=1)
    args = {k: nc.dram_tensor(k, a.shape, mybir.dt.from_np(a.dtype), kind="ExternalInput").ap() for k, a in arrays.items()}
    out = nc.dram_tensor("out", (N_TOK + TILE, D), F32, kind="ExternalOutput").ap()
    audio_tower(nc, out=out, **args)
    result = run_bass_kernel_spmd(nc, [arrays], core_ids=[0])
    return result.results[0]["out"][:N_TOK].reshape(BATCH, SEQ, D)
```

```python
from contextlib import ExitStack

import concourse.bass as bass
import numpy as np
from concourse import mybir

ALU = mybir.AluOpType
ACT = mybir.ActivationFunctionType
AX = mybir.AxisListType
F32 = mybir.dt.float32
F32R = mybir.dt.float32r
BF16 = mybir.dt.bfloat16
I32 = mybir.dt.int32
U32 = mybir.dt.uint32

BATCH, TIME, D_IN = 64, 125, 64
CONTEXT = 5
SEQ = TIME - (CONTEXT - 1)
N_TOK = BATCH * SEQ
D = 128
HEADS, DH = 8, 16
EPS = 1e-5
GROUPS, PER_GROUP = 4, 4
EXPERTS = GROUPS * PER_GROUP
PICKED = 4
HID = 512
HC = HID // 128
TOP_P = 0.9
P = 128

CHUNK_B = 4
CHUNKS = BATCH // CHUNK_B
CHUNK = CHUNK_B * SEQ

ROW_W = D
ROW_ID = D + EXPERTS
ROW = D + EXPERTS + 4
TILE = 512
SUB = TILE // P
CAP = N_TOK + TILE
TILES = (N_TOK * PICKED) // TILE + EXPERTS
LOGITS = GROUPS + EXPERTS
ROWS = 4
assert TILES % ROWS == 0

R = 8
ROUTES = BATCH // R
PROBS = 1 + GROUPS

ROUTE_BASE = 2 * R - 1
LOOP_GROUPS = (1, 5)
STEP_FIRST, STEP_END = -4, BATCH + R
SCATTERS = PICKED * R

STAGE_AT = 5

LAST, NEXT_TO_LAST, THIRD_LAST = ROUTES - 1, ROUTES - 2, ROUTES - 3
FIRST_PART = 0


TR3_FIRST, TR3_LAST = -3, BATCH + 4
SMALL_FIRST, SMALL_LAST = -4, BATCH + 5
LN_FIRST, LN_LAST = -3, BATCH + 4


def is_group(g, only):
    return isinstance(g, int) and g == only


def routed_group(g):
    return not isinstance(g, int) or 0 <= g < ROUTES


def parts_of(g, v):
    if is_group(g, LAST):
        when = {0: (2, 3, 4, 5, 6, 7)}
    elif is_group(g, NEXT_TO_LAST):
        when = {0: (2,), 1: (3, 4), 3: (5, 6, 7)}
    else:
        when = {1: (2,), 2: (3,), 3: (4,), 4: (5, 6), 5: (7,)}
    parts = [(g, part) for part in when.get(v, ())] if routed_group(g) else []
    return parts + ([(g + 1, FIRST_PART)] if v == R - 1 and routed_group(g + 1) else [])


def counted(g, v):
    return routed_group(g) and not is_group(g, LAST) and v == (2 if is_group(g, NEXT_TO_LAST) else 3)


def staged(g, v):
    at = 0 if is_group(g, LAST) else 3 if is_group(g, NEXT_TO_LAST) else STAGE_AT
    return routed_group(g) and v == at


def stage_buffer(g):
    return 1 if is_group(g, NEXT_TO_LAST) else 0


def scatters_of(g, v):
    def share(group, i, n):
        per = -(-SCATTERS // n)
        first, end = i * per, min((i + 1) * per, SCATTERS)
        return [(group, first, end)] if routed_group(group) and first < end else []
    if is_group(g, LAST):
        return share(g, 0, 1)
    if is_group(g, NEXT_TO_LAST):
        return share(g - 1, v + 2, 6) if v < 4 else share(g, v - 4, 4)
    if is_group(g, THIRD_LAST) and v > STAGE_AT:
        return share(g, v - STAGE_AT - 1, 6)
    return share(g, v - STAGE_AT - 1, R - 1) if v > STAGE_AT else share(g - 1, v + R - STAGE_AT - 1, R - 1)


def ds(at, n):
    return bass.ds(at, n)


def audio_tower(nc, x_t, conv_w, col_params, row_params, rope_tab, attn_w, route_w, expert_w, out):
    routed = nc.dram_tensor("routed", (EXPERTS * CAP + TILE, ROW), F32, kind="Internal").ap()
    with ExitStack() as ctx:
        def sb(name, shape, dt=F32):
            return ctx.enter_context(nc.sbuf_tensor(name, shape, dt))

        def sem(name):
            return ctx.enter_context(nc.semaphore(name))

        ident = sb("ident", [P, P])
        conv_sb = sb("conv_sb", [P, 3, D])
        colp = sb("colp", [P, 6])
        conv_b, gamma_c, beta_c, bq_c, bqr_c, bv_c = (colp[:, i:i + 1] for i in range(6))
        rowp = sb("rowp", [SEQ, 2 * D + LOGITS])
        bv_row, bo_row, route_b = rowp[:, 0:D], rowp[:, D:2 * D], rowp[:, 2 * D:2 * D + LOGITS]
        rope_sb = sb("rope_sb", [P, 2, SEQ])
        attn_sb = sb("attn_sb", [P, 4, D])
        wq_sb, wqr_sb, wv_sb, wo_sb = (attn_sb[:, i, :] for i in range(4))
        route_sb = sb("route_sb", [P, LOGITS])
        head_mask = sb("head_mask", [P, 4])
        bv_heads = sb("bv_heads", [P, 4])
        minus_half = sb("minus_half", [P, 2])
        marker = sb("marker", [P, 1])
        ones_e = sb("ones_e", [P, EXPERTS])
        eps_t = sb("eps_t", [P, 2])

        conv_in = sb("conv_in", [P, BATCH * TIME])
        y_all = conv_in[:, 0:N_TOK]
        resid = sb("resid", [SEQ, BATCH, D])
        xn_all = sb("xn_all", [P, BATCH * D])
        logits = sb("logits", [SEQ, R, LOGITS])
        stats_y = sb("stats_y", [P, CHUNKS, 6])
        bn = sb("bn", [P, 6])

        h_cm = sb("h_cm", [P, 2, SEQ])
        stat6 = sb("stat6", [SEQ, 2, 6])
        mv = sb("mv", [SEQ, 2, 2, 2])
        var_eps = sb("var_eps", [SEQ, 2, 2])
        rstd = sb("rstd", [SEQ, 2, 2])
        shift1 = sb("shift1", [SEQ, BATCH])
        shift2 = sb("shift2", [SEQ, 2])
        rstd1 = sb("rstd1", [SEQ, 2])
        xn = sb("xn", [SEQ, 2, D])
        xn2 = sb("xn2", [SEQ, 2, D])
        cm3 = sb("cm3", [P, 2, 3, SEQ])
        q_a = sb("q_a", [P, SEQ])
        q_b = sb("q_b", [P, SEQ])
        q_cm = sb("q_cm", [P, 2, SEQ])
        v_heads = sb("v_heads", [P, 2, 4, SEQ])
        v_tok = sb("v_tok", [SEQ, 4, HEADS, 32])
        row_low = sb("row_low", [SEQ, 2, HEADS])
        probs = sb("probs", [SEQ, 2, HEADS, SEQ])
        probs_t = sb("probs_t", [SEQ, 2, HEADS, SEQ])
        o_sb = sb("o_sb", [P, 2, 2, SEQ])
        rz = sb("rz", [SEQ, HEADS])
        att = sb("att", [SEQ, 2, HEADS, DH])

        less = sb("less", [SEQ, 160])
        pmax = sb("pmax", [SEQ, R * PROBS])
        first_p = sb("first_p", [SEQ, R * PROBS])
        second_p = sb("second_p", [SEQ, R * PROBS])
        part = sb("part", [SEQ, R * PROBS])
        ratio = sb("ratio", [SEQ, 2, R * PROBS])
        pairs = sb("pairs", [SEQ, R * PROBS, 4, 4])
        tie = sb("tie", [SEQ, 4, 4])
        rank = sb("rank", [SEQ, R * PROBS * 4])
        picks = sb("picks", [SEQ, 2, R, LOGITS])
        weigh = sb("weigh", [SEQ, 2, R, LOGITS])
        chosen = sb("chosen", [SEQ, R, LOGITS])
        sel = sb("sel", [SEQ, EXPERTS, R], BF16)
        from_here = sb("from_here", [SEQ, P], BF16)
        ones_b = sb("ones_b", [SEQ, P], BF16)
        no_carry = sb("no_carry", [SEQ, EXPERTS, R])
        sel_upto = sb("sel_upto", [SEQ, EXPERTS, R], BF16)
        next_row = sb("next_row", [P, EXPERTS])
        flat = pairs[:].rearrange("p q i j -> p (q i j)")
        place = flat[:, 0:128].rearrange("p (b e) -> p b e", e=EXPERTS)
        place2 = flat[:, 128:384].rearrange("p (k b e) -> p k b e", k=2, e=EXPERTS)
        by_group = flat[:, 384:448].rearrange("p (k b g) -> p k b g", k=2, g=GROUPS)
        by_pick = flat[:, 448:576].rearrange("p (a k b g) -> p a k b g", a=2, k=2, g=GROUPS)
        slots_f = sb("slots_f", [SEQ, PICKED * R])
        slots = [sb(f"slots{i}", [SEQ, PICKED * R], U32) for i in range(2)]
        stages = [sb(f"stage{i}", [SEQ, R, ROW]) for i in range(2)]
        tok_id = sb("tok_id", [SEQ, R])
        pad_rows = sb("pad_rows", [P, SUB, ROW])
        tile_no = sb("tile_no", [P, TILES])
        expert_no = sb("expert_no", [P, EXPERTS])
        region = sb("region", [P, EXPERTS])
        n_tiles = sb("n_tiles", [P, EXPERTS])
        n_tiles_i = sb("n_tiles_i", [P, EXPERTS], I32)
        last_tile = sb("last_tile", [P, EXPERTS])
        tile_row_i = sb("tile_row_i", [P, TILES], I32)
        tile_e_i = sb("tile_e_i", [P, TILES], I32)
        ends_i = sb("ends_i", [P, EXPERTS], I32)
        W_COLS = 3 * HID
        w_hi, w_lo = (sb(n, [P, 2, W_COLS], F32R) for n in ("w_hi", "w_lo"))
        x_hi, x_lo = (sb(n, [P, 2, TILE], F32R) for n in ("x_hi", "x_lo"))
        hid_hi, hid_lo = (sb(n, [P, HC, TILE], F32R) for n in ("hid_hi", "hid_lo"))
        taken = {}

        def in_place_of(name, old, copies, n=TILE):
            at = taken.get(name, 0)
            taken[name] = at + copies * n
            return old[:, at:at + copies * n].rearrange("p (k n) -> p k n", k=copies)
        w_raw = in_place_of("input", conv_in, 2, W_COLS)
        y_cm = in_place_of("input", conv_in, 1)[:, 0, :]
        y_rows = in_place_of("input", conv_in, 2).rearrange("p k (s d) -> p k s d", s=SUB)
        silu, hid = (in_place_of("input", conv_in, 2) for _ in range(2))
        x_rows = in_place_of("norm", xn_all, ROWS, SUB * ROW).rearrange("p k (s c) -> p k s c", s=SUB)
        tile_e, tile_s, tile_v = (in_place_of("norm", xn_all, 1, TILES)[:, 0, :] for _ in range(3))
        past, past2 = (in_place_of("norm", xn_all, TILES, EXPERTS) for _ in range(2))
        w_part = in_place_of("norm", xn_all, SUB, EXPERTS)
        w_row = sb("w_row", [P, ROWS, SUB])
        out_ids = sb("out_ids", [P, ROWS, SUB], U32)

        def bank(name, shape=(P, 512)):
            return ctx.enter_context(nc.psum_tensor(name, list(shape), F32))

        scores_ps = bank("scores_ps", (P, 2, 512))
        pt_ps = bank("pt_ps", (P, 2, 512))
        proj_ps = bank("proj_ps")
        dve_ps = bank("dve_ps")
        act_ps = bank("act_ps")
        o_ps = bank("o_ps")
        conv_ps = [proj_ps, dve_ps]
        counts_at = 2 * D + LOGITS
        count_ps = dve_ps[0:SEQ, counts_at:counts_at + EXPERTS * R].rearrange("p (e b) -> p e b", b=R)
        total_ps = dve_ps[:, counts_at + EXPERTS * R:counts_at + EXPERTS * (R + 1)]
        gate_ps, up_ps = [scores_ps[:, i, :] for i in range(2)], [pt_ps[:, i, :] for i in range(2)]
        x_ps, y_ps, y_tok_ps = act_ps, [o_ps, proj_ps], dve_ps
        qT_ps, qrT_ps = (proj_ps[:, i * SEQ:(i + 1) * SEQ] for i in range(2))
        vT_ps = act_ps[:, 3 * SEQ:4 * SEQ]
        v_ps = proj_ps[0:SEQ, 2 * SEQ:2 * SEQ + D]
        h_tok_ps, wo_ps, logit_ps = dve_ps[0:SEQ, 0:D], dve_ps[0:SEQ, D:2 * D], dve_ps[0:SEQ, 2 * D:2 * D + LOGITS]
        o_cm_ps = o_ps[:, 0:2 * SEQ].rearrange("p (s i) -> p s i", s=2)
        o_tok_ps = o_ps[0:SEQ, 0:2 * D].rearrange("p (h e) -> p h e", e=32)

        conv_w_in, w_in = sem("conv_w_in"), sem("w_in")
        x_in = [sem(f"x_in{i}") for i in range(4)]
        consts = sem("consts")
        conv_done, conv_read, stats_done = sem("conv_done"), sem("conv_read"), sem("stats_done")
        bn_link, bn_var, bn_rstd, bn_ready = sem("bn_link"), sem("bn_var"), sem("bn_rstd"), sem("bn_ready")
        h_ready, heads_ready = sem("h_ready"), sem("heads_ready")
        scores_done, scores_read, exp_done = sem("scores_done"), sem("scores_read"), sem("exp_done")
        otr_done, att_ready = sem("otr_done"), sem("att_ready")
        tr3_done, tr3_read = sem("tr3_done"), sem("tr3_read")
        pt_done, pt_read = sem("pt_done"), sem("pt_read")
        proj_done, proj_read = sem("proj_done"), sem("proj_read")
        pv_done, o_read = sem("pv_done"), sem("o_read")
        small_done, small_read = sem("small_done"), sem("small_read")
        mv_ready, ln_link, rstd_ready = sem("mv_ready"), sem("ln_link"), sem("rstd_ready")
        xn_ready, xn2_ready, row_ready = sem("xn_ready"), sem("xn2_ready"), sem("row_ready")
        stats1_done, h1_done, stats2_done, logits_done = sem("stats1_done"), sem("h1_done"), sem("stats2_done"), sem("logits_done")
        rz_done, shift1_done, shift2_done = sem("rz_done"), sem("shift1_done"), sem("shift2_done")
        eps_set = sem("eps_set")
        tables, pool_link = sem("tables"), sem("pool_link")
        route_link = sem("route_link")
        less_ready, exps_ready, sel_ready, counts_done, counts_read, place_ready = (
            sem(n) for n in ("less_ready", "exps_ready", "sel_ready", "counts_done", "counts_read", "place_ready"))
        pairs_ready, picks_ready, shares_ready, weigh_ready, by_group_ready, slots_ready = (
            sem(n) for n in ("pairs_ready", "picks_ready", "shares_ready", "weigh_ready", "by_group_ready", "slots_ready"))
        LINKS = {0: 1, 2: 3, 3: 4, 4: 7, 5: 2, 6: 1, 7: 1}
        links_of = {v: sem(f"route_link{v}") for v in LINKS}
        stage_x, stage_ready = sem("stage_x"), sem("stage_ready")
        scattered = [sem(f"scattered{i}") for i in range(2)]
        ends_ready, pads_in, table_ready, resid_out = sem("ends_ready"), sem("pads_in"), sem("table_ready"), sem("resid_out")
        table_link, hid_free = sem("table_link"), sem("hid_free")
        rows_in = [sem(f"rows_in{i}") for i in range(ROWS)]
        weights_in = [sem(f"weights_in{i}") for i in range(2)]
        x_done, x_read, gate_done, up_done, silu_done, hid_ready = (
            sem(n) for n in ("x_done", "x_read", "gate_done", "up_done", "silu_done", "hid_ready"))
        x_hi_done, w_hi_done, w_lo_done, hid_done, hid_hi_done = (
            sem(n) for n in ("x_hi_done", "w_hi_done", "w_lo_done", "hid_done", "hid_hi_done"))
        y_done, y_read, y_tok_done, w_link, w_link2, ids_ready, y_rows_ready, added, down_done = (
            sem(n) for n in ("y_done", "y_read", "y_tok_done", "w_link", "w_link2", "ids_ready", "y_rows_ready", "added",
                             "down_done"))
        low_done, rope_link = sem("low_done"), sem("rope_link")
        marked = sem("marked")

        def ok(b):
            return not isinstance(b, int) or 0 <= b < BATCH

        def need(eng, s, b):
            if isinstance(b, int):
                if b < 0:
                    return
                b = min(b, BATCH - 1)
            eng.wait_ge(s, b + 1)

        def need_step(eng, s, n, first, last):
            if isinstance(n, int):
                if n < first:
                    return
                n = min(n, last)
            eng.wait_ge(s, n - first + 1)

        def steps(eng, step, route=None):
            def run(n, u, g, v):
                if not isinstance(n, int) or n < BATCH + R:
                    step(n, u, g, v)
                if route is not None:
                    route(g, v)
            for n in range(STEP_FIRST, ROUTE_BASE + R * LOOP_GROUPS[0]):
                run(n, n, (n - ROUTE_BASE) // R, (n - ROUTE_BASE) % R)
            with eng.Fori(*LOOP_GROUPS) as g:
                for v in range(R):
                    run(g * R + (ROUTE_BASE + v), ROUTE_BASE + v, g, v)
            for n in range(ROUTE_BASE + R * LOOP_GROUPS[1], STEP_END):
                run(n, n, (n - ROUTE_BASE) // R, (n - ROUTE_BASE) % R)

        def stage_free(eng, g):
            if not is_group(g, NEXT_TO_LAST):
                before = NEXT_TO_LAST if is_group(g, LAST) else g
                eng.wait_ge(scattered[0], before * (16 * SCATTERS) + 16)

        def tiles(eng, tile):
            for t in range(ROWS):
                tile(t, t)
            with eng.Fori(1, TILES // ROWS - 1) as i:
                for u in range(ROWS):
                    tile(i * ROWS + u, u)
            for t in range(TILES - ROWS, TILES):
                tile(t, t % ROWS)

        def since(t, first):
            return not isinstance(t, int) or t >= first

        def is_tile(t):
            return not isinstance(t, int) or 0 <= t < TILES

        def loads(t, u, ring):
            return (t - u % ring) * (16 // ring) + 16

        block = ctx.enter_context(nc.Block())

        @block.sync
        def _(sp):
            sp.dma_start(conv_sb[:, 0:2, :], conv_w[0:2 * P, :].rearrange("(c p) o -> p c o", p=P)).then_inc(conv_w_in, 16)
            sp.dma_start(conv_sb[0:64, 2, :], conv_w[2 * P:2 * P + 64, :]).then_inc(conv_w_in, 16)
            sp.dma_start(colp[:], col_params).then_inc(conv_w_in, 16)
            n = BATCH * TIME // 4
            for i in range(4):
                sp.dma_start(conv_in[0:64, i * n:(i + 1) * n], x_t[:, i * n:(i + 1) * n]).then_inc(x_in[i], 16)
                hi = min((i + 1) * n, BATCH * TIME - 1)
                sp.dma_start(conv_in[64:128, i * n:hi], x_t[:, i * n + 1:hi + 1]).then_inc(x_in[i], 16)
            sp.dma_start(attn_sb[:], attn_w.rearrange("w p o -> p w o")).then_inc(w_in, 16)
            sp.dma_start(rope_sb[:], rope_tab.rearrange("w p s -> p w s")).then_inc(w_in, 16)
            sp.dma_start(route_sb[:], route_w).then_inc(w_in, 16)
            sp.dma_start(rowp[:], row_params.rearrange("(a n) -> a n", a=1).broadcast_to([SEQ, 2 * D + LOGITS])).then_inc(w_in, 16)
            sp.wait_ge(tables, 1)
            out_b = out[0:N_TOK, :].rearrange("(b s) d -> s b d", s=SEQ)

            def store_residual(g):
                sp.wait_ge(h1_done, g * R + R)
                sp.dma_start(out_b[:, ds(g * R, R), :], resid[:, ds(g * R, R), :]).then_inc(resid_out, 16)
            with sp.Fori(0, ROUTES) as g:
                store_residual(g)
            sp.dma_start(out[N_TOK:N_TOK + TILE, :].rearrange("(p s) d -> p s d", s=SUB),
                         pad_rows[:, :, 0:D]).then_inc(resid_out, 16)
            sp.wait_ge(ends_ready, 1)
            for e in range(EXPERTS):
                end = sp.value_load(ends_i[0:1, e:e + 1], min_val=e * CAP, max_val=e * CAP + N_TOK)
                sp.dma_start(routed[ds(end, TILE), :].rearrange("(p s) c -> p s c", s=SUB),
                             pad_rows[:]).then_inc(pads_in, 16)
            sp.wait_ge(table_ready, 1)

            def load_tile(t, u):
                e = sp.value_load(tile_e_i[0:1, ds(t, 1)], min_val=0, max_val=EXPERTS - 1)
                row = sp.value_load(tile_row_i[0:1, ds(t, 1)], min_val=0, max_val=EXPERTS * CAP)
                if since(t, 2):
                    sp.wait_ge(w_lo_done, t * HC - HC)
                sp.dma_start(w_raw[:, u % 2, :], expert_w[ds(e, 1), :, :].rearrange("e p n -> p (e n)")).then_inc(weights_in[u % 2], 16)
                if since(t, ROWS):
                    sp.wait_ge(x_done, t - (ROWS - 1))
                    sp.wait_ge(ids_ready, t - (ROWS - 1))
                if isinstance(t, int) and t == 0:
                    sp.wait_ge(pads_in, 16 * EXPERTS)
                    sp.wait_ge(scattered[0], 16 * SCATTERS * (ROUTES - 1) + 16)
                    sp.wait_ge(scattered[1], 16 * SCATTERS)
                sp.dma_start(x_rows[:, u, :, :], routed[ds(row, TILE), :].rearrange("(p s) c -> p s c", s=SUB)).then_inc(rows_in[u], 16)
            tiles(sp, load_tile)
            sp.wait_ge(added, 16 * SUB * TILES)

        @block.gpsimd
        def _(pool):
            pool.memset(ident[:], 0.0).then_inc(consts, 1)
            pool.memset(v_tok[:], 0.0).then_inc(consts, 1)
            pool.memset(minus_half[:], -0.5).then_inc(consts, 1)
            pool.memset(head_mask[:], 1.0).then_inc(consts, 1)
            pool.memset(eps_t[:], EPS).then_inc(eps_set, 1)
            pool.wait_ge(consts, 4)
            pool.wait_ge(eps_set, 1)
            pool.affine_select(out=ident[:], in_=ident[:], compare_op=ALU.not_equal, fill=1.0, base=0,
                               pattern=[[-1, P]], channel_multiplier=1).then_inc(consts, 1)
            pool.wait_ge(consts, 5)
            pool.memset(v_tok[:, :, :, DH:DH + 1], 1.0).then_inc(consts, 1)
            pool.wait_ge(consts, 6)
            for half in range(2):
                m = head_mask[64 * half:64 * half + 64, :]
                pool.affine_select(out=m, in_=m, compare_op=ALU.is_ge, fill=0.0, base=0,
                                   pattern=[[-DH, 4]], channel_multiplier=1).then_inc(consts, 1)
                pool.wait_ge(consts, 7 + 2 * half)
                pool.affine_select(out=m, in_=m, compare_op=ALU.is_ge, fill=0.0, base=DH - 1,
                                   pattern=[[DH, 4]], channel_multiplier=-1).then_inc(consts, 1)
                pool.wait_ge(consts, 8 + 2 * half)

            pool.memset(ones_e[:], 1.0).then_inc(pool_link, 1)
            pool.memset(pad_rows[:], 0.0).then_inc(pool_link, 1)
            pool.memset(tie[:], 0.0).then_inc(pool_link, 1)
            pool.memset(from_here[:], -1.0).then_inc(pool_link, 1)
            pool.memset(ones_b[:], 1.0).then_inc(pool_link, 1)
            pool.memset(no_carry[:], 1.0).then_inc(pool_link, 1)
            pool.memset(stages[0][:, :, ROW_ID + 1:ROW], 0.0).then_inc(pool_link, 1)
            pool.memset(stages[1][:, :, ROW_ID + 1:ROW], 0.0).then_inc(pool_link, 1)
            pool.iota(tok_id[:], pattern=[[SEQ, R]], base=0, channel_multiplier=1,
                      allow_small_or_imprecise_dtypes=True).then_inc(pool_link, 1)
            pool.iota(tile_no[:], pattern=[[1, TILES]], base=0, channel_multiplier=0,
                      allow_small_or_imprecise_dtypes=True).then_inc(pool_link, 1)
            pool.iota(expert_no[:], pattern=[[1, EXPERTS]], base=0, channel_multiplier=0,
                      allow_small_or_imprecise_dtypes=True).then_inc(pool_link, 1)
            pool.iota(region[:], pattern=[[CAP, EXPERTS]], base=0, channel_multiplier=0,
                      allow_small_or_imprecise_dtypes=True).then_inc(pool_link, 1)
            pool.iota(next_row[:], pattern=[[CAP, EXPERTS]], base=0, channel_multiplier=0,
                      allow_small_or_imprecise_dtypes=True).then_inc(pool_link, 1)
            pool.wait_ge(pool_link, 13)
            pool.iota(pad_rows[:, :, ROW_ID], pattern=[[1, SUB]], base=N_TOK, channel_multiplier=SUB,
                      allow_small_or_imprecise_dtypes=True).then_inc(pool_link, 1)
            pool.wait_ge(pool_link, 14)
            pool.affine_select(out=tie[:], in_=tie[:], compare_op=ALU.is_ge, fill=1e-37, base=0,
                               pattern=[[1, 4], [-1, 4]], channel_multiplier=0).then_inc(pool_link, 1)
            pool.wait_ge(pool_link, 15)
            pool.affine_select(out=tie[:], in_=tie[:], compare_op=ALU.not_equal, fill=1.0, base=0,
                               pattern=[[1, 4], [-1, 4]], channel_multiplier=0).then_inc(pool_link, 1)
            pool.wait_ge(pool_link, 16)
            pool.affine_select(out=from_here[:], in_=from_here[:], compare_op=ALU.is_ge, fill=0.0, base=0,
                               pattern=[[-1, P]], channel_multiplier=1).then_inc(pool_link, 1)
            pool.wait_ge(pool_link, 17)
            pool.memset(no_carry[:, :, 0:1], 0.0).then_inc(tables, 1)
            pool.wait_ge(tables, 1)
            pool.memset(marker[:], 0.0).then_inc(marked, 1)
            pool.dma_start(routed[EXPERTS * CAP:EXPERTS * CAP + TILE, :].rearrange("(p s) c -> p s c", s=SUB),
                           pad_rows[:]).then_inc(scattered[0], 16)
            pool.wait_ge(bn_var, 1)
            pool.tensor_scalar(bn[:, 2:3], bn[:, 1:2], EPS, None, ALU.add).then_inc(bn_rstd, 1)
            pool.wait_ge(bn_rstd, 1)
            pool.tensor_tensor(bn[:, 3:4], bn[:, 2:3], minus_half[:, 0:1], ALU.pow).then_inc(bn_rstd, 1)

            def step(n, u, g, v):
                ks = [k for k, b in ((0, n + 3), (1, n - 5)) if ok(b)]
                if ks:
                    a, z = ks[0], ks[-1] + 1
                    need_step(pool, mv_ready, n, LN_FIRST, LN_LAST)
                    pool.tensor_tensor(var_eps[:, u % 2, a:z], mv[:, u % 2, a:z, 1], eps_t[0:SEQ, a:z], ALU.add).then_inc(ln_link, 1)
                    need_step(pool, ln_link, n, LN_FIRST, LN_LAST)
                    pool.tensor_tensor(rstd[:, u % 2, a:z], var_eps[:, u % 2, a:z], minus_half[0:SEQ, a:z],
                                       ALU.pow).then_inc(rstd_ready, 1)
            def mark(before):
                pool.wait_ge(marked, before + 1)
                pool.tensor_tensor(marker[:], eps_t[:, 0:1], eps_t[:, 0:1], ALU.add).then_inc(marked, 1)

            def scatter(g, first, end):
                if first == 0:
                    pool.wait_ge(stage_x, g + 1)
                    pool.wait_ge(stage_ready, g + 1)
                    mark(g)
                k = stage_buffer(g)
                for i in range(first, end):
                    pool.indirect_dma_start(
                        out=routed, out_offset=bass.IndirectOffsetOnAxis(ap=slots[k][:, i:i + 1], axis=0),
                        in_=stages[k][:, i % R, :], in_offset=None).then_inc(scattered[k], 16)

            def route(g, v):
                for some in scatters_of(g, v):
                    scatter(*some)
            steps(pool, step, route)

            pool.wait_ge(resid_out, 16 * (ROUTES + 1))

            def add_rows(t, u):
                pool.wait_ge(y_rows_ready, t + 1)
                if since(t, 1):
                    pool.wait_ge(added, t * (16 * SUB))
                mark(ROUTES + t)
                for s in range(SUB):
                    pool.indirect_dma_start(
                        out=out, out_offset=bass.IndirectOffsetOnAxis(ap=out_ids[:, u % ROWS, s:s + 1], axis=0),
                        in_=y_rows[:, u % 2, s, :], in_offset=None, compute_op=ALU.add).then_inc(added, 16)

            def weights_lo(t, u):
                for q in range(HC):
                    pool.wait_ge(w_hi_done, t * HC + (q + 1))
                    r = slice(q * W_COLS // HC, (q + 1) * W_COLS // HC)
                    pool.tensor_tensor(w_lo[:, u % 2, r], w_raw[:, u % 2, r], w_hi[:, u % 2, r].bitcast(F32),
                                       ALU.subtract).then_inc(w_lo_done, 1)

            def tile(t, u):
                if is_tile(t + 1):
                    weights_lo(t + 1, u + 1)
                if is_tile(t - 2):
                    add_rows(t - 2, u - 2)
            weights_lo(0, 0)
            tiles(pool, tile)
            add_rows(TILES - 2, ROWS - 2)
            add_rows(TILES - 1, ROWS - 1)

        @block.tensor
        def _(pe):
            pe.wait_ge(conv_w_in, 16 * 3)
            for c in range(CHUNKS):
                if c % 4 == 0:
                    pe.wait_ge(x_in[c // 4], 32)
                if c >= 2:
                    pe.wait_ge(conv_read, c - 1)
                for i, rows in ((0, P), (2, P), (4, 64)):
                    src = conv_in[0:rows, c * CHUNK_B * TIME:(c + 1) * CHUNK_B * TIME].rearrange("p (b t) -> p b t", t=TIME)
                    mm = pe.matmul(conv_ps[c % 2][:, 0:CHUNK], conv_sb[0:rows, i // 2, :], src[:, :, i:i + SEQ],
                                   start=(i == 0), stop=(i == 4))
                mm.then_inc(conv_done, 1)
            pe.wait_ge(conv_read, CHUNKS)
            pe.wait_ge(consts, 10)
            pe.wait_ge(w_in, 16 * 4)

            def counts(g):
                pe.wait_ge(sel_ready, g + 1)
                pe.matmul(count_ps, ones_b[:, 0:SEQ], sel_upto[:], start=True, stop=False)
                pe.matmul(count_ps, from_here[:, 0:SEQ], sel[:], start=False, stop=True)
                pe.matmul(total_ps, ones_b[:], sel_upto[:, :, R - 1], start=True, stop=True).then_inc(counts_done, 1)

            def step(n, u, g, v):
                if ok(n):
                    need(pe, proj_read, n)
                    need(pe, heads_ready, n)
                    need(pe, exp_done, n - 1)
                    for half in range(2):
                        r = slice(64 * half, 64 * half + 64)
                        mm = pe.matmul(scores_ps[0:SEQ, half, 0:4 * SEQ], q_cm[r, u % 2, :],
                                       v_heads[r, u % 2, :, :], start=True, stop=True)
                    mm.then_inc(scores_done, 1)
                if ok(n + 2):
                    need_step(pe, tr3_read, n - 1, TR3_FIRST, TR3_LAST)
                    need(pe, proj_read, n + 1)
                    x = cm3[:, (u - 1) % 2, 0, :]
                    pe.matmul(qT_ps, wq_sb, x, start=True, stop=True)
                    pe.matmul(qrT_ps, wqr_sb, x, start=True, stop=True)
                    pe.matmul(v_ps, x, wv_sb, start=True, stop=True).then_inc(proj_done, 1)
                if ok(n - 2):
                    need(pe, pt_read, n - 2)
                    need(pe, att_ready, n - 3)
                    for h in range(HEADS):
                        q, s = h % 4, h // 4
                        mm = pe.matmul(o_cm_ps[32 * q:32 * q + 32, s, :], v_tok[:, (u - 2) % 4, h, :],
                                       probs_t[:, u % 2, h, :], start=True, stop=True)
                    mm.then_inc(pv_done, 1)
                if ok(n - 1):
                    need(pe, exp_done, n - 1)
                    need(pe, pt_read, n - 2)
                    for h in range(HEADS):
                        mm = pe.transpose(pt_ps[0:SEQ, h // 4, (h % 4) * SEQ:(h % 4 + 1) * SEQ],
                                          probs[:, (u - 1) % 2, h, :], ident[0:SEQ, 0:SEQ])
                    mm.then_inc(pt_done, 1)
                if ok(n - 2):
                    need(pe, o_read, n - 2)
                    for s in range(2):
                        mm = pe.transpose(o_ps[0:SEQ, s * D:(s + 1) * D], o_sb[:, u % 2, s, :], ident[:])
                    mm.then_inc(otr_done, 1)
                moved = [(0, n + 3, xn_ready, xn[:, (u + 3) % 2, :]),
                         (1, n - 3, att_ready, att[:, (u - 3) % 2, :, :].rearrange("p h e -> p (h e)")),
                         (2, n - 5, xn2_ready, xn2[:, (u - 5) % 2, :])]
                moved = [m for m in moved if ok(m[1])]
                if moved:
                    need_step(pe, tr3_read, n - 1, TR3_FIRST, TR3_LAST)
                    need(pe, heads_ready, n + 1)
                    if ok(n + 2):
                        pe.matmul(vT_ps, wv_sb, cm3[:, (u - 1) % 2, 0, :], start=True, stop=True)
                    for k, b, ready, src in moved:
                        need(pe, ready, b)
                        mm = pe.transpose(act_ps[:, k * SEQ:(k + 1) * SEQ], src, ident[0:SEQ, 0:SEQ])
                    mm.then_inc(tr3_done, 1)
                todo = [ok(n + 4), ok(n - 4), ok(n - 6)]
                if any(todo):
                    need_step(pe, tr3_read, n - 1, TR3_FIRST, TR3_LAST)
                    need(pe, small_read, n + 3)
                    need(pe, h1_done, n - 5)
                    need(pe, logits_done, n - 7)
                    if counted(g, v - 1):
                        pe.wait_ge(counts_read, g + 1)
                    if counted(g, v):
                        counts(g)
                    if todo[0]:
                        need(pe, h_ready, n + 4)
                        mm = pe.transpose(h_tok_ps, h_cm[:, u % 2, :], ident[:])
                    if todo[1]:
                        mm = pe.matmul(wo_ps, cm3[:, (u - 1) % 2, 1, :], wo_sb, start=True, stop=True)
                    if todo[2]:
                        mm = pe.matmul(logit_ps, cm3[:, (u - 1) % 2, 2, :], route_sb[:], start=True, stop=True)
                    mm.then_inc(small_done, 1)

            def route(g, v):
                if is_group(g, LAST):
                    need(pe, logits_done, BATCH - 1)
                    counts(g)
            steps(pe, step, route)

            def product(ps, w, x, start, stop):
                (w_h, w_l), (x_h, x_l) = w, x
                pe.matmul(ps, w_h, x_h, start=start, stop=False)
                pe.matmul(ps, w_h, x_l, start=False, stop=False)
                return pe.matmul(ps, w_l, x_h, start=False, stop=stop)

            def w_part_of(k, i, c):
                r = slice((c * 3 + i) * P, (c * 3 + i + 1) * P)
                return w_hi[:, k, r], w_lo[:, k, r]

            def x_transpose(t, u):
                pe.wait_ge(rows_in[u % ROWS], loads(t, u, ROWS))
                if since(t, 1):
                    pe.wait_ge(x_read, t)
                for s in range(SUB):
                    mm = pe.transpose(x_ps[:, s * P:(s + 1) * P], x_rows[:, u % ROWS, s, 0:D], ident[:])
                mm.then_inc(x_done, 1)

            def down(t, u, c):
                pe.wait_ge(hid_ready, t * HC + (c + 1))
                if c == 0 and since(t, 2):
                    pe.wait_ge(y_read, t - 1)
                product(y_ps[u % 2][:], w_part_of(u % 2, 2, c), (hid_hi[:, c, :], hid_lo[:, c, :]), c == 0,
                        c == HC - 1).then_inc(down_done, 1)

            def y_transpose(t):
                pe.wait_ge(y_read, t + 1)
                if since(t, 1):
                    pe.wait_ge(y_rows_ready, t)
                for s in range(SUB):
                    mm = pe.transpose(y_tok_ps[:, s * P:(s + 1) * P], y_cm[:, s * P:(s + 1) * P], ident[:])
                mm.then_inc(y_tok_done, 1)

            def tile(t, u):
                x = (x_hi[:, u % 2, :], x_lo[:, u % 2, :])
                for c in range(HC):
                    if c == 0:
                        pe.wait_ge(x_read, t + 1)
                    pe.wait_ge(w_lo_done, t * HC + (c + 1))
                    if since(t, 1) or c >= 2:
                        pe.wait_ge(silu_done, t * HC + (c - 1))
                        pe.wait_ge(hid_done, t * HC + (c - 1))
                    product(gate_ps[c % 2], w_part_of(u % 2, 0, c), x, True, True).then_inc(gate_done, 1)
                    product(up_ps[c % 2], w_part_of(u % 2, 1, c), x, True, True).then_inc(up_done, 1)
                    if c < 2 and is_tile(t - 1):
                        down(t - 1, u - 1, HC - 2 + c)
                    if c >= 2:
                        down(t, u, c - 2)
                    if c == 2 and is_tile(t - 1):
                        y_transpose(t - 1)
                    if c == 0 and is_tile(t + 1):
                        x_transpose(t + 1, u + 1)
            x_transpose(0, 0)
            tiles(pe, tile)
            down(TILES - 1, TILES - 1, HC - 2)
            down(TILES - 1, TILES - 1, HC - 1)
            y_transpose(TILES - 1)

        @block.scalar
        def _(act):
            act.wait_ge(conv_w_in, 16 * 3)
            for c in range(CHUNKS):
                act.wait_ge(conv_done, c + 1)
                nc.scalar.activation(y_all[:, c * CHUNK:(c + 1) * CHUNK], conv_ps[c % 2][:, 0:CHUNK], ACT.Relu,
                                     bias=conv_b).then_inc(conv_read, 1)
            act.wait_ge(bn_ready, 1)

            def step(n, u, g, v):
                if ok(n + 4):
                    need_step(act, small_done, n - 2, SMALL_FIRST, SMALL_LAST)
                    nc.scalar.activation(h_cm[:, u % 2, :], y_all[:, ds((n + 4) * SEQ, SEQ)], ACT.Identity,
                                         bias=bn[:, 5:6], scale=bn[:, 4:5]).then_inc(h_ready, 1)
                if ok(n - 2):
                    need(act, pv_done, n - 2)
                    need(act, otr_done, n - 4)
                    nc.scalar.activation(o_sb[:, u % 2, :, :], o_cm_ps, ACT.Copy).then_inc(o_read, 1)
                if ok(n):
                    need(act, low_done, n)
                    need(act, pt_done, n - 2)
                    for h in range(HEADS):
                        ex = nc.scalar.activation(probs[:, u % 2, h, :], scores_ps[0:SEQ, h // 4, (h % 4) * SEQ:(h % 4 + 1) * SEQ],
                                                  ACT.Exp, bias=row_low[:, u % 2, h:h + 1], scale=-1.0)
                    ex.then_inc(exp_done, 1)
                if ok(n - 1):
                    need(act, pt_done, n - 1)
                    need(act, pv_done, n - 3)
                    for half in range(2):
                        cp = nc.scalar.activation(probs_t[:, (u - 1) % 2, 4 * half:4 * half + 4, :],
                                                  pt_ps[0:SEQ, half, 0:4 * SEQ].rearrange("p (h s) -> p h s", s=SEQ),
                                                  ACT.Copy)
                    cp.then_inc(pt_read, 1)
                ks = [k for k, b in ((0, n + 3), (1, n - 3), (2, n - 5)) if ok(b)]
                if ks:
                    need_step(act, tr3_done, n, TR3_FIRST, TR3_LAST)
                    need(act, proj_done, n + 1)
                    need_step(act, small_done, n - 1, SMALL_FIRST, SMALL_LAST)
                    runs = [ks] if ks[-1] - ks[0] + 1 == len(ks) else [[k] for k in ks]
                    for r in runs:
                        a, z = r[0], r[-1] + 1
                        cp = nc.scalar.activation(cm3[:, u % 2, a:z, :],
                                                  act_ps[:, a * SEQ:z * SEQ].rearrange("p (k s) -> p k s", s=SEQ),
                                                  ACT.Copy)
                    cp.then_inc(tr3_read, 1)
                if ok(n + 2):
                    need(act, scores_done, n)
                    for h in range(4):
                        cp = nc.scalar.activation(v_heads[:, u % 2, h, :], vT_ps, ACT.Identity,
                                                  bias=bv_heads[:, h:h + 1], scale=head_mask[:, h:h + 1])
                    cp.then_inc(heads_ready, 1)
                if ok(n - 5):
                    need(act, xn2_ready, n - 5)
                    act.wait_ge(tables, 1)
                    nc.scalar.activation(xn_all[0:SEQ, ds((n - 5) * D, D)], xn2[:, (u - 5) % 2, :], ACT.Copy).then_inc(row_ready, 1)
            def route(g, v):
                if staged(g, v):
                    act.wait_ge(row_ready, g * R + R)
                    stage_free(act, g)
                    nc.scalar.activation(stages[stage_buffer(g)][:, :, 0:D],
                                         xn_all[0:SEQ, ds(g * (R * D), R * D)].rearrange("p (b d) -> p b d", d=D),
                                         ACT.Copy).then_inc(stage_x, 1)
                if v == 0 and routed_group(g):
                    act.wait_ge(less_ready, g + 1)
                    nc.scalar.activation(less[:], less[:], ACT.Exp).then_inc(exps_ready, 1)
            steps(act, step, route)

            def weights_hi(t, u, q):
                if q == 0:
                    act.wait_ge(weights_in[u % 2], loads(t, u, 2))
                if since(t, 2):
                    act.wait_ge(down_done, t * HC + (q + 1 - 2 * HC))
                r = slice(q * W_COLS // HC, (q + 1) * W_COLS // HC)
                nc.scalar.activation(w_hi[:, u % 2, r], w_raw[:, u % 2, r], ACT.Copy).then_inc(w_hi_done, 1)

            def hidden_hi(t, c):
                act.wait_ge(hid_done, t * HC + (c + 1))
                if since(t, 1):
                    act.wait_ge(down_done, t * HC + (c + 1 - HC))
                nc.scalar.activation(hid_hi[:, c, :], hid[:, c % 2, :], ACT.Copy).then_inc(hid_hi_done, 1)

            def x_round(t, u):
                act.wait_ge(x_done, t + 1)
                if since(t, 2):
                    act.wait_ge(up_done, t * HC - HC)
                nc.scalar.activation(x_hi[:, u % 2, :], x_ps[:], ACT.Copy).then_inc(x_hi_done, 1)

            def out_cm(t, u):
                act.wait_ge(down_done, t * HC + HC)
                if since(t, 1):
                    act.wait_ge(y_tok_done, t)
                nc.scalar.activation(y_cm, y_ps[u % 2][:], ACT.Copy).then_inc(y_read, 1)

            def tile(t, u):
                for c in range(HC):
                    act.wait_ge(gate_done, t * HC + (c + 1))
                    if since(t, 1) or c >= 2:
                        act.wait_ge(hid_done, t * HC + (c - 1))
                    nc.scalar.activation(silu[:, c % 2, :], gate_ps[c % 2], ACT.Silu).then_inc(silu_done, 1)
                    if c == 2 and is_tile(t - 1):
                        out_cm(t - 1, u - 1)
                    if is_tile(t + 1):
                        if c == 1:
                            x_round(t + 1, u + 1)
                        weights_hi(t + 1, u + 1, c)
                    hidden_hi(t, c)
            for q in range(HC):
                weights_hi(0, 0, q)
            x_round(0, 0)
            tiles(act, tile)
            out_cm(TILES - 1, ROWS - 1)

        @block.vector
        def _(dve):
            for c in range(CHUNKS):
                dve.wait_ge(conv_read, c + 1)
                st = nc.vector.bn_stats(stats_y[:, c, :], y_all[:, c * CHUNK:(c + 1) * CHUNK])
            st.then_inc(stats_done, 1)
            dve.wait_ge(stats_done, 1)
            nc.vector.bn_aggr(bn[:, 0:2], stats_y[:]).then_inc(bn_var, 1)
            dve.wait_ge(consts, 10)
            dve.wait_ge(conv_w_in, 16 * 3)
            dve.wait_ge(w_in, 16 * 4)
            nc.vector.tensor_scalar(bv_heads[:], head_mask[:], bv_c, None, ALU.mult)
            dve.wait_ge(bn_rstd, 2)
            nc.vector.tensor_tensor(bn[:, 4:5], bn[:, 3:4], gamma_c, ALU.mult).then_inc(bn_link, 1)
            dve.wait_ge(bn_link, 1)
            nc.vector.tensor_tensor(bn[:, 2:3], bn[:, 0:1], bn[:, 4:5], ALU.mult).then_inc(bn_link, 1)
            dve.wait_ge(bn_link, 2)
            nc.vector.tensor_tensor(bn[:, 5:6], beta_c, bn[:, 2:3], ALU.subtract).then_inc(bn_ready, 1)

            def step(n, u, g, v):
                p = u % 2
                x, r2 = (u + 3) % 2, (u - 5) % 2
                has1, has2, has3 = ok(n + 3), ok(n - 5), ok(n - 7)
                if has1 or has2 or has3:
                    need_step(dve, small_done, n - 1, SMALL_FIRST, SMALL_LAST)
                if has1:
                    nc.vector.bn_stats(stat6[:, 0, :], h_tok_ps).then_inc(stats1_done, 1)
                if has2:
                    h1 = resid[:, ds(n - 5, 1), :].rearrange("p b d -> p (b d)")
                    nc.vector.scalar_tensor_tensor(out=h1, in0=wo_ps, scalar=shift1[:, ds(n - 5, 1)], in1=h1,
                                                   op0=ALU.add, op1=ALU.add).then_inc(h1_done, 1)
                    need(dve, h1_done, n - 5)
                if has3:
                    nc.vector.tensor_tensor(logits[:, (u - 7) % R, :], logit_ps,
                                            route_b, ALU.add).then_inc(logits_done, 1)
                if counted(g, v - 1):
                    read_counts(g)
                if has2:
                    nc.vector.bn_stats(stat6[:, 1, :], h1).then_inc(stats2_done, 1)
                need(dve, otr_done, n - 3)
                if has1:
                    need(dve, stats1_done, n + 3)
                need(dve, stats2_done, n - 5)
                if ok(n - 3):
                    nc.vector.reciprocal(rz[:], o_tok_ps[:, :, DH]).then_inc(rz_done, 1)
                if has1:
                    ag = nc.vector.bn_aggr(mv[:, p, 0, :], stat6[:, 0, :])
                if has2:
                    ag = nc.vector.bn_aggr(mv[:, p, 1, :], stat6[:, 1, :])
                if has1 or has2:
                    ag.then_inc(mv_ready, 1)
                if ok(n - 3):
                    need(dve, rz_done, n - 3)
                    need_step(dve, tr3_done, n - 2, TR3_FIRST, TR3_LAST)
                    nc.vector.tensor_tensor(att[:, (u - 3) % 2, :, :], o_tok_ps[:, :, 0:DH],
                                            rz[:].unsqueeze(2).broadcast_to([SEQ, HEADS, DH]),
                                            ALU.mult).then_inc(att_ready, 1)
                if ok(n):
                    need(dve, scores_done, n)
                    need(dve, exp_done, n - 2)
                    nc.vector.tensor_reduce(row_low[:, p, :].rearrange("p (a h) -> p a h", a=2),
                                            scores_ps[0:SEQ, :, 0:4 * SEQ].rearrange("p a (h j) -> p a h j", j=SEQ), AX.X,
                                            ALU.min).then_inc(low_done, 1)
                if has1 or has2:
                    need_step(dve, rstd_ready, n, LN_FIRST, LN_LAST)
                if has1:
                    sh = shift1[:, ds(n + 3, 1)]
                    nc.vector.scalar_tensor_tensor(out=sh, in0=mv[:, p, 0, 0:1], scalar=-1.0, in1=rstd[:, p, 0:1],
                                                   op0=ALU.mult, op1=ALU.mult)
                    nc.vector.tensor_scalar(rstd1[:, p:p + 1], rstd[:, p, 0:1], 1.0, None, ALU.add).then_inc(shift1_done, 1)
                if has2:
                    nc.vector.scalar_tensor_tensor(out=shift2[:, p:p + 1], in0=mv[:, p, 1, 0:1], scalar=-1.0,
                                                   in1=rstd[:, p, 1:2], op0=ALU.mult, op1=ALU.mult).then_inc(shift2_done, 1)
                need_step(dve, tr3_done, n - 2, TR3_FIRST, TR3_LAST)
                if has1:
                    need(dve, shift1_done, n + 3)
                    nc.vector.tensor_scalar(xn[:, x, :], h_tok_ps, rstd[:, p, 0:1], sh, ALU.mult, ALU.add).then_inc(xn_ready, 1)
                if has2:
                    need(dve, shift2_done, n - 5)
                    need(dve, row_ready, n - 7)
                    nc.vector.tensor_scalar(xn2[:, r2, :], h1, rstd[:, p, 1:2], shift2[:, p:p + 1],
                                            ALU.mult, ALU.add).then_inc(xn2_ready, 1)
                if has1:
                    nc.vector.scalar_tensor_tensor(out=resid[:, ds(n + 3, 1), :].rearrange("p b d -> p (b d)"),
                                                   in0=h_tok_ps, scalar=rstd1[:, p:p + 1], in1=bo_row,
                                                   op0=ALU.mult, op1=ALU.add).then_inc(small_read, 1)
                if ok(n + 2):
                    need(dve, proj_done, n + 2)
                    need(dve, pv_done, n - 2)
                    nc.vector.scalar_tensor_tensor(out=q_a[:], in0=qT_ps, scalar=bq_c, in1=rope_sb[:, 0, :],
                                                   op0=ALU.add, op1=ALU.mult)
                    nc.vector.scalar_tensor_tensor(out=q_b[:], in0=qrT_ps, scalar=bqr_c, in1=rope_sb[:, 1, :],
                                                   op0=ALU.add, op1=ALU.mult).then_inc(rope_link, 1)
                    nc.vector.tensor_tensor(v_tok[:, (u + 2) % 4, :, 0:DH], v_ps.rearrange("p (h e) -> p h e", e=DH),
                                            bv_row.rearrange("p (h e) -> p h e", e=DH), ALU.add)
                    need(dve, rope_link, n + 2)
                    nc.vector.tensor_tensor(q_cm[:, p, :], q_a[:], q_b[:], ALU.add).then_inc(proj_read, 1)
            def over(x, n=4):
                return x.unsqueeze(2).broadcast_to([SEQ, R * PROBS, n])
            prob = less[:].rearrange("p (q i) -> p q i", i=4)

            def read_counts(g):
                dve.wait_ge(counts_done, g + 1)
                nc.vector.tensor_tensor(place.rearrange("p b e -> p e b"), count_ps,
                                        next_row[0:SEQ, :].unsqueeze(2).broadcast_to([SEQ, EXPERTS, R]), ALU.add).then_inc(place_ready, 1)
                dve.wait_ge(place_ready, g + 1)
                nc.vector.tensor_tensor(next_row[:], next_row[:], total_ps, ALU.add).then_inc(counts_read, 1)

            def route(g, v):
                for group, part in parts_of(g, v):
                    if is_group(group, LAST) and part == 6:
                        read_counts(group)
                    route_part(group, part)
                if staged(g, v):
                    to_stage(g)

            def route_part(g, v):
                links, at = links_of[v], [0]
                steps_links = LINKS[v]

                def link(ins):
                    at[0] += 1
                    ins.then_inc(links, 1)
                    dve.wait_ge(links, g * steps_links + at[0])
                flat_picks = [picks[:, k, :, :].rearrange("p b l -> p (b l)") for k in range(2)]
                if v == 0:
                    lg = logits[:].rearrange("p b (q i) -> p (b q) i", i=4)
                    dve.wait_ge(logits_done, g * R + R)
                    link(nc.vector.tensor_reduce(pmax[:], lg, AX.X, ALU.max))
                    nc.vector.tensor_tensor(prob, lg, over(pmax[:]), ALU.subtract).then_inc(less_ready, 1)
                if v == 2:
                    dve.wait_ge(exps_ready, g + 1)
                    link(nc.vector.tensor_reduce(part[:], prob, AX.X, ALU.add))
                    link(nc.vector.reciprocal(first_p[:], part[:]))
                    link(nc.vector.tensor_tensor(prob, prob, over(first_p[:]), ALU.mult))
                    q4 = [SEQ, R * PROBS, 4, 4]
                    nc.vector.tensor_tensor(pairs[:], prob.unsqueeze(2).broadcast_to(q4), prob.unsqueeze(3).broadcast_to(q4),
                                            ALU.subtract).then_inc(pairs_ready, 1)
                if v == 3:
                    dve.wait_ge(pairs_ready, g + 1)
                    flat_pairs = pairs[:].rearrange("p q i j -> p q (i j)")
                    link(nc.vector.tensor_tensor(flat_pairs, flat_pairs,
                                                 tie[:].rearrange("p i j -> p (i j)").unsqueeze(1).broadcast_to([SEQ, R * PROBS, 16]),
                                                 ALU.is_ge))
                    link(nc.vector.tensor_reduce(rank[:].rearrange("p (q i) -> p q i", i=4), pairs[:], AX.X, ALU.add))
                    nc.vector.tensor_scalar(flat_picks[0], rank[:], 0.0, None, ALU.is_equal)
                    nc.vector.tensor_scalar(flat_picks[1], rank[:], 1.0, None, ALU.is_equal).then_inc(picks_ready, 1)
                    link(nc.vector.tensor_scalar(chosen[:].rearrange("p b l -> p (b l)"), rank[:], 2.0, None, ALU.is_lt))
                    ch_g = chosen[:, :, 0:GROUPS]
                    ch_e = chosen[:, :, GROUPS:].rearrange("p b (g e) -> p b g e", e=PER_GROUP)
                    link(nc.vector.tensor_tensor(sel[:].rearrange("p (g e) b -> p g e b", e=PER_GROUP),
                                                 ch_e.rearrange("p b g e -> p g e b"),
                                                 ch_g.rearrange("p b g -> p g b").unsqueeze(2).broadcast_to([SEQ, GROUPS, PER_GROUP, R]),
                                                 ALU.mult))
                    nc.vector.tensor_tensor_scan(sel_upto[:].rearrange("p e b -> p (e b)"), no_carry[:].rearrange("p e b -> p (e b)"),
                                                 sel[:].rearrange("p e b -> p (e b)"), 0.0, ALU.mult, ALU.add).then_inc(sel_ready, 1)
                if v == 4:
                    dve.wait_ge(picks_ready, g + 1)
                    flat = weigh[:, 0, :, :].rearrange("p b l -> p (b l)")
                    link(nc.vector.tensor_tensor(flat, less[:], flat_picks[1], ALU.mult))
                    link(nc.vector.tensor_reduce(second_p[:], flat.rearrange("p (q i) -> p q i", i=4), AX.X, ALU.add))
                    link(nc.vector.tensor_tensor(part[:], first_p[:], second_p[:], ALU.add))
                    link(nc.vector.tensor_scalar(part[:], part[:], TOP_P, None, ALU.is_le))
                    link(nc.vector.tensor_tensor(second_p[:], second_p[:], part[:], ALU.mult))
                    link(nc.vector.tensor_tensor(part[:], first_p[:], second_p[:], ALU.add))
                    link(nc.vector.tensor_scalar(part[:], part[:], 1e-9, None, ALU.add))
                    nc.vector.reciprocal(pmax[:], part[:]).then_inc(shares_ready, 1)
                if v == 5:
                    dve.wait_ge(shares_ready, g + 1)
                    nc.vector.tensor_tensor(ratio[:, 0, :], first_p[:], pmax[:], ALU.mult)
                    link(nc.vector.tensor_tensor(ratio[:, 1, :], second_p[:], pmax[:], ALU.mult))
                    of_groups = ratio[:].rearrange("p k (b q) -> p k b q", q=PROBS)[:, :, :, 0]
                    link(nc.vector.tensor_scalar(of_groups, of_groups, GROUPS ** -0.5, None, ALU.mult))
                    for k in range(2):
                        last = nc.vector.tensor_tensor(weigh[:, k, :, :].rearrange("p b (q i) -> p (b q) i", i=4),
                                                       picks[:, k, :, :].rearrange("p b (q i) -> p (b q) i", i=4),
                                                       over(ratio[:, k, :]), ALU.mult)
                    last.then_inc(weigh_ready, 1)
                if v == 6:
                    dve.wait_ge(weigh_ready, g + 1)
                    nc.vector.tensor_tensor(weigh[:, 0, :, :], weigh[:, 0, :, :], weigh[:, 1, :, :], ALU.add)
                    dve.wait_ge(counts_read, g + 1)
                    link(nc.vector.tensor_tensor(place2, picks[:, :, :, GROUPS:],
                                                 place.unsqueeze(1).broadcast_to([SEQ, 2, R, EXPERTS]), ALU.mult))
                    nc.vector.tensor_reduce(by_group.rearrange("p k b g -> p (k b g)"),
                                            place2.rearrange("p k b (g e) -> p (k b g) e", e=PER_GROUP), AX.X,
                                            ALU.add).then_inc(by_group_ready, 1)
                if v == 7:
                    dve.wait_ge(by_group_ready, g + 1)
                    for gp in range(2):
                        last = nc.vector.tensor_tensor(by_pick[:, gp, :, :, :], by_group,
                                                       picks[:, gp, :, 0:GROUPS].unsqueeze(1).broadcast_to([SEQ, 2, R, GROUPS]), ALU.mult)
                    link(last)
                    nc.vector.tensor_reduce(slots_f[:], by_pick.rearrange("p a k b g -> p (a k b) g"), AX.X,
                                            ALU.add).then_inc(slots_ready, 1)
                assert at[0] == steps_links, (v, at)

            def to_stage(g):
                stage, k = stages[stage_buffer(g)], stage_buffer(g)
                dve.wait_ge(slots_ready, g + 1)
                dve.wait_ge(tables, 1)
                stage_free(dve, g)
                nc.vector.tensor_tensor(stage[:, :, ROW_W:ROW_ID].rearrange("p b (g e) -> p b g e", e=PER_GROUP),
                                        weigh[:, 0, :, GROUPS:].rearrange("p b (g e) -> p b g e", e=PER_GROUP),
                                        weigh[:, 0, :, 0:GROUPS].unsqueeze(3).broadcast_to([SEQ, R, GROUPS, PER_GROUP]),
                                        ALU.mult)
                nc.vector.tensor_copy(stage[:, :, ROW_ID], tok_id[:])
                nc.vector.tensor_copy(slots[k][:], slots_f[:]).then_inc(stage_ready, 1)
                dve.wait_ge(stage_ready, g + 1)
                nc.vector.tensor_scalar(tok_id[:], tok_id[:], float(R * SEQ), None, ALU.add)
            steps(dve, step, route)

            count = [0]

            def link(ins):
                count[0] += 1
                ins.then_inc(table_link, 1)
                dve.wait_ge(table_link, count[0])
            dve.wait_ge(stage_ready, ROUTES)
            nc.vector.tensor_copy(ends_i[:], next_row[:]).then_inc(ends_ready, 1)
            link(nc.vector.tensor_tensor(n_tiles[:], next_row[:], region[:], ALU.subtract))
            link(nc.vector.tensor_scalar(n_tiles_i[:], n_tiles[:], float(TILE - 1), None, ALU.add))
            link(nc.vector.tensor_scalar(n_tiles_i[:], n_tiles_i[:], TILE.bit_length() - 1, None, ALU.logical_shift_right))
            link(nc.vector.tensor_copy(n_tiles[:], n_tiles_i[:]))
            link(nc.vector.tensor_tensor_scan(last_tile[:], ones_e[:], n_tiles[:], 0.0, ALU.mult, ALU.add))
            t_e = [P, TILES, EXPERTS]
            link(nc.vector.tensor_tensor(past[:], tile_no[:].unsqueeze(2).broadcast_to(t_e),
                                         last_tile[:].unsqueeze(1).broadcast_to(t_e), ALU.is_ge))
            nc.vector.tensor_tensor(past2[:], past[:], n_tiles[:].unsqueeze(1).broadcast_to(t_e), ALU.mult)
            link(nc.vector.tensor_reduce(tile_e[:], past[:], AX.X, ALU.add))
            link(nc.vector.tensor_reduce(tile_s[:], past2[:], AX.X, ALU.add))
            nc.vector.tensor_tensor(past[:], tile_e[:].unsqueeze(2).broadcast_to(t_e),
                                    expert_no[:].unsqueeze(1).broadcast_to(t_e), ALU.is_equal)
            nc.vector.tensor_scalar(tile_v[:], tile_e[:], float(EXPERTS), float(TILE), ALU.is_lt, ALU.mult)
            link(nc.vector.tensor_tensor(tile_s[:], tile_no[:], tile_s[:], ALU.subtract))
            link(nc.vector.tensor_tensor(tile_s[:], tile_s[:], tile_v[:], ALU.mult))
            link(nc.vector.scalar_tensor_tensor(out=tile_row_i[:], in0=tile_e[:], scalar=float(CAP), in1=tile_s[:],
                                                op0=ALU.mult, op1=ALU.add))
            nc.vector.tensor_scalar(tile_e_i[:], tile_e[:], float(EXPERTS - 1), None, ALU.min).then_inc(table_ready, 1)

            def x_rest(t, u):
                dve.wait_ge(x_hi_done, t + 1)
                nc.vector.tensor_tensor(x_lo[:, u % 2, :], x_ps[:], x_hi[:, u % 2, :].bitcast(F32), ALU.subtract).then_inc(x_read, 1)

            def hidden_lo(t, c):
                dve.wait_ge(hid_hi_done, t * HC + (c + 1))
                nc.vector.tensor_tensor(hid_lo[:, c, :], hid[:, c % 2, :], hid_hi[:, c, :].bitcast(F32),
                                        ALU.subtract).then_inc(hid_ready, 1)

            def weights(t, u):
                dve.wait_ge(rows_in[u], loads(t, u, ROWS))
                nc.vector.tensor_tensor(w_part[:], x_rows[:, u, :, ROW_W:ROW_ID],
                                        past[:, ds(t, 1), :].broadcast_to([P, SUB, EXPERTS]), ALU.mult).then_inc(w_link, 1)
                dve.wait_ge(w_link, t + 1)
                nc.vector.tensor_reduce(w_row[:, u, :], w_part[:], AX.X, ALU.add).then_inc(w_link2, 1)
                if since(t, ROWS):
                    dve.wait_ge(added, (t - (ROWS - 1)) * (16 * SUB))
                nc.vector.tensor_copy(out_ids[:, u, :], x_rows[:, u, :, ROW_ID]).then_inc(ids_ready, 1)

            def out_half(t, u, half):
                if half == 0:
                    dve.wait_ge(y_tok_done, t + 1)
                    dve.wait_ge(w_link2, t + 1)
                    if since(t, 2):
                        dve.wait_ge(added, (t - 1) * (16 * SUB))
                for s in range(half * SUB // 2, (half + 1) * SUB // 2):
                    last = nc.vector.tensor_scalar(y_rows[:, u % 2, s, :], y_tok_ps[:, s * P:(s + 1) * P],
                                                   w_row[:, u % ROWS, s:s + 1], None, ALU.mult)
                if half == 1:
                    last.then_inc(y_rows_ready, 1)

            def tile(t, u):
                for c in range(HC):
                    dve.wait_ge(silu_done, t * HC + (c + 1))
                    dve.wait_ge(up_done, t * HC + (c + 1))
                    if since(t, 1) or c >= 2:
                        dve.wait_ge(hid_ready, t * HC + (c - 1))
                    nc.vector.tensor_tensor(hid[:, c % 2, :], silu[:, c % 2, :], up_ps[c % 2], ALU.mult).then_inc(hid_done, 1)
                    if c == 0 and is_tile(t - 2):
                        out_half(t - 2, u - 2, 1)
                    if c == 1:
                        weights(t, u)
                    if c == 2 and is_tile(t + 1):
                        x_rest(t + 1, u + 1)
                    if c == 3 and is_tile(t - 1):
                        out_half(t - 1, u - 1, 0)
                    hidden_lo(t, c)
            x_rest(0, 0)
            tiles(dve, tile)
            out_half(TILES - 2, ROWS - 2, 1)
            out_half(TILES - 1, ROWS - 1, 0)
            out_half(TILES - 1, ROWS - 1, 1)


def lay_out(inputs):
    a = {k: np.asarray(v) for k, v in inputs.items()}
    perm = np.arange(D).reshape(HEADS, 2, DH // 2)[:, ::-1, :].reshape(-1)
    theta = (1.0 / 10000.0 ** (np.arange(0, DH, 2, dtype=np.float32) / np.float32(DH))).astype(np.float32)
    angle = np.arange(SEQ, dtype=np.float32)[None, :] * np.tile(theta, 2 * HEADS)[:, None]
    sign = np.tile(np.repeat(np.array([-1.0, 1.0], np.float32), DH // 2), HEADS)[:, None]
    scale = np.float32(DH ** -0.5)
    gate, up = (a[k].reshape(EXPERTS, P, HC, P) for k in ("L0_ffn_W1", "L0_ffn_W3"))
    down = a["L0_ffn_W2"].reshape(EXPERTS, HC, P, D).transpose(0, 2, 1, 3)
    arrays = {
        "x_t": a["x"].reshape(BATCH * TIME, D_IN).T,
        "conv_w": a["L0_tok_W"].T,
        "col_params": np.stack([a["L0_tok_b"], a["L0_tok_gamma"], a["L0_tok_beta"], a["L0_attn_bq"],
                                a["L0_attn_bq"][perm], a["L0_attn_bv"]], axis=1),
        "row_params": np.concatenate([a["L0_attn_bv"], a["L0_attn_bo"], a["L0_ffn_br"], a["L0_ffn_bgate"].reshape(-1)]),
        "rope_tab": np.stack([-np.cos(angle) * scale, -np.sin(angle) * sign * scale]).astype(np.float32),
        "attn_w": np.stack([a["L0_attn_Wq"], a["L0_attn_Wq"][:, perm], a["L0_attn_Wv"], a["L0_attn_Wo"]]),
        "route_w": np.concatenate([a["L0_ffn_Wr"], a["L0_ffn_Wgate"].transpose(1, 0, 2).reshape(D, EXPERTS)], axis=1),
        "expert_w": np.stack([gate, up, down], axis=3).reshape(EXPERTS, P, 3 * HID),
    }
    return {k: np.ascontiguousarray(v) for k, v in arrays.items()}


def kernel(**inputs):
    import concourse.bacc as bacc
    from concourse.bass_utils import run_bass_kernel_spmd

    arrays = lay_out(inputs)
    nc = bacc.Bacc("TRN2", target_bir_lowering=False, num_devices=1)
    args = {k: nc.dram_tensor(k, a.shape, mybir.dt.from_np(a.dtype), kind="ExternalInput").ap() for k, a in arrays.items()}
    out = nc.dram_tensor("out", (N_TOK + TILE, D), F32, kind="ExternalOutput").ap()
    audio_tower(nc, out=out, **args)
    result = run_bass_kernel_spmd(nc, [arrays], core_ids=[0])
    return result.results[0]["out"][:N_TOK].reshape(BATCH, SEQ, D)
```

```python
from contextlib import ExitStack

import concourse.bass as bass
import numpy as np
from concourse import mybir

ALU = mybir.AluOpType
ACT = mybir.ActivationFunctionType
AX = mybir.AxisListType
F32 = mybir.dt.float32
F32R = mybir.dt.float32r
BF16 = mybir.dt.bfloat16
I32 = mybir.dt.int32
U32 = mybir.dt.uint32

BATCH, TIME, D_IN = 64, 125, 64
CONTEXT = 5
SEQ = TIME - (CONTEXT - 1)
N_TOK = BATCH * SEQ
D = 128
HEADS, DH = 8, 16
EPS = 1e-5
GROUPS, PER_GROUP = 4, 4
EXPERTS = GROUPS * PER_GROUP
PICKED = 4
HID = 512
HC = HID // 128
TOP_P = 0.9
P = 128

CHUNK_B = 4
CHUNKS = BATCH // CHUNK_B
CHUNK = CHUNK_B * SEQ

ROW_W = D
ROW_ID = D + EXPERTS
ROW = D + EXPERTS + 4
TILE = 512
SUB = TILE // P
CAP = N_TOK + TILE
TILES = (N_TOK * PICKED) // TILE + EXPERTS
LOGITS = GROUPS + EXPERTS
ROWS = 4
assert TILES % ROWS == 0
FEWEST_TILES = -(-N_TOK * PICKED // TILE)
SURE_TILES = -(-FEWEST_TILES // 2) * 2 // ROWS * ROWS
TABLE = TILES + 3

R = 8
ROUTES = BATCH // R
SCALE_UP = 2.0 ** 100
LEAST_LEAD = 2.0 ** -80
PROBS = 1 + GROUPS

ROUTE_BASE = 2 * R - 1
LOOP_GROUPS = (1, 5)
STEP_FIRST, STEP_END = -4, BATCH + R
SCATTERS = PICKED * R

LAST, NEXT_TO_LAST, THIRD_LAST = ROUTES - 1, ROUTES - 2, ROUTES - 3
FIRST_PART = 0


TR3_FIRST, TR3_LAST = -3, BATCH + 4
SMALL_FIRST, SMALL_LAST = -4, BATCH + 5
LN_FIRST, LN_LAST = -3, BATCH + 4


def is_group(g, only):
    return isinstance(g, int) and g == only


def routed_group(g):
    return not isinstance(g, int) or 0 <= g < ROUTES


def parts_of(g, v):
    if is_group(g, LAST):
        when = {0: (1, 2, 3, 4, 5, 6, 7)}
    elif is_group(g, NEXT_TO_LAST):
        when = {0: (1,), 1: (2, 3, 4), 3: (5, 6, 7)}
    elif is_group(g, THIRD_LAST):
        when = {1: (1,), 2: (2, 3), 3: (4,), 4: (5, 6), 5: (7,)}
    else:
        when = {i: (i,) for i in range(1, R)}
    parts = [(g, part) for part in when.get(v, ())] if routed_group(g) else []
    return parts + ([(g + 1, FIRST_PART)] if v == R - 1 and routed_group(g + 1) else [])


def counted(g, v):
    at = 2 if is_group(g, NEXT_TO_LAST) else 3 if is_group(g, THIRD_LAST) else 4
    return routed_group(g) and not is_group(g, LAST) and v == at


def staged(g, v):
    for group, at in ((LAST, 0), (NEXT_TO_LAST, 3), (THIRD_LAST, 5)):
        if is_group(g, group) and v == at:
            return [g]
    late = is_group(g, LAST) or is_group(g, NEXT_TO_LAST)
    return [g - 1] if v == 0 and not late and not is_group(g, THIRD_LAST) and routed_group(g - 1) else []


def staged_in_front(g, v):
    return [g - 1] if v == 0 and is_group(g, THIRD_LAST) else []


def stage_buffer(g):
    return 1 if is_group(g, LAST) or is_group(g, THIRD_LAST) else 0


def scatters_of(g, v):
    def share(group, i, n):
        per = -(-SCATTERS // n)
        first, end = i * per, min((i + 1) * per, SCATTERS)
        return [(group, first, end)] if routed_group(group) and 0 <= first < end else []
    if is_group(g, LAST):
        return share(g, 0, 1)
    if is_group(g, NEXT_TO_LAST):
        return share(g - 1, v + 1, 5) if v < 4 else share(g, v - 4, 4)
    if is_group(g, THIRD_LAST):
        return share(g - 1, v, 7) if v < 7 else share(g, v - 7, 5)
    return share(g - 1, v - 1, R - 1)


def ds(at, n):
    return bass.ds(at, n)


def audio_tower(nc, x_t, conv_w, col_params, row_params, rope_tab, attn_w, route_w, expert_w, out):
    routed = nc.dram_tensor("routed", (EXPERTS * CAP + TILE, ROW), F32, kind="Internal").ap()
    with ExitStack() as ctx:
        def sb(name, shape, dt=F32):
            return ctx.enter_context(nc.sbuf_tensor(name, shape, dt))

        def sem(name):
            return ctx.enter_context(nc.semaphore(name))

        ident = sb("ident", [P, P])
        conv_sb = sb("conv_sb", [P, 3, D])
        colp = sb("colp", [P, 6])
        conv_b, gamma_c, beta_c, bq_c, bqr_c, bv_c = (colp[:, i:i + 1] for i in range(6))
        rowp = sb("rowp", [SEQ, 2 * D + LOGITS])
        bv_row, bo_row, route_b = rowp[:, 0:D], rowp[:, D:2 * D], rowp[:, 2 * D:2 * D + LOGITS]
        rope_sb = sb("rope_sb", [P, 2, SEQ])
        attn_sb = sb("attn_sb", [P, 4, D])
        wq_sb, wqr_sb, wv_sb, wo_sb = (attn_sb[:, i, :] for i in range(4))
        route_sb = sb("route_sb", [P, LOGITS])
        head_mask = sb("head_mask", [P, 4])
        bv_heads = sb("bv_heads", [P, 4])
        minus_half = sb("minus_half", [P, 2])
        marker = sb("marker", [P, 1])
        ones_e = sb("ones_e", [P, EXPERTS])
        eps_t = sb("eps_t", [P, 2])

        conv_in = sb("conv_in", [P, BATCH * TIME])
        y_all = conv_in[:, 0:N_TOK]
        resid = sb("resid", [SEQ, BATCH, D])
        xn_all = sb("xn_all", [P, BATCH * D])
        logits = sb("logits", [SEQ, R, LOGITS])
        stats_y = sb("stats_y", [P, CHUNKS, 6])
        bn = sb("bn", [P, 6])

        h_cm = sb("h_cm", [P, 2, SEQ])
        stat6 = sb("stat6", [SEQ, 2, 6])
        mv = sb("mv", [SEQ, 2, 2, 2])
        var_eps = sb("var_eps", [SEQ, 2, 2])
        rstd = sb("rstd", [SEQ, 2, 2])
        shift1 = sb("shift1", [SEQ, BATCH])
        shift2 = sb("shift2", [SEQ, 2])
        rstd1 = sb("rstd1", [SEQ, 2])
        xn = sb("xn", [SEQ, 2, D])
        xn2 = sb("xn2", [SEQ, 2, D])
        cm3 = sb("cm3", [P, 2, 3, SEQ])
        q_a = sb("q_a", [P, SEQ])
        q_b = sb("q_b", [P, SEQ])
        q_cm = sb("q_cm", [P, 2, SEQ])
        v_heads = sb("v_heads", [P, 2, 4, SEQ])
        v_tok = sb("v_tok", [SEQ, 4, HEADS, 32])
        row_low = sb("row_low", [SEQ, 2, HEADS])
        probs = sb("probs", [SEQ, 2, HEADS, SEQ])
        probs_t = sb("probs_t", [SEQ, 2, HEADS, SEQ])
        o_sb = sb("o_sb", [P, 2, 2, SEQ])
        rz = sb("rz", [SEQ, HEADS])
        att = sb("att", [SEQ, 2, HEADS, DH])

        less = sb("less", [SEQ, 160])
        pmax = sb("pmax", [SEQ, R * PROBS])
        first_p = sb("first_p", [SEQ, R * PROBS])
        second_p = sb("second_p", [SEQ, R * PROBS])
        part = sb("part", [SEQ, R * PROBS])
        ratio = sb("ratio", [SEQ, 2, R * PROBS])
        pairs = sb("pairs", [SEQ, R * PROBS, 4, 4])
        tie = sb("tie", [SEQ, 4, 4])
        rank = sb("rank", [SEQ, R * PROBS * 4])
        picks = sb("picks", [SEQ, 2, R, LOGITS])
        weigh = sb("weigh", [SEQ, 2, R, LOGITS])
        chosen = sb("chosen", [SEQ, R, LOGITS])
        sel = sb("sel", [SEQ, EXPERTS, R], BF16)
        from_here = sb("from_here", [SEQ, P], BF16)
        ones_b = sb("ones_b", [SEQ, P], BF16)
        no_carry = sb("no_carry", [SEQ, EXPERTS, R])
        sel_upto = sb("sel_upto", [SEQ, EXPERTS, R], BF16)
        next_row = sb("next_row", [P, EXPERTS])
        flat = pairs[:].rearrange("p q i j -> p (q i j)")
        place = flat[:, 0:128].rearrange("p (b e) -> p b e", e=EXPERTS)
        place2 = flat[:, 128:384].rearrange("p (k b e) -> p k b e", k=2, e=EXPERTS)
        by_group = flat[:, 384:448].rearrange("p (k b g) -> p k b g", k=2, g=GROUPS)
        by_pick = flat[:, 448:576].rearrange("p (a k b g) -> p a k b g", a=2, k=2, g=GROUPS)
        slots_f = sb("slots_f", [SEQ, PICKED * R])
        slots = [sb(f"slots{i}", [SEQ, PICKED * R], U32) for i in range(2)]
        stages = [sb(f"stage{i}", [SEQ, R, ROW]) for i in range(2)]
        tok_id = sb("tok_id", [SEQ, R])
        pad_rows = sb("pad_rows", [P, SUB, ROW])
        tile_no = sb("tile_no", [P, TABLE])
        expert_no = sb("expert_no", [P, EXPERTS])
        region = sb("region", [P, EXPERTS])
        n_tiles = sb("n_tiles", [P, EXPERTS])
        n_tiles_i = sb("n_tiles_i", [P, EXPERTS], I32)
        last_tile = sb("last_tile", [P, EXPERTS])
        more_tiles_i = sb("more_tiles_i", [P, 4], I32)
        tile_row_i = sb("tile_row_i", [P, TABLE], I32)
        tile_e_i = sb("tile_e_i", [P, TABLE], I32)
        ends_i = sb("ends_i", [P, EXPERTS], I32)
        W_COLS = 3 * HID
        w_hi, w_lo = (sb(n, [P, 2, W_COLS], F32R) for n in ("w_hi", "w_lo"))
        x_hi, x_lo = (sb(n, [P, 2, TILE], F32R) for n in ("x_hi", "x_lo"))
        hid_hi, hid_lo = (sb(n, [P, HC, TILE], F32R) for n in ("hid_hi", "hid_lo"))
        taken = {}

        def in_place_of(name, old, copies, n=TILE):
            at = taken.get(name, 0)
            taken[name] = at + copies * n
            return old[:, at:at + copies * n].rearrange("p (k n) -> p k n", k=copies)
        w_raw = in_place_of("input", conv_in, 2, W_COLS)
        y_cm = in_place_of("input", conv_in, 1)[:, 0, :]
        y_rows = in_place_of("input", conv_in, 2).rearrange("p k (s d) -> p k s d", s=SUB)
        silu, hid = (in_place_of("input", conv_in, 2) for _ in range(2))
        x_rows = in_place_of("norm", xn_all, ROWS, SUB * ROW).rearrange("p k (s c) -> p k s c", s=SUB)
        tile_e, tile_s, tile_v = (in_place_of("norm", xn_all, 1, TABLE)[:, 0, :] for _ in range(3))
        past, past2 = (in_place_of("norm", xn_all, TABLE, EXPERTS) for _ in range(2))
        w_part = in_place_of("norm", xn_all, SUB, EXPERTS)
        w_row = sb("w_row", [P, ROWS, SUB])
        out_ids = sb("out_ids", [P, ROWS, SUB], U32)

        def bank(name, shape=(P, 512)):
            return ctx.enter_context(nc.psum_tensor(name, list(shape), F32))

        scores_ps = bank("scores_ps", (P, 2, 512))
        pt_ps = bank("pt_ps", (P, 2, 512))
        proj_ps = bank("proj_ps")
        dve_ps = bank("dve_ps")
        act_ps = bank("act_ps")
        o_ps = bank("o_ps")
        conv_ps = [proj_ps, dve_ps]
        counts_at = 2 * D + LOGITS
        count_ps = dve_ps[0:SEQ, counts_at:counts_at + EXPERTS * R].rearrange("p (e b) -> p e b", b=R)
        total_ps = dve_ps[:, counts_at + EXPERTS * R:counts_at + EXPERTS * (R + 1)]
        gate_ps, up_ps = [scores_ps[:, i, :] for i in range(2)], [pt_ps[:, i, :] for i in range(2)]
        x_ps, y_ps, y_tok_ps = act_ps, [o_ps, proj_ps], dve_ps
        qT_ps, qrT_ps = (proj_ps[:, i * SEQ:(i + 1) * SEQ] for i in range(2))
        vT_ps = act_ps[:, 3 * SEQ:4 * SEQ]
        v_ps = proj_ps[0:SEQ, 2 * SEQ:2 * SEQ + D]
        h_tok_ps, wo_ps, logit_ps = dve_ps[0:SEQ, 0:D], dve_ps[0:SEQ, D:2 * D], dve_ps[0:SEQ, 2 * D:2 * D + LOGITS]
        o_cm_ps = o_ps[:, 0:2 * SEQ].rearrange("p (s i) -> p s i", s=2)
        o_tok_ps = o_ps[0:SEQ, 0:2 * D].rearrange("p (h e) -> p h e", e=32)

        conv_w_in, w_in = sem("conv_w_in"), sem("w_in")
        x_in = [sem(f"x_in{i}") for i in range(4)]
        consts = sem("consts")
        conv_done, conv_read, stats_done = sem("conv_done"), sem("conv_read"), sem("stats_done")
        bn_link, bn_var, bn_rstd, bn_ready = sem("bn_link"), sem("bn_var"), sem("bn_rstd"), sem("bn_ready")
        h_ready, heads_ready = sem("h_ready"), sem("heads_ready")
        scores_done, exp_done = sem("scores_done"), sem("exp_done")
        otr_done, att_ready = sem("otr_done"), sem("att_ready")
        tr3_done, tr3_read = sem("tr3_done"), sem("tr3_read")
        pt_done, pt_read = sem("pt_done"), sem("pt_read")
        proj_done, proj_read = sem("proj_done"), sem("proj_read")
        pv_done, o_read = sem("pv_done"), sem("o_read")
        small_done, small_read = sem("small_done"), sem("small_read")
        mv_ready, ln_link, rstd_ready = sem("mv_ready"), sem("ln_link"), sem("rstd_ready")
        xn_ready, xn2_ready, row_ready = sem("xn_ready"), sem("xn2_ready"), sem("row_ready")
        stats1_done, h1_done, stats2_done, logits_done = sem("stats1_done"), sem("h1_done"), sem("stats2_done"), sem("logits_done")
        rz_done, shift1_done, shift2_done = sem("rz_done"), sem("shift1_done"), sem("shift2_done")
        eps_set = sem("eps_set")
        tables, pool_link = sem("tables"), sem("pool_link")
        less_ready, exps_ready, sel_ready, counts_done, counts_read, place_ready = (
            sem(n) for n in ("less_ready", "exps_ready", "sel_ready", "counts_done", "counts_read", "place_ready"))
        pairs_ready, rank_ready, picks_ready, shares_ready, weigh_ready, by_group_ready, slots_ready = (
            sem(n) for n in ("pairs_ready", "rank_ready", "picks_ready", "shares_ready", "weigh_ready", "by_group_ready", "slots_ready"))
        LINKS = (1, 3, 1, 2, 5, 2, 1, 1)
        links_of = [sem(f"route_link{part}") for part in range(len(LINKS))]
        stage_x, stage_ready = sem("stage_x"), sem("stage_ready")
        scattered = [sem(f"scattered{i}") for i in range(2)]
        ends_ready, pads_in, table_ready, resid_out = sem("ends_ready"), sem("pads_in"), sem("table_ready"), sem("resid_out")
        table_link = sem("table_link")
        rows_in = [sem(f"rows_in{i}") for i in range(ROWS)]
        weights_in = [sem(f"weights_in{i}") for i in range(2)]
        x_done, x_read, gate_done, up_done, silu_done, hid_ready = (
            sem(n) for n in ("x_done", "x_read", "gate_done", "up_done", "silu_done", "hid_ready"))
        x_hi_done, w_hi_done, w_lo_done, hid_done, hid_hi_done = (
            sem(n) for n in ("x_hi_done", "w_hi_done", "w_lo_done", "hid_done", "hid_hi_done"))
        y_read, y_tok_done, w_link, w_row_done, ids_ready, y_rows_ready, added, down_done = (
            sem(n) for n in ("y_read", "y_tok_done", "w_link", "w_row_done", "ids_ready", "y_rows_ready", "added",
                             "down_done"))
        low_done, rope_link = sem("low_done"), sem("rope_link")
        marked = sem("marked")

        def ok(b):
            return not isinstance(b, int) or 0 <= b < BATCH

        def need(eng, s, b):
            if isinstance(b, int):
                if b < 0:
                    return
                b = min(b, BATCH - 1)
            eng.wait_ge(s, b + 1)

        def need_step(eng, s, n, first, last):
            if isinstance(n, int):
                if n < first:
                    return
                n = min(n, last)
            eng.wait_ge(s, n - first + 1)

        def steps(eng, step, route=None, stage=None):
            def run(n, u, g, v):
                if stage is not None:
                    for group in staged_in_front(g, v):
                        stage(group)
                if not isinstance(n, int) or n < BATCH + R:
                    step(n, u, g, v)
                if route is not None:
                    route(g, v)
            for n in range(STEP_FIRST, ROUTE_BASE + R * LOOP_GROUPS[0]):
                run(n, n, (n - ROUTE_BASE) // R, (n - ROUTE_BASE) % R)
            with eng.Fori(*LOOP_GROUPS) as g:
                for v in range(R):
                    run(g * R + (ROUTE_BASE + v), ROUTE_BASE + v, g, v)
            for n in range(ROUTE_BASE + R * LOOP_GROUPS[1], STEP_END):
                run(n, n, (n - ROUTE_BASE) // R, (n - ROUTE_BASE) % R)

        def stage_free(eng, g):
            if is_group(g, LAST):
                eng.wait_ge(scattered[1], 16 * SCATTERS)
            elif not is_group(g, THIRD_LAST):
                before = THIRD_LAST if is_group(g, NEXT_TO_LAST) else g
                eng.wait_ge(scattered[0], before * (16 * SCATTERS) + 16)

        def tiles(eng, tile, finish):
            for t in range(ROWS):
                tile(t, t)
            with eng.Fori(1, SURE_TILES // ROWS) as i:
                for u in range(ROWS):
                    tile(i * ROWS + u, u)
            eng.wait_ge(table_ready, 1)
            rounds_end = eng.value_load(more_tiles_i[0:1, 0:1], min_val=0, max_val=TILES - SURE_TILES) + SURE_TILES
            rest = eng.value_load(more_tiles_i[0:1, 1:2], min_val=0, max_val=2)
            with eng.Fori(SURE_TILES // ROWS, TILES // ROWS) as i:
                with eng.If(i * ROWS < rounds_end):
                    for u in range(ROWS):
                        tile(i * ROWS + u, u)
            with eng.If(rest < 1):
                finish(rounds_end, ROWS)
            with eng.If(0 < rest):
                for u in range(2):
                    tile(rounds_end + u, u)
                finish(rounds_end + 2, 2)
            return rounds_end + rest

        def since(t, first):
            return not isinstance(t, int) or t >= first

        def is_tile(t):
            return not isinstance(t, int) or t >= 0

        def loads(t, u, ring):
            return (t - u % ring) * (16 // ring) + 16

        block = ctx.enter_context(nc.Block())

        @block.sync
        def _(sp):
            sp.dma_start(conv_sb[:, 0:2, :], conv_w[0:2 * P, :].rearrange("(c p) o -> p c o", p=P)).then_inc(conv_w_in, 16)
            sp.dma_start(conv_sb[0:64, 2, :], conv_w[2 * P:2 * P + 64, :]).then_inc(conv_w_in, 16)
            sp.dma_start(colp[:], col_params).then_inc(conv_w_in, 16)
            n = BATCH * TIME // 4
            for i in range(4):
                sp.dma_start(conv_in[0:64, i * n:(i + 1) * n], x_t[:, i * n:(i + 1) * n]).then_inc(x_in[i], 16)
                hi = min((i + 1) * n, BATCH * TIME - 1)
                sp.dma_start(conv_in[64:128, i * n:hi], x_t[:, i * n + 1:hi + 1]).then_inc(x_in[i], 16)
            sp.dma_start(attn_sb[:], attn_w.rearrange("w p o -> p w o")).then_inc(w_in, 16)
            sp.dma_start(rope_sb[:], rope_tab.rearrange("w p s -> p w s")).then_inc(w_in, 16)
            sp.dma_start(route_sb[:], route_w).then_inc(w_in, 16)
            sp.dma_start(rowp[:], row_params.rearrange("(a n) -> a n", a=1).broadcast_to([SEQ, 2 * D + LOGITS])).then_inc(w_in, 16)
            sp.wait_ge(tables, 1)
            out_b = out[0:N_TOK, :].rearrange("(b s) d -> s b d", s=SEQ)

            def store_residual(g):
                sp.wait_ge(h1_done, g * R + R)
                sp.dma_start(out_b[:, ds(g * R, R), :], resid[:, ds(g * R, R), :]).then_inc(resid_out, 16)
            with sp.Fori(0, ROUTES) as g:
                store_residual(g)
            sp.dma_start(out[N_TOK:N_TOK + TILE, :].rearrange("(p s) d -> p s d", s=SUB),
                         pad_rows[:, :, 0:D]).then_inc(resid_out, 16)
            sp.wait_ge(ends_ready, 1)
            for e in range(EXPERTS):
                end = sp.value_load(ends_i[0:1, e:e + 1], min_val=e * CAP, max_val=e * CAP + N_TOK)
                sp.dma_start(routed[ds(end, TILE), :].rearrange("(p s) c -> p s c", s=SUB),
                             pad_rows[:]).then_inc(pads_in, 16)
            sp.wait_ge(table_ready, 1)

            def load_tile(t, u):
                e = sp.value_load(tile_e_i[0:1, ds(t, 1)], min_val=0, max_val=EXPERTS - 1)
                row = sp.value_load(tile_row_i[0:1, ds(t, 1)], min_val=0, max_val=EXPERTS * CAP)
                if since(t, 2):
                    sp.wait_ge(w_lo_done, t * HC - HC)
                sp.dma_start(w_raw[:, u % 2, :], expert_w[ds(e, 1), :, :].rearrange("e p n -> p (e n)")).then_inc(weights_in[u % 2], 16)
                if since(t, ROWS):
                    sp.wait_ge(x_done, t - (ROWS - 1))
                    sp.wait_ge(ids_ready, t - (ROWS - 1))
                if isinstance(t, int) and t == 0:
                    sp.wait_ge(pads_in, 16 * EXPERTS)
                    sp.wait_ge(scattered[0], 16 * SCATTERS * (ROUTES - 2) + 16)
                    sp.wait_ge(scattered[1], 16 * SCATTERS * 2)
                sp.dma_start(x_rows[:, u, :, :], routed[ds(row, TILE), :].rearrange("(p s) c -> p s c", s=SUB)).then_inc(rows_in[u], 16)
            tiles(sp, load_tile, lambda t, u: load_tile(t, u % ROWS))

        @block.gpsimd
        def _(pool):
            pool.memset(ident[:], 0.0).then_inc(consts, 1)
            pool.memset(v_tok[:], 0.0).then_inc(consts, 1)
            pool.memset(minus_half[:], -0.5).then_inc(consts, 1)
            pool.memset(head_mask[:], 1.0).then_inc(consts, 1)
            pool.memset(eps_t[:], EPS).then_inc(eps_set, 1)
            pool.wait_ge(consts, 4)
            pool.wait_ge(eps_set, 1)
            pool.affine_select(out=ident[:], in_=ident[:], compare_op=ALU.not_equal, fill=1.0, base=0,
                               pattern=[[-1, P]], channel_multiplier=1).then_inc(consts, 1)
            pool.wait_ge(consts, 5)
            pool.memset(v_tok[:, :, :, DH:DH + 1], 1.0).then_inc(consts, 1)
            pool.wait_ge(consts, 6)
            for half in range(2):
                m = head_mask[64 * half:64 * half + 64, :]
                pool.affine_select(out=m, in_=m, compare_op=ALU.is_ge, fill=0.0, base=0,
                                   pattern=[[-DH, 4]], channel_multiplier=1).then_inc(consts, 1)
                pool.wait_ge(consts, 7 + 2 * half)
                pool.affine_select(out=m, in_=m, compare_op=ALU.is_ge, fill=0.0, base=DH - 1,
                                   pattern=[[DH, 4]], channel_multiplier=-1).then_inc(consts, 1)
                pool.wait_ge(consts, 8 + 2 * half)

            pool.memset(ones_e[:], 1.0).then_inc(pool_link, 1)
            pool.memset(pad_rows[:], 0.0).then_inc(pool_link, 1)
            pool.memset(tie[:], 0.0).then_inc(pool_link, 1)
            pool.memset(from_here[:], -1.0).then_inc(pool_link, 1)
            pool.memset(ones_b[:], 1.0).then_inc(pool_link, 1)
            pool.memset(no_carry[:], 1.0).then_inc(pool_link, 1)
            pool.memset(stages[0][:, :, ROW_ID + 1:ROW], 0.0).then_inc(pool_link, 1)
            pool.memset(stages[1][:, :, ROW_ID + 1:ROW], 0.0).then_inc(pool_link, 1)
            pool.iota(tok_id[:], pattern=[[SEQ, R]], base=0, channel_multiplier=1,
                      allow_small_or_imprecise_dtypes=True).then_inc(pool_link, 1)
            pool.iota(tile_no[:], pattern=[[1, TABLE]], base=0, channel_multiplier=0,
                      allow_small_or_imprecise_dtypes=True).then_inc(pool_link, 1)
            pool.iota(expert_no[:], pattern=[[1, EXPERTS]], base=0, channel_multiplier=0,
                      allow_small_or_imprecise_dtypes=True).then_inc(pool_link, 1)
            pool.iota(region[:], pattern=[[CAP, EXPERTS]], base=0, channel_multiplier=0,
                      allow_small_or_imprecise_dtypes=True).then_inc(pool_link, 1)
            pool.iota(next_row[:], pattern=[[CAP, EXPERTS]], base=0, channel_multiplier=0,
                      allow_small_or_imprecise_dtypes=True).then_inc(pool_link, 1)
            pool.wait_ge(pool_link, 13)
            pool.iota(pad_rows[:, :, ROW_ID], pattern=[[1, SUB]], base=N_TOK, channel_multiplier=SUB,
                      allow_small_or_imprecise_dtypes=True).then_inc(pool_link, 1)
            pool.wait_ge(pool_link, 14)
            pool.affine_select(out=tie[:], in_=tie[:], compare_op=ALU.is_ge, fill=LEAST_LEAD, base=0,
                               pattern=[[1, 4], [-1, 4]], channel_multiplier=0).then_inc(pool_link, 1)
            pool.wait_ge(pool_link, 15)
            pool.affine_select(out=tie[:], in_=tie[:], compare_op=ALU.not_equal, fill=1.0, base=0,
                               pattern=[[1, 4], [-1, 4]], channel_multiplier=0).then_inc(pool_link, 1)
            pool.wait_ge(pool_link, 16)
            pool.affine_select(out=from_here[:], in_=from_here[:], compare_op=ALU.is_ge, fill=0.0, base=0,
                               pattern=[[-1, P]], channel_multiplier=1).then_inc(pool_link, 1)
            pool.wait_ge(pool_link, 17)
            pool.memset(no_carry[:, :, 0:1], 0.0).then_inc(tables, 1)
            pool.wait_ge(tables, 1)
            pool.memset(marker[:], 0.0).then_inc(marked, 1)
            pool.dma_start(routed[EXPERTS * CAP:EXPERTS * CAP + TILE, :].rearrange("(p s) c -> p s c", s=SUB),
                           pad_rows[:]).then_inc(scattered[0], 16)
            pool.wait_ge(bn_var, 1)
            pool.tensor_scalar(bn[:, 2:3], bn[:, 1:2], EPS, None, ALU.add).then_inc(bn_rstd, 1)
            pool.wait_ge(bn_rstd, 1)
            pool.tensor_tensor(bn[:, 3:4], bn[:, 2:3], minus_half[:, 0:1], ALU.pow).then_inc(bn_rstd, 1)

            def step(n, u, g, v):
                ks = [k for k, b in ((0, n + 3), (1, n - 5)) if ok(b)]
                if ks:
                    a, z = ks[0], ks[-1] + 1
                    need_step(pool, mv_ready, n, LN_FIRST, LN_LAST)
                    pool.tensor_tensor(var_eps[:, u % 2, a:z], mv[:, u % 2, a:z, 1], eps_t[0:SEQ, a:z], ALU.add).then_inc(ln_link, 1)
                    need_step(pool, ln_link, n, LN_FIRST, LN_LAST)
                    pool.tensor_tensor(rstd[:, u % 2, a:z], var_eps[:, u % 2, a:z], minus_half[0:SEQ, a:z],
                                       ALU.pow).then_inc(rstd_ready, 1)

            def mark(before):
                pool.wait_ge(marked, before + 1)
                pool.tensor_tensor(marker[:], eps_t[:, 0:1], eps_t[:, 0:1], ALU.add).then_inc(marked, 1)

            def scatter(g, first, end):
                if first == 0:
                    pool.wait_ge(stage_x, g + 1)
                    pool.wait_ge(stage_ready, g + 1)
                    mark(g)
                k = stage_buffer(g)
                for i in range(first, end):
                    pool.indirect_dma_start(
                        out=routed, out_offset=bass.IndirectOffsetOnAxis(ap=slots[k][:, i:i + 1], axis=0),
                        in_=stages[k][:, i % R, :], in_offset=None).then_inc(scattered[k], 16)

            def route(g, v):
                for some in scatters_of(g, v):
                    scatter(*some)
            steps(pool, step, route)

            pool.wait_ge(resid_out, 16 * (ROUTES + 1))

            def add_rows(t, u):
                pool.wait_ge(y_rows_ready, t + 1)
                if since(t, 1):
                    pool.wait_ge(added, t * (16 * SUB))
                mark(ROUTES + t)
                for s in range(SUB):
                    pool.indirect_dma_start(
                        out=out, out_offset=bass.IndirectOffsetOnAxis(ap=out_ids[:, u % ROWS, s:s + 1], axis=0),
                        in_=y_rows[:, u % 2, s, :], in_offset=None, compute_op=ALU.add).then_inc(added, 16)

            def weights_lo(t, u):
                for q in range(HC):
                    pool.wait_ge(w_hi_done, t * HC + (q + 1))
                    r = slice(q * W_COLS // HC, (q + 1) * W_COLS // HC)
                    pool.tensor_tensor(w_lo[:, u % 2, r], w_raw[:, u % 2, r], w_hi[:, u % 2, r].bitcast(F32),
                                       ALU.subtract).then_inc(w_lo_done, 1)

            def tile(t, u):
                if is_tile(t + 1):
                    weights_lo(t + 1, u + 1)
                if is_tile(t - 2):
                    add_rows(t - 2, u - 2)
            weights_lo(0, 0)

            def finish(t, u):
                add_rows(t - 2, u - 2)
                add_rows(t - 1, u - 1)
            end = tiles(pool, tile, finish)
            pool.wait_ge(added, end * (16 * SUB))

        @block.tensor
        def _(pe):
            pe.wait_ge(conv_w_in, 16 * 3)
            for c in range(CHUNKS):
                if c % 4 == 0:
                    pe.wait_ge(x_in[c // 4], 32)
                if c >= 2:
                    pe.wait_ge(conv_read, c - 1)
                for i, rows in ((0, P), (2, P), (4, 64)):
                    src = conv_in[0:rows, c * CHUNK_B * TIME:(c + 1) * CHUNK_B * TIME].rearrange("p (b t) -> p b t", t=TIME)
                    mm = pe.matmul(conv_ps[c % 2][:, 0:CHUNK], conv_sb[0:rows, i // 2, :], src[:, :, i:i + SEQ],
                                   start=(i == 0), stop=(i == 4))
                mm.then_inc(conv_done, 1)
            pe.wait_ge(conv_read, CHUNKS)
            pe.wait_ge(consts, 10)
            pe.wait_ge(w_in, 16 * 4)

            def counts(g):
                pe.wait_ge(sel_ready, g + 1)
                pe.matmul(count_ps, ones_b[:, 0:SEQ], sel_upto[:], start=True, stop=False)
                pe.matmul(count_ps, from_here[:, 0:SEQ], sel[:], start=False, stop=True)
                pe.matmul(total_ps, ones_b[:], sel_upto[:, :, R - 1], start=True, stop=True).then_inc(counts_done, 1)

            def step(n, u, g, v):
                if ok(n):
                    need(pe, proj_read, n)
                    need(pe, heads_ready, n)
                    need(pe, exp_done, n - 1)
                    for half in range(2):
                        r = slice(64 * half, 64 * half + 64)
                        mm = pe.matmul(scores_ps[0:SEQ, half, 0:4 * SEQ], q_cm[r, u % 2, :],
                                       v_heads[r, u % 2, :, :], start=True, stop=True)
                    mm.then_inc(scores_done, 1)
                if ok(n + 2):
                    need_step(pe, tr3_read, n - 1, TR3_FIRST, TR3_LAST)
                    need(pe, proj_read, n + 1)
                    x = cm3[:, (u - 1) % 2, 0, :]
                    pe.matmul(qT_ps, wq_sb, x, start=True, stop=True)
                    pe.matmul(qrT_ps, wqr_sb, x, start=True, stop=True)
                    pe.matmul(v_ps, x, wv_sb, start=True, stop=True).then_inc(proj_done, 1)
                if ok(n - 2):
                    need(pe, pt_read, n - 2)
                    need(pe, att_ready, n - 3)
                    for h in range(HEADS):
                        q, s = h % 4, h // 4
                        mm = pe.matmul(o_cm_ps[32 * q:32 * q + 32, s, :], v_tok[:, (u - 2) % 4, h, :],
                                       probs_t[:, u % 2, h, :], start=True, stop=True)
                    mm.then_inc(pv_done, 1)
                if ok(n - 1):
                    need(pe, exp_done, n - 1)
                    need(pe, pt_read, n - 2)
                    for h in range(HEADS):
                        mm = pe.transpose(pt_ps[0:SEQ, h // 4, (h % 4) * SEQ:(h % 4 + 1) * SEQ],
                                          probs[:, (u - 1) % 2, h, :], ident[0:SEQ, 0:SEQ])
                    mm.then_inc(pt_done, 1)
                if ok(n - 2):
                    need(pe, o_read, n - 2)
                    for s in range(2):
                        mm = pe.transpose(o_ps[0:SEQ, s * D:(s + 1) * D], o_sb[:, u % 2, s, :], ident[:])
                    mm.then_inc(otr_done, 1)
                moved = [(0, n + 3, xn_ready, xn[:, (u + 3) % 2, :]),
                         (1, n - 3, att_ready, att[:, (u - 3) % 2, :, :].rearrange("p h e -> p (h e)")),
                         (2, n - 5, xn2_ready, xn2[:, (u - 5) % 2, :])]
                moved = [m for m in moved if ok(m[1])]
                if moved:
                    need_step(pe, tr3_read, n - 1, TR3_FIRST, TR3_LAST)
                    need(pe, heads_ready, n + 1)
                    if ok(n + 2):
                        pe.matmul(vT_ps, wv_sb, cm3[:, (u - 1) % 2, 0, :], start=True, stop=True)
                    for k, b, ready, src in moved:
                        need(pe, ready, b)
                        mm = pe.transpose(act_ps[:, k * SEQ:(k + 1) * SEQ], src, ident[0:SEQ, 0:SEQ])
                    mm.then_inc(tr3_done, 1)
                todo = [ok(n + 4), ok(n - 4), ok(n - 6)]
                if any(todo):
                    need_step(pe, tr3_read, n - 1, TR3_FIRST, TR3_LAST)
                    need(pe, small_read, n + 3)
                    need(pe, h1_done, n - 5)
                    need(pe, logits_done, n - 7)
                    if counted(g, v - 1):
                        pe.wait_ge(counts_read, g + 1)
                    if counted(g, v):
                        counts(g)
                    if todo[0]:
                        need(pe, h_ready, n + 4)
                        mm = pe.transpose(h_tok_ps, h_cm[:, u % 2, :], ident[:])
                    if todo[1]:
                        mm = pe.matmul(wo_ps, cm3[:, (u - 1) % 2, 1, :], wo_sb, start=True, stop=True)
                    if todo[2]:
                        mm = pe.matmul(logit_ps, cm3[:, (u - 1) % 2, 2, :], route_sb[:], start=True, stop=True)
                    mm.then_inc(small_done, 1)

            def route(g, v):
                if is_group(g, LAST):
                    need(pe, logits_done, BATCH - 1)
                    counts(g)
            steps(pe, step, route)

            def product(ps, w, x, start, stop):
                (w_h, w_l), (x_h, x_l) = w, x
                pe.matmul(ps, w_h, x_h, start=start, stop=False)
                pe.matmul(ps, w_h, x_l, start=False, stop=False)
                return pe.matmul(ps, w_l, x_h, start=False, stop=stop)

            def w_part_of(k, i, c):
                r = slice((c * 3 + i) * P, (c * 3 + i + 1) * P)
                return w_hi[:, k, r], w_lo[:, k, r]

            def x_transpose(t, u):
                pe.wait_ge(rows_in[u % ROWS], loads(t, u, ROWS))
                if since(t, 1):
                    pe.wait_ge(x_read, t)
                for s in range(SUB):
                    mm = pe.transpose(x_ps[:, s * P:(s + 1) * P], x_rows[:, u % ROWS, s, 0:D], ident[:])
                mm.then_inc(x_done, 1)

            def down(t, u, c):
                pe.wait_ge(hid_ready, t * HC + (c + 1))
                if c == 0 and since(t, 2):
                    pe.wait_ge(y_read, t - 1)
                product(y_ps[u % 2][:], w_part_of(u % 2, 2, c), (hid_hi[:, c, :], hid_lo[:, c, :]), c == 0,
                        c == HC - 1).then_inc(down_done, 1)

            def y_transpose(t):
                pe.wait_ge(y_read, t + 1)
                if since(t, 1):
                    pe.wait_ge(y_rows_ready, t)
                for s in range(SUB):
                    mm = pe.transpose(y_tok_ps[:, s * P:(s + 1) * P], y_cm[:, s * P:(s + 1) * P], ident[:])
                mm.then_inc(y_tok_done, 1)

            def tile(t, u):
                x = (x_hi[:, u % 2, :], x_lo[:, u % 2, :])
                for c in range(HC):
                    if c == 0:
                        pe.wait_ge(x_read, t + 1)
                    pe.wait_ge(w_lo_done, t * HC + (c + 1))
                    if since(t, 1) or c >= 2:
                        pe.wait_ge(silu_done, t * HC + (c - 1))
                        pe.wait_ge(hid_done, t * HC + (c - 1))
                    product(gate_ps[c % 2], w_part_of(u % 2, 0, c), x, True, True).then_inc(gate_done, 1)
                    product(up_ps[c % 2], w_part_of(u % 2, 1, c), x, True, True).then_inc(up_done, 1)
                    if c < 2 and is_tile(t - 1):
                        down(t - 1, u - 1, HC - 2 + c)
                    if c >= 2:
                        down(t, u, c - 2)
                    if c == 2 and is_tile(t - 1):
                        y_transpose(t - 1)
                    if c == 0 and is_tile(t + 1):
                        x_transpose(t + 1, u + 1)
            x_transpose(0, 0)

            def finish(t, u):
                down(t - 1, u - 1, HC - 2)
                down(t - 1, u - 1, HC - 1)
                y_transpose(t - 1)
            tiles(pe, tile, finish)

        @block.scalar
        def _(act):
            act.wait_ge(conv_w_in, 16 * 3)
            for c in range(CHUNKS):
                act.wait_ge(conv_done, c + 1)
                nc.scalar.activation(y_all[:, c * CHUNK:(c + 1) * CHUNK], conv_ps[c % 2][:, 0:CHUNK], ACT.Relu,
                                     bias=conv_b).then_inc(conv_read, 1)
            act.wait_ge(bn_ready, 1)

            def step(n, u, g, v):
                if ok(n + 4):
                    need_step(act, small_done, n - 2, SMALL_FIRST, SMALL_LAST)
                    nc.scalar.activation(h_cm[:, u % 2, :], y_all[:, ds((n + 4) * SEQ, SEQ)], ACT.Identity,
                                         bias=bn[:, 5:6], scale=bn[:, 4:5]).then_inc(h_ready, 1)
                if ok(n - 2):
                    need(act, pv_done, n - 2)
                    need(act, otr_done, n - 4)
                    nc.scalar.activation(o_sb[:, u % 2, :, :], o_cm_ps, ACT.Copy).then_inc(o_read, 1)
                if ok(n):
                    need(act, low_done, n)
                    need(act, pt_done, n - 2)
                    for h in range(HEADS):
                        ex = nc.scalar.activation(probs[:, u % 2, h, :], scores_ps[0:SEQ, h // 4, (h % 4) * SEQ:(h % 4 + 1) * SEQ],
                                                  ACT.Exp, bias=row_low[:, u % 2, h:h + 1], scale=-1.0)
                    ex.then_inc(exp_done, 1)
                if ok(n - 1):
                    need(act, pt_done, n - 1)
                    need(act, pv_done, n - 3)
                    for half in range(2):
                        cp = nc.scalar.activation(probs_t[:, (u - 1) % 2, 4 * half:4 * half + 4, :],
                                                  pt_ps[0:SEQ, half, 0:4 * SEQ].rearrange("p (h s) -> p h s", s=SEQ),
                                                  ACT.Copy)
                    cp.then_inc(pt_read, 1)
                ks = [k for k, b in ((0, n + 3), (1, n - 3), (2, n - 5)) if ok(b)]
                if ks:
                    need_step(act, tr3_done, n, TR3_FIRST, TR3_LAST)
                    need(act, proj_done, n + 1)
                    need_step(act, small_done, n - 1, SMALL_FIRST, SMALL_LAST)
                    runs = [ks] if ks[-1] - ks[0] + 1 == len(ks) else [[k] for k in ks]
                    for r in runs:
                        a, z = r[0], r[-1] + 1
                        cp = nc.scalar.activation(cm3[:, u % 2, a:z, :],
                                                  act_ps[:, a * SEQ:z * SEQ].rearrange("p (k s) -> p k s", s=SEQ),
                                                  ACT.Copy)
                    cp.then_inc(tr3_read, 1)
                if ok(n + 2):
                    need(act, scores_done, n)
                    for h in range(4):
                        cp = nc.scalar.activation(v_heads[:, u % 2, h, :], vT_ps, ACT.Identity,
                                                  bias=bv_heads[:, h:h + 1], scale=head_mask[:, h:h + 1])
                    cp.then_inc(heads_ready, 1)
                if ok(n - 5):
                    need(act, xn2_ready, n - 5)
                    act.wait_ge(tables, 1)
                    nc.scalar.activation(xn_all[0:SEQ, ds((n - 5) * D, D)], xn2[:, (u - 5) % 2, :], ACT.Copy).then_inc(row_ready, 1)

            def rows_to_stage(b):
                act.wait_ge(row_ready, b * R + R)
                stage_free(act, b)
                nc.scalar.activation(stages[stage_buffer(b)][:, :, 0:D],
                                     xn_all[0:SEQ, ds(b * (R * D), R * D)].rearrange("p (b d) -> p b d", d=D),
                                     ACT.Copy).then_inc(stage_x, 1)

            def route(g, v):
                for b in staged(g, v):
                    rows_to_stage(b)
                if v == 0 and routed_group(g):
                    act.wait_ge(less_ready, g + 1)
                    nc.scalar.activation(less[:], less[:], ACT.Exp).then_inc(exps_ready, 1)
            steps(act, step, route, rows_to_stage)

            def weights_hi(t, u, q):
                if q == 0:
                    act.wait_ge(weights_in[u % 2], loads(t, u, 2))
                if since(t, 2):
                    act.wait_ge(down_done, t * HC + (q + 1 - 2 * HC))
                r = slice(q * W_COLS // HC, (q + 1) * W_COLS // HC)
                nc.scalar.activation(w_hi[:, u % 2, r], w_raw[:, u % 2, r], ACT.Copy).then_inc(w_hi_done, 1)

            def hidden_hi(t, c):
                act.wait_ge(hid_done, t * HC + (c + 1))
                if since(t, 1):
                    act.wait_ge(down_done, t * HC + (c + 1 - HC))
                nc.scalar.activation(hid_hi[:, c, :], hid[:, c % 2, :], ACT.Copy).then_inc(hid_hi_done, 1)

            def x_round(t, u):
                act.wait_ge(x_done, t + 1)
                if since(t, 2):
                    act.wait_ge(up_done, t * HC - HC)
                nc.scalar.activation(x_hi[:, u % 2, :], x_ps[:], ACT.Copy).then_inc(x_hi_done, 1)

            def out_cm(t, u):
                act.wait_ge(down_done, t * HC + HC)
                if since(t, 1):
                    act.wait_ge(y_tok_done, t)
                nc.scalar.activation(y_cm, y_ps[u % 2][:], ACT.Copy).then_inc(y_read, 1)

            def tile(t, u):
                for c in range(HC):
                    act.wait_ge(gate_done, t * HC + (c + 1))
                    if since(t, 1) or c >= 2:
                        act.wait_ge(hid_done, t * HC + (c - 1))
                    nc.scalar.activation(silu[:, c % 2, :], gate_ps[c % 2], ACT.Silu).then_inc(silu_done, 1)
                    if c == 2 and is_tile(t - 1):
                        out_cm(t - 1, u - 1)
                    if is_tile(t + 1):
                        if c == 1:
                            x_round(t + 1, u + 1)
                        weights_hi(t + 1, u + 1, c)
                    hidden_hi(t, c)
            for q in range(HC):
                weights_hi(0, 0, q)
            x_round(0, 0)
            tiles(act, tile, lambda t, u: out_cm(t - 1, u - 1))

        @block.vector
        def _(dve):
            for c in range(CHUNKS):
                dve.wait_ge(conv_read, c + 1)
                st = nc.vector.bn_stats(stats_y[:, c, :], y_all[:, c * CHUNK:(c + 1) * CHUNK])
            st.then_inc(stats_done, 1)
            dve.wait_ge(stats_done, 1)
            nc.vector.bn_aggr(bn[:, 0:2], stats_y[:]).then_inc(bn_var, 1)
            dve.wait_ge(consts, 10)
            dve.wait_ge(conv_w_in, 16 * 3)
            dve.wait_ge(w_in, 16 * 4)
            nc.vector.tensor_scalar(bv_heads[:], head_mask[:], bv_c, None, ALU.mult)
            dve.wait_ge(bn_rstd, 2)
            nc.vector.tensor_tensor(bn[:, 4:5], bn[:, 3:4], gamma_c, ALU.mult).then_inc(bn_link, 1)
            dve.wait_ge(bn_link, 1)
            nc.vector.tensor_tensor(bn[:, 2:3], bn[:, 0:1], bn[:, 4:5], ALU.mult).then_inc(bn_link, 1)
            dve.wait_ge(bn_link, 2)
            nc.vector.tensor_tensor(bn[:, 5:6], beta_c, bn[:, 2:3], ALU.subtract).then_inc(bn_ready, 1)

            def step(n, u, g, v):
                p = u % 2
                x, r2 = (u + 3) % 2, (u - 5) % 2
                has1, has2, has3 = ok(n + 3), ok(n - 5), ok(n - 7)
                if has1 or has2 or has3:
                    need_step(dve, small_done, n - 1, SMALL_FIRST, SMALL_LAST)
                if has1:
                    nc.vector.bn_stats(stat6[:, 0, :], h_tok_ps).then_inc(stats1_done, 1)
                if has2:
                    h1 = resid[:, ds(n - 5, 1), :].rearrange("p b d -> p (b d)")
                    nc.vector.scalar_tensor_tensor(out=h1, in0=wo_ps, scalar=shift1[:, ds(n - 5, 1)], in1=h1,
                                                   op0=ALU.add, op1=ALU.add).then_inc(h1_done, 1)
                    need(dve, h1_done, n - 5)
                if has3:
                    nc.vector.tensor_tensor(logits[:, (u - 7) % R, :], logit_ps,
                                            route_b, ALU.add).then_inc(logits_done, 1)
                if counted(g, v - 1):
                    read_counts(g)
                if has2:
                    nc.vector.bn_stats(stat6[:, 1, :], h1).then_inc(stats2_done, 1)
                need(dve, otr_done, n - 3)
                if has1:
                    need(dve, stats1_done, n + 3)
                need(dve, stats2_done, n - 5)
                if ok(n - 3):
                    nc.vector.reciprocal(rz[:], o_tok_ps[:, :, DH]).then_inc(rz_done, 1)
                if has1:
                    ag = nc.vector.bn_aggr(mv[:, p, 0, :], stat6[:, 0, :])
                if has2:
                    ag = nc.vector.bn_aggr(mv[:, p, 1, :], stat6[:, 1, :])
                if has1 or has2:
                    ag.then_inc(mv_ready, 1)
                if ok(n - 3):
                    need(dve, rz_done, n - 3)
                    need_step(dve, tr3_done, n - 2, TR3_FIRST, TR3_LAST)
                    nc.vector.tensor_tensor(att[:, (u - 3) % 2, :, :], o_tok_ps[:, :, 0:DH],
                                            rz[:].unsqueeze(2).broadcast_to([SEQ, HEADS, DH]),
                                            ALU.mult).then_inc(att_ready, 1)
                if ok(n):
                    need(dve, scores_done, n)
                    need(dve, exp_done, n - 2)
                    nc.vector.tensor_reduce(row_low[:, p, :].rearrange("p (a h) -> p a h", a=2),
                                            scores_ps[0:SEQ, :, 0:4 * SEQ].rearrange("p a (h j) -> p a h j", j=SEQ), AX.X,
                                            ALU.min).then_inc(low_done, 1)
                if has1 or has2:
                    need_step(dve, rstd_ready, n, LN_FIRST, LN_LAST)
                if has1:
                    sh = shift1[:, ds(n + 3, 1)]
                    nc.vector.scalar_tensor_tensor(out=sh, in0=mv[:, p, 0, 0:1], scalar=-1.0, in1=rstd[:, p, 0:1],
                                                   op0=ALU.mult, op1=ALU.mult)
                    nc.vector.tensor_scalar(rstd1[:, p:p + 1], rstd[:, p, 0:1], 1.0, None, ALU.add).then_inc(shift1_done, 1)
                if has2:
                    nc.vector.scalar_tensor_tensor(out=shift2[:, p:p + 1], in0=mv[:, p, 1, 0:1], scalar=-1.0,
                                                   in1=rstd[:, p, 1:2], op0=ALU.mult, op1=ALU.mult).then_inc(shift2_done, 1)
                need_step(dve, tr3_done, n - 2, TR3_FIRST, TR3_LAST)
                if has1:
                    need(dve, shift1_done, n + 3)
                    nc.vector.tensor_scalar(xn[:, x, :], h_tok_ps, rstd[:, p, 0:1], sh, ALU.mult, ALU.add).then_inc(xn_ready, 1)
                if has2:
                    need(dve, shift2_done, n - 5)
                    need(dve, row_ready, n - 7)
                    nc.vector.tensor_scalar(xn2[:, r2, :], h1, rstd[:, p, 1:2], shift2[:, p:p + 1],
                                            ALU.mult, ALU.add).then_inc(xn2_ready, 1)
                if has1:
                    nc.vector.scalar_tensor_tensor(out=resid[:, ds(n + 3, 1), :].rearrange("p b d -> p (b d)"),
                                                   in0=h_tok_ps, scalar=rstd1[:, p:p + 1], in1=bo_row,
                                                   op0=ALU.mult, op1=ALU.add).then_inc(small_read, 1)
                if ok(n + 2):
                    need(dve, proj_done, n + 2)
                    need(dve, pv_done, n - 2)
                    nc.vector.scalar_tensor_tensor(out=q_a[:], in0=qT_ps, scalar=bq_c, in1=rope_sb[:, 0, :],
                                                   op0=ALU.add, op1=ALU.mult)
                    nc.vector.scalar_tensor_tensor(out=q_b[:], in0=qrT_ps, scalar=bqr_c, in1=rope_sb[:, 1, :],
                                                   op0=ALU.add, op1=ALU.mult).then_inc(rope_link, 1)
                    nc.vector.tensor_tensor(v_tok[:, (u + 2) % 4, :, 0:DH], v_ps.rearrange("p (h e) -> p h e", e=DH),
                                            bv_row.rearrange("p (h e) -> p h e", e=DH), ALU.add)
                    need(dve, rope_link, n + 2)
                    nc.vector.tensor_tensor(q_cm[:, p, :], q_a[:], q_b[:], ALU.add).then_inc(proj_read, 1)

            def over(x, n=4):
                return x.unsqueeze(2).broadcast_to([SEQ, R * PROBS, n])
            prob = less[:].rearrange("p (q i) -> p q i", i=4)

            def read_counts(g):
                dve.wait_ge(counts_done, g + 1)
                nc.vector.tensor_tensor(place.rearrange("p b e -> p e b"), count_ps,
                                        next_row[0:SEQ, :].unsqueeze(2).broadcast_to([SEQ, EXPERTS, R]), ALU.add).then_inc(place_ready, 1)
                dve.wait_ge(place_ready, g + 1)
                nc.vector.tensor_tensor(next_row[:], next_row[:], total_ps, ALU.add).then_inc(counts_read, 1)

            def route(g, v):
                for group, part in parts_of(g, v):
                    if is_group(group, LAST) and part == 6:
                        read_counts(group)
                    route_part(group, part)
                for b in staged(g, v):
                    to_stage(b)

            def route_part(g, which):
                links, at = links_of[which], [0]
                own_links = LINKS[which]

                def link(ins):
                    at[0] += 1
                    ins.then_inc(links, 1)
                    dve.wait_ge(links, g * own_links + at[0])
                flat_picks = [picks[:, k, :, :].rearrange("p b l -> p (b l)") for k in range(2)]
                if which == 0:
                    lg = logits[:].rearrange("p b (q i) -> p (b q) i", i=4)
                    dve.wait_ge(logits_done, g * R + R)
                    link(nc.vector.tensor_reduce(pmax[:], lg, AX.X, ALU.max))
                    nc.vector.tensor_tensor(prob, lg, over(pmax[:]), ALU.subtract).then_inc(less_ready, 1)
                if which == 1:
                    dve.wait_ge(exps_ready, g + 1)
                    link(nc.vector.tensor_reduce(part[:], prob, AX.X, ALU.add))
                    link(nc.vector.reciprocal(first_p[:], part[:]))
                    scaled = rank[:].rearrange("p (q i) -> p q i", i=4)
                    link(nc.vector.scalar_tensor_tensor(out=scaled, in0=prob, scalar=SCALE_UP, in1=over(first_p[:]),
                                                        op0=ALU.mult, op1=ALU.mult))
                    nc.vector.tensor_tensor(prob, prob, over(first_p[:]), ALU.mult)
                    q4 = [SEQ, R * PROBS, 4, 4]
                    nc.vector.tensor_tensor(pairs[:], scaled.unsqueeze(2).broadcast_to(q4), scaled.unsqueeze(3).broadcast_to(q4),
                                            ALU.subtract).then_inc(pairs_ready, 1)
                if which == 2:
                    dve.wait_ge(pairs_ready, g + 1)
                    flat_pairs = pairs[:].rearrange("p q i j -> p q (i j)")
                    link(nc.vector.tensor_tensor(flat_pairs, flat_pairs,
                                                 tie[:].rearrange("p i j -> p (i j)").unsqueeze(1).broadcast_to([SEQ, R * PROBS, 16]),
                                                 ALU.is_ge))
                    nc.vector.tensor_reduce(rank[:].rearrange("p (q i) -> p q i", i=4), pairs[:], AX.X,
                                            ALU.add).then_inc(rank_ready, 1)
                if which == 3:
                    dve.wait_ge(rank_ready, g + 1)
                    nc.vector.tensor_scalar(flat_picks[0], rank[:], 0.0, None, ALU.is_equal)
                    nc.vector.tensor_scalar(flat_picks[1], rank[:], 1.0, None, ALU.is_equal).then_inc(picks_ready, 1)
                    link(nc.vector.tensor_scalar(chosen[:].rearrange("p b l -> p (b l)"), rank[:], 2.0, None, ALU.is_lt))
                    ch_g = chosen[:, :, 0:GROUPS]
                    ch_e = chosen[:, :, GROUPS:].rearrange("p b (g e) -> p b g e", e=PER_GROUP)
                    link(nc.vector.tensor_tensor(sel[:].rearrange("p (g e) b -> p g e b", e=PER_GROUP),
                                                 ch_e.rearrange("p b g e -> p g e b"),
                                                 ch_g.rearrange("p b g -> p g b").unsqueeze(2).broadcast_to([SEQ, GROUPS, PER_GROUP, R]),
                                                 ALU.mult))
                    nc.vector.tensor_tensor_scan(sel_upto[:].rearrange("p e b -> p (e b)"), no_carry[:].rearrange("p e b -> p (e b)"),
                                                 sel[:].rearrange("p e b -> p (e b)"), 0.0, ALU.mult, ALU.add).then_inc(sel_ready, 1)
                if which == 4:
                    dve.wait_ge(picks_ready, g + 1)
                    flat = weigh[:, 0, :, :].rearrange("p b l -> p (b l)")
                    link(nc.vector.tensor_tensor(flat, less[:], flat_picks[1], ALU.mult))
                    link(nc.vector.tensor_reduce(second_p[:], flat.rearrange("p (q i) -> p q i", i=4), AX.X, ALU.add))
                    link(nc.vector.tensor_tensor(part[:], first_p[:], second_p[:], ALU.add))
                    link(nc.vector.scalar_tensor_tensor(out=second_p[:], in0=part[:], scalar=TOP_P, in1=second_p[:],
                                                        op0=ALU.is_le, op1=ALU.mult))
                    link(nc.vector.scalar_tensor_tensor(out=part[:], in0=second_p[:], scalar=1e-9, in1=first_p[:],
                                                        op0=ALU.add, op1=ALU.add))
                    nc.vector.reciprocal(pmax[:], part[:]).then_inc(shares_ready, 1)
                if which == 5:
                    dve.wait_ge(shares_ready, g + 1)
                    nc.vector.tensor_tensor(ratio[:, 0, :], first_p[:], pmax[:], ALU.mult)
                    link(nc.vector.tensor_tensor(ratio[:, 1, :], second_p[:], pmax[:], ALU.mult))
                    of_groups = ratio[:].rearrange("p k (b q) -> p k b q", q=PROBS)[:, :, :, 0]
                    link(nc.vector.tensor_scalar(of_groups, of_groups, GROUPS ** -0.5, None, ALU.mult))
                    for k in range(2):
                        last = nc.vector.tensor_tensor(weigh[:, k, :, :].rearrange("p b (q i) -> p (b q) i", i=4),
                                                       picks[:, k, :, :].rearrange("p b (q i) -> p (b q) i", i=4),
                                                       over(ratio[:, k, :]), ALU.mult)
                    last.then_inc(weigh_ready, 1)
                if which == 6:
                    dve.wait_ge(weigh_ready, g + 1)
                    nc.vector.tensor_tensor(weigh[:, 0, :, :], weigh[:, 0, :, :], weigh[:, 1, :, :], ALU.add)
                    dve.wait_ge(counts_read, g + 1)
                    link(nc.vector.tensor_tensor(place2, picks[:, :, :, GROUPS:],
                                                 place.unsqueeze(1).broadcast_to([SEQ, 2, R, EXPERTS]), ALU.mult))
                    nc.vector.tensor_reduce(by_group.rearrange("p k b g -> p (k b g)"),
                                            place2.rearrange("p k b (g e) -> p (k b g) e", e=PER_GROUP), AX.X,
                                            ALU.add).then_inc(by_group_ready, 1)
                if which == 7:
                    dve.wait_ge(by_group_ready, g + 1)
                    for gp in range(2):
                        last = nc.vector.tensor_tensor(by_pick[:, gp, :, :, :], by_group,
                                                       picks[:, gp, :, 0:GROUPS].unsqueeze(1).broadcast_to([SEQ, 2, R, GROUPS]), ALU.mult)
                    link(last)
                    nc.vector.tensor_reduce(slots_f[:], by_pick.rearrange("p a k b g -> p (a k b) g"), AX.X,
                                            ALU.add).then_inc(slots_ready, 1)
                assert at[0] == own_links, (which, at)

            def to_stage(g):
                stage, k = stages[stage_buffer(g)], stage_buffer(g)
                dve.wait_ge(slots_ready, g + 1)
                dve.wait_ge(tables, 1)
                stage_free(dve, g)
                nc.vector.tensor_tensor(stage[:, :, ROW_W:ROW_ID].rearrange("p b (g e) -> p b g e", e=PER_GROUP),
                                        weigh[:, 0, :, GROUPS:].rearrange("p b (g e) -> p b g e", e=PER_GROUP),
                                        weigh[:, 0, :, 0:GROUPS].unsqueeze(3).broadcast_to([SEQ, R, GROUPS, PER_GROUP]),
                                        ALU.mult)
                nc.vector.tensor_copy(stage[:, :, ROW_ID], tok_id[:])
                nc.vector.tensor_copy(slots[k][:], slots_f[:]).then_inc(stage_ready, 1)
                dve.wait_ge(stage_ready, g + 1)
                nc.vector.tensor_scalar(tok_id[:], tok_id[:], float(R * SEQ), None, ALU.add)
            steps(dve, step, route, to_stage)

            count = [0]

            def link(ins):
                count[0] += 1
                ins.then_inc(table_link, 1)
                dve.wait_ge(table_link, count[0])
            dve.wait_ge(stage_ready, ROUTES)
            nc.vector.tensor_copy(ends_i[:], next_row[:]).then_inc(ends_ready, 1)
            link(nc.vector.tensor_tensor(n_tiles[:], next_row[:], region[:], ALU.subtract))
            link(nc.vector.tensor_scalar(n_tiles_i[:], n_tiles[:], float(TILE - 1), None, ALU.add))
            link(nc.vector.tensor_scalar(n_tiles_i[:], n_tiles_i[:], TILE.bit_length() - 1, None, ALU.logical_shift_right))
            link(nc.vector.tensor_copy(n_tiles[:], n_tiles_i[:]))
            link(nc.vector.tensor_tensor_scan(last_tile[:], ones_e[:], n_tiles[:], 0.0, ALU.mult, ALU.add))

            def whole(to, of, n):
                shift, tmp = n.bit_length() - 1, more_tiles_i[:, 3:4]
                link(nc.vector.tensor_scalar(tmp, of, shift, None, ALU.logical_shift_right))
                link(nc.vector.tensor_scalar(to, tmp, shift, None, ALU.logical_shift_left))
            in_rounds, in_rest, both = (more_tiles_i[:, i:i + 1] for i in range(3))
            link(nc.vector.tensor_scalar(both, last_tile[:, EXPERTS - 1:EXPERTS], float(1 - SURE_TILES), None, ALU.add))
            whole(both, both, 2)
            whole(in_rounds, both, ROWS)
            link(nc.vector.tensor_tensor(in_rest, both, in_rounds, ALU.subtract))
            t_e = [P, TABLE, EXPERTS]
            link(nc.vector.tensor_tensor(past[:], tile_no[:].unsqueeze(2).broadcast_to(t_e),
                                         last_tile[:].unsqueeze(1).broadcast_to(t_e), ALU.is_ge))
            nc.vector.tensor_tensor(past2[:], past[:], n_tiles[:].unsqueeze(1).broadcast_to(t_e), ALU.mult)
            link(nc.vector.tensor_reduce(tile_e[:], past[:], AX.X, ALU.add))
            link(nc.vector.tensor_reduce(tile_s[:], past2[:], AX.X, ALU.add))
            nc.vector.tensor_tensor(past[:], tile_e[:].unsqueeze(2).broadcast_to(t_e),
                                    expert_no[:].unsqueeze(1).broadcast_to(t_e), ALU.is_equal)
            nc.vector.tensor_scalar(tile_v[:], tile_e[:], float(EXPERTS), float(TILE), ALU.is_lt, ALU.mult)
            link(nc.vector.tensor_tensor(tile_s[:], tile_no[:], tile_s[:], ALU.subtract))
            link(nc.vector.tensor_tensor(tile_s[:], tile_s[:], tile_v[:], ALU.mult))
            link(nc.vector.scalar_tensor_tensor(out=tile_row_i[:], in0=tile_e[:], scalar=float(CAP), in1=tile_s[:],
                                                op0=ALU.mult, op1=ALU.add))
            nc.vector.tensor_scalar(tile_e_i[:], tile_e[:], float(EXPERTS - 1), None, ALU.min).then_inc(table_ready, 1)

            def x_rest(t, u):
                dve.wait_ge(x_hi_done, t + 1)
                nc.vector.tensor_tensor(x_lo[:, u % 2, :], x_ps[:], x_hi[:, u % 2, :].bitcast(F32), ALU.subtract).then_inc(x_read, 1)

            def hidden_lo(t, c):
                dve.wait_ge(hid_hi_done, t * HC + (c + 1))
                nc.vector.tensor_tensor(hid_lo[:, c, :], hid[:, c % 2, :], hid_hi[:, c, :].bitcast(F32),
                                        ALU.subtract).then_inc(hid_ready, 1)

            def weights(t, u):
                dve.wait_ge(rows_in[u], loads(t, u, ROWS))
                nc.vector.tensor_tensor(w_part[:], x_rows[:, u, :, ROW_W:ROW_ID],
                                        past[:, ds(t, 1), :].broadcast_to([P, SUB, EXPERTS]), ALU.mult).then_inc(w_link, 1)
                dve.wait_ge(w_link, t + 1)
                nc.vector.tensor_reduce(w_row[:, u, :], w_part[:], AX.X, ALU.add).then_inc(w_row_done, 1)
                if since(t, ROWS):
                    dve.wait_ge(added, (t - (ROWS - 1)) * (16 * SUB))
                nc.vector.tensor_copy(out_ids[:, u, :], x_rows[:, u, :, ROW_ID]).then_inc(ids_ready, 1)

            def out_half(t, u, half):
                if half == 0:
                    dve.wait_ge(y_tok_done, t + 1)
                    dve.wait_ge(w_row_done, t + 1)
                    if since(t, 2):
                        dve.wait_ge(added, (t - 1) * (16 * SUB))
                for s in range(half * SUB // 2, (half + 1) * SUB // 2):
                    last = nc.vector.tensor_scalar(y_rows[:, u % 2, s, :], y_tok_ps[:, s * P:(s + 1) * P],
                                                   w_row[:, u % ROWS, s:s + 1], None, ALU.mult)
                if half == 1:
                    last.then_inc(y_rows_ready, 1)

            def tile(t, u):
                for c in range(HC):
                    dve.wait_ge(silu_done, t * HC + (c + 1))
                    dve.wait_ge(up_done, t * HC + (c + 1))
                    if since(t, 1) or c >= 2:
                        dve.wait_ge(hid_ready, t * HC + (c - 1))
                    nc.vector.tensor_tensor(hid[:, c % 2, :], silu[:, c % 2, :], up_ps[c % 2], ALU.mult).then_inc(hid_done, 1)
                    if c == 0 and is_tile(t - 2):
                        out_half(t - 2, u - 2, 1)
                    if c == 1:
                        weights(t, u)
                    if c == 2 and is_tile(t + 1):
                        x_rest(t + 1, u + 1)
                    if c == 3 and is_tile(t - 1):
                        out_half(t - 1, u - 1, 0)
                    hidden_lo(t, c)
            x_rest(0, 0)

            def finish(t, u):
                out_half(t - 2, u - 2, 1)
                out_half(t - 1, u - 1, 0)
                out_half(t - 1, u - 1, 1)
            tiles(dve, tile, finish)


def lay_out(inputs):
    a = {k: np.asarray(v) for k, v in inputs.items()}
    perm = np.arange(D).reshape(HEADS, 2, DH // 2)[:, ::-1, :].reshape(-1)
    theta = (1.0 / 10000.0 ** (np.arange(0, DH, 2, dtype=np.float32) / np.float32(DH))).astype(np.float32)
    angle = np.arange(SEQ, dtype=np.float32)[None, :] * np.tile(theta, 2 * HEADS)[:, None]
    sign = np.tile(np.repeat(np.array([-1.0, 1.0], np.float32), DH // 2), HEADS)[:, None]
    scale = np.float32(DH ** -0.5)
    gate, up = (a[k].reshape(EXPERTS, P, HC, P) for k in ("L0_ffn_W1", "L0_ffn_W3"))
    down = a["L0_ffn_W2"].reshape(EXPERTS, HC, P, D).transpose(0, 2, 1, 3)
    arrays = {
        "x_t": a["x"].reshape(BATCH * TIME, D_IN).T,
        "conv_w": a["L0_tok_W"].T,
        "col_params": np.stack([a["L0_tok_b"], a["L0_tok_gamma"], a["L0_tok_beta"], a["L0_attn_bq"],
                                a["L0_attn_bq"][perm], a["L0_attn_bv"]], axis=1),
        "row_params": np.concatenate([a["L0_attn_bv"], a["L0_attn_bo"], a["L0_ffn_br"], a["L0_ffn_bgate"].reshape(-1)]),
        "rope_tab": np.stack([-np.cos(angle) * scale, -np.sin(angle) * sign * scale]).astype(np.float32),
        "attn_w": np.stack([a["L0_attn_Wq"], a["L0_attn_Wq"][:, perm], a["L0_attn_Wv"], a["L0_attn_Wo"]]),
        "route_w": np.concatenate([a["L0_ffn_Wr"], a["L0_ffn_Wgate"].transpose(1, 0, 2).reshape(D, EXPERTS)], axis=1),
        "expert_w": np.stack([gate, up, down], axis=3).reshape(EXPERTS, P, 3 * HID),
    }
    return {k: np.ascontiguousarray(v) for k, v in arrays.items()}


def kernel(**inputs):
    import concourse.bacc as bacc
    from concourse.bass_utils import run_bass_kernel_spmd

    arrays = lay_out(inputs)
    nc = bacc.Bacc("TRN2", target_bir_lowering=False, num_devices=1)
    args = {k: nc.dram_tensor(k, a.shape, mybir.dt.from_np(a.dtype), kind="ExternalInput").ap() for k, a in arrays.items()}
    out = nc.dram_tensor("out", (N_TOK + TILE, D), F32, kind="ExternalOutput").ap()
    audio_tower(nc, out=out, **args)
    result = run_bass_kernel_spmd(nc, [arrays], core_ids=[0])
    return result.results[0]["out"][:N_TOK].reshape(BATCH, SEQ, D)
```
